# Optimizing a Trainium2 kernel written in Bass

```python
import numpy as np
import jax
import jax.numpy as jnp

def _softmax(x, axis=-1):
    return jax.nn.softmax(x, axis=axis)

def _gelu(x):
    return jax.nn.gelu(x, approximate=True)

def _silu(x):
    return jax.nn.silu(x)

def _sigmoid(x):
    return jax.nn.sigmoid(x)

def _layernorm(x, axis=-1, eps=1e-05):
    m = jnp.mean(x, axis=axis, keepdims=True)
    v = jnp.var(x, axis=axis, keepdims=True)
    return (x - m) / jnp.sqrt(v + eps)

def _scatter_add(tgt, idx, src, axis=0):
    return tgt.at[idx].add(src)

def _segment_sum(src, seg, n):
    return jax.ops.segment_sum(src, seg, n)
kernel_name = 'mk_vit_tower_d2_tok_img1024_r4_f4b596'

def setup_inputs(seed: int=0):
    np.random.seed(seed)
    _w = jnp.asarray

    def _rec_inputs():
        import jax
        import jax.numpy as jnp
        _rk = jax.random.key(seed)
        x = -0.00016672 + 0.999947 * jax.random.normal(jax.random.fold_in(_rk, 1), (16, 3, 96, 96), jnp.float32)
        return x
    x = _rec_inputs()

    def _L0_tok_setup():
        import jax, jax.numpy as jnp
        import numpy as np
        B, C, H, W = (64, 3, 96, 96)
        P = 16
        NP = H // P * (W // P)
        PD = C * P * P
        ED = 256
        NCLS = 1

        def _layernorm(x, g, b, eps=1e-05):
            mu = jnp.mean(x, axis=-1, keepdims=True)
            var = jnp.mean(jnp.square(x - mu), axis=-1, keepdims=True)
            return (x - mu) * jax.lax.rsqrt(var + eps) * g + b
        key = jax.random.key(seed)
        ks = jax.random.split(key, 8)
        x = jax.random.normal(ks[0], (B, C, H, W), dtype=jnp.float32)
        ln1_g = jnp.ones((PD,), jnp.float32)
        ln1_b = jnp.zeros((PD,), jnp.float32)
        W_proj = jax.random.normal(ks[1], (PD, ED), jnp.float32) / np.sqrt(PD)
        b_proj = jnp.zeros((ED,), jnp.float32)
        ln2_g = jnp.ones((ED,), jnp.float32)
        ln2_b = jnp.zeros((ED,), jnp.float32)
        cls_token = jax.random.normal(ks[2], (1, NCLS, ED), jnp.float32)
        pos_emb = jax.random.normal(ks[3], (1, NP + NCLS, ED), jnp.float32)
        return {'x': x, 'ln1_g': ln1_g, 'ln1_b': ln1_b, 'W_proj': W_proj, 'b_proj': b_proj, 'ln2_g': ln2_g, 'ln2_b': ln2_b, 'cls_token': cls_token, 'pos_emb': pos_emb}
    _L0_tok_all = _L0_tok_setup()
    _L0_tok_in = {k: v for k, v in _L0_tok_all.items() if k in ('ln1_g', 'ln1_b', 'W_proj', 'b_proj', 'ln2_g', 'ln2_b', 'cls_token', 'pos_emb')}
    del _L0_tok_all

    def _L0_attn_setup():
        import jax, jax.numpy as jnp
        import numpy as np
        EPS = 1e-12
        HEADS = 16
        DIM_KEYS = 16
        DIM_VALUES = 64

        def l2norm(t):
            n = jnp.linalg.norm(t, axis=-1, keepdims=True)
            return t / jnp.maximum(n, EPS)

        def tanh_norm(t):
            n = jnp.linalg.norm(t, axis=-1, keepdims=True)
            return jnp.tanh(n) * (t / jnp.maximum(n, EPS))

        def split_heads(x, h):
            b, n, hd = x.shape
            return x.reshape(b, n, h, hd // h).transpose(0, 2, 1, 3)
        key = jax.random.key(seed)
        k1, k2, k3, k4 = jax.random.split(key, 4)
        b, n, dim = (4, 512, 256)
        dim_inner = (DIM_KEYS + DIM_VALUES) * HEADS
        tokens = jax.random.normal(k1, (b, n, dim), dtype=jnp.float32)
        Wqg = jax.random.normal(k2, (dim, dim_inner), dtype=jnp.float32) * dim ** (-0.5)
        Wkv = jax.random.normal(k3, (dim, dim_inner), dtype=jnp.float32) * dim ** (-0.5)
        Wout = jax.random.normal(k4, (DIM_VALUES * HEADS, dim), dtype=jnp.float32) * (DIM_VALUES * HEADS) ** (-0.5)
        return {'tokens': tokens, 'Wqg': Wqg, 'Wkv': Wkv, 'Wout': Wout}
    _L0_attn_all = _L0_attn_setup()
    _L0_attn_in = {k: v for k, v in _L0_attn_all.items() if k in ('Wqg', 'Wkv', 'Wout')}
    del _L0_attn_all

    def _L0_ffn_setup():
        import jax, jax.numpy as jnp
        import numpy as np
        H_DIM, E_DIM = (256, 128)
        N_SHARED, N_ROUTED, TOP_K = (2, 16, 4)
        B, S = (4, 512)
        key = jax.random.key(seed)
        ks = jax.random.split(key, 6)
        sc = 1.0 / np.sqrt(H_DIM)
        ec = 1.0 / np.sqrt(E_DIM)
        return {'x': jax.random.normal(ks[0], (B, S, H_DIM), dtype=jnp.float32), 'shared_up': jax.random.uniform(ks[1], (N_SHARED, E_DIM, H_DIM), jnp.float32, -sc, sc), 'shared_down': jax.random.uniform(ks[2], (N_SHARED, H_DIM, E_DIM), jnp.float32, -ec, ec), 'routed_up': jax.random.uniform(ks[3], (N_ROUTED, E_DIM, H_DIM), jnp.float32, -sc, sc), 'routed_down': jax.random.uniform(ks[4], (N_ROUTED, H_DIM, E_DIM), jnp.float32, -ec, ec), 'router_w': jax.random.uniform(ks[5], (N_ROUTED, H_DIM), jnp.float32, -sc, sc)}
    _L0_ffn_all = _L0_ffn_setup()
    _L0_ffn_in = {k: v for k, v in _L0_ffn_all.items() if k in ('shared_up', 'shared_down', 'routed_up', 'routed_down', 'router_w')}
    del _L0_ffn_all

    def _L1_attn_setup():
        import jax, jax.numpy as jnp
        import numpy as np
        DIM = 256
        HEADS = 16
        DIM_HEAD = 64
        INNER = HEADS * DIM_HEAD
        SEQ = 1024
        BATCH = 1
        key = jax.random.key(seed)
        ks = jax.random.split(key, 6)
        s = 0.02
        return {'x': jax.random.normal(ks[0], (BATCH, SEQ, DIM), dtype=jnp.float32), 'Wq': jax.random.normal(ks[1], (DIM, INNER), dtype=jnp.float32) * s, 'Wk': jax.random.normal(ks[2], (DIM, INNER), dtype=jnp.float32) * s, 'Wv': jax.random.normal(ks[3], (DIM, INNER), dtype=jnp.float32) * s, 'Wo': jax.random.normal(ks[4], (INNER, DIM), dtype=jnp.float32) * s, 'bo': jax.random.normal(ks[5], (DIM,), dtype=jnp.float32) * s}
    _L1_attn_all = _L1_attn_setup()
    _L1_attn_in = {k: v for k, v in _L1_attn_all.items() if k in ('Wq', 'Wk', 'Wv', 'Wo', 'bo')}
    del _L1_attn_all

    def _L1_ffn_setup():
        import jax, jax.numpy as jnp
        import numpy as np
        QMAX = 127.0
        EPS = 1e-08

        def _quantize_per_token(x):
            amax = jnp.clip(jnp.max(jnp.abs(x), axis=-1, keepdims=True), EPS, None)
            scale = amax / QMAX
            x_q = jnp.clip(jnp.round(x / scale), -128, 127)
            return (x_q, scale)

        def _quantize_per_channel(w):
            amax = jnp.clip(jnp.max(jnp.abs(w), axis=-1, keepdims=True), EPS, None)
            scale = amax / QMAX
            w_q = jnp.clip(jnp.round(w / scale), -128, 127)
            return (w_q, scale)
        key = jax.random.key(seed)
        k1, k2, k3 = jax.random.split(key, 3)
        B, S, DIN, DOUT = (8, 1024, 256, 256)
        x = jax.random.normal(k1, (B, S, DIN), dtype=jnp.float32)
        weight = jax.random.normal(k2, (DOUT, DIN), dtype=jnp.float32) * 0.02
        bias = jax.random.normal(k3, (DOUT,), dtype=jnp.float32)
        return {'x': x, 'weight': weight, 'bias': bias}
    _L1_ffn_all = _L1_ffn_setup()
    _L1_ffn_in = {k: v for k, v in _L1_ffn_all.items() if k in ('weight', 'bias')}
    del _L1_ffn_all
    return {'x': x, 'L0_tok_ln1_g': _L0_tok_in['ln1_g'], 'L0_tok_ln1_b': _L0_tok_in['ln1_b'], 'L0_tok_W_proj': _L0_tok_in['W_proj'], 'L0_tok_b_proj': _L0_tok_in['b_proj'], 'L0_tok_ln2_g': _L0_tok_in['ln2_g'], 'L0_tok_ln2_b': _L0_tok_in['ln2_b'], 'L0_tok_cls_token': _L0_tok_in['cls_token'], 'L0_tok_pos_emb': _L0_tok_in['pos_emb'], 'L0_attn_Wqg': _L0_attn_in['Wqg'], 'L0_attn_Wkv': _L0_attn_in['Wkv'], 'L0_attn_Wout': _L0_attn_in['Wout'], 'L0_ffn_shared_up': _L0_ffn_in['shared_up'], 'L0_ffn_shared_down': _L0_ffn_in['shared_down'], 'L0_ffn_routed_up': _L0_ffn_in['routed_up'], 'L0_ffn_routed_down': _L0_ffn_in['routed_down'], 'L0_ffn_router_w': _L0_ffn_in['router_w'], 'L1_attn_Wq': _L1_attn_in['Wq'], 'L1_attn_Wk': _L1_attn_in['Wk'], 'L1_attn_Wv': _L1_attn_in['Wv'], 'L1_attn_Wo': _L1_attn_in['Wo'], 'L1_attn_bo': _L1_attn_in['bo'], 'L1_ffn_weight': _L1_ffn_in['weight'], 'L1_ffn_bias': _L1_ffn_in['bias']}

def reference(x, L0_tok_ln1_g, L0_tok_ln1_b, L0_tok_W_proj, L0_tok_b_proj, L0_tok_ln2_g, L0_tok_ln2_b, L0_tok_cls_token, L0_tok_pos_emb, L0_attn_Wqg, L0_attn_Wkv, L0_attn_Wout, L0_ffn_shared_up, L0_ffn_shared_down, L0_ffn_routed_up, L0_ffn_routed_down, L0_ffn_router_w, L1_attn_Wq, L1_attn_Wk, L1_attn_Wv, L1_attn_Wo, L1_attn_bo, L1_ffn_weight, L1_ffn_bias):
    import jax
    import jax.numpy as jnp

    def _L0_tok_ref(x, ln1_g, ln1_b, W_proj, b_proj, ln2_g, ln2_b, cls_token, pos_emb):
        import jax, jax.numpy as jnp
        import numpy as np
        B, C, H, W = (64, 3, 96, 96)
        P = 16
        NP = H // P * (W // P)
        PD = C * P * P
        ED = 256
        NCLS = 1

        def _layernorm(x, g, b, eps=1e-05):
            mu = jnp.mean(x, axis=-1, keepdims=True)
            var = jnp.mean(jnp.square(x - mu), axis=-1, keepdims=True)
            return (x - mu) * jax.lax.rsqrt(var + eps) * g + b
        b = x.shape[0]
        h, w = (H // P, W // P)
        patches = x.reshape(b, C, h, P, w, P)
        patches = patches.transpose(0, 2, 4, 3, 5, 1).reshape(b, h * w, P * P * C)
        z = _layernorm(patches, ln1_g, ln1_b)
        z = jnp.einsum('bnp,pe->bne', z, W_proj) + b_proj
        z = _layernorm(z, ln2_g, ln2_b)
        cls = jnp.broadcast_to(cls_token, (b, NCLS, ED))
        z = jnp.concatenate([cls, z], axis=1)
        z = z + pos_emb
        return z

    def _L0_attn_ref(tokens, Wqg, Wkv, Wout):
        import jax, jax.numpy as jnp
        import numpy as np
        EPS = 1e-12
        HEADS = 16
        DIM_KEYS = 16
        DIM_VALUES = 64

        def l2norm(t):
            n = jnp.linalg.norm(t, axis=-1, keepdims=True)
            return t / jnp.maximum(n, EPS)

        def tanh_norm(t):
            n = jnp.linalg.norm(t, axis=-1, keepdims=True)
            return jnp.tanh(n) * (t / jnp.maximum(n, EPS))

        def split_heads(x, h):
            b, n, hd = x.shape
            return x.reshape(b, n, h, hd // h).transpose(0, 2, 1, 3)
        qg = split_heads(tokens @ Wqg, HEADS)
        kv = split_heads(tokens @ Wkv, HEADS)
        queries, gates = (qg[..., :DIM_KEYS], qg[..., DIM_KEYS:])
        keys, values = (kv[..., :DIM_KEYS], kv[..., DIM_KEYS:])
        queries, keys, values = (l2norm(queries), l2norm(keys), l2norm(values))
        sim = jnp.einsum('bhid,bhjd->bhij', queries, keys)
        attn = jnp.square(jax.nn.relu(sim))
        aggr = jnp.einsum('bhij,bhjd->bhid', attn, values)
        out = tanh_norm(aggr) * jnp.tanh(jax.nn.silu(gates))
        b, h, n, d = out.shape
        out = out.transpose(0, 2, 1, 3).reshape(b, n, h * d)
        return out @ Wout

    def _L0_ffn_ref(x, shared_up, shared_down, routed_up, routed_down, router_w):
        import jax, jax.numpy as jnp
        import numpy as np
        H_DIM, E_DIM = (256, 128)
        N_SHARED, N_ROUTED, TOP_K = (2, 16, 4)
        B, S = (4, 512)
        b, s, h = x.shape
        xt = x.reshape(-1, h)
        up_s = jnp.einsum('th,seh->tse', xt, shared_up)
        shared = jnp.einsum('tse,she->th', jax.nn.gelu(up_s, approximate=False), shared_down)
        probs = jax.nn.softmax(xt @ router_w.T, axis=-1)
        topk_p, topk_i = jax.lax.top_k(probs, TOP_K)
        gate = jnp.zeros_like(probs).at[jnp.arange(xt.shape[0])[:, None], topk_i].add(topk_p)
        up_r = jnp.einsum('th,reh->tre', xt, routed_up)
        act = jax.nn.gelu(up_r, approximate=False) * gate[:, :, None]
        routed = jnp.einsum('tre,rhe->th', act, routed_down)
        return (shared + routed).reshape(b, s, h)

    def _L1_attn_ref(x, Wq, Wk, Wv, Wo, bo):
        import jax, jax.numpy as jnp
        import numpy as np
        DIM = 256
        HEADS = 16
        DIM_HEAD = 64
        INNER = HEADS * DIM_HEAD
        SEQ = 1024
        BATCH = 1
        b, n, _ = x.shape
        beta = 1.0 / jnp.sqrt(jnp.float32(DIM_HEAD))

        def split_heads(t):
            return t.reshape(b, n, HEADS, DIM_HEAD).transpose(0, 2, 1, 3)
        q = split_heads(x @ Wq)
        k = split_heads(x @ Wk)
        v = split_heads(x @ Wv)
        scores = jnp.einsum('bhid,bhjd->bhij', q * beta, k)
        mask_value = -jnp.finfo(scores.dtype).max
        causal = jnp.triu(jnp.ones((n, n), dtype=bool), k=1)
        scores = jnp.where(causal, mask_value, scores)
        attn = jax.nn.softmax(scores, axis=-1)
        out = jnp.einsum('bhij,bhjd->bhid', attn, v)
        out = out.transpose(0, 2, 1, 3).reshape(b, n, INNER)
        return out @ Wo + bo

    def _L1_ffn_ref(x, weight, bias):
        import jax, jax.numpy as jnp
        import numpy as np
        QMAX = 127.0
        EPS = 1e-08

        def _quantize_per_token(x):
            amax = jnp.clip(jnp.max(jnp.abs(x), axis=-1, keepdims=True), EPS, None)
            scale = amax / QMAX
            x_q = jnp.clip(jnp.round(x / scale), -128, 127)
            return (x_q, scale)

        def _quantize_per_channel(w):
            amax = jnp.clip(jnp.max(jnp.abs(w), axis=-1, keepdims=True), EPS, None)
            scale = amax / QMAX
            w_q = jnp.clip(jnp.round(w / scale), -128, 127)
            return (w_q, scale)
        B, S, DIN = x.shape
        w_q, w_scale = _quantize_per_channel(weight.astype(jnp.float32))
        x_flat = x.reshape(-1, DIN).astype(jnp.float32)
        x_q, x_scale = _quantize_per_token(x_flat)
        out = jnp.matmul(x_q, w_q.T) * x_scale * w_scale.T
        out = out.reshape(B, S, -1) + bias
        return out.astype(x.dtype)
    h = _L0_tok_ref(x, L0_tok_ln1_g, L0_tok_ln1_b, L0_tok_W_proj, L0_tok_b_proj, L0_tok_ln2_g, L0_tok_ln2_b, L0_tok_cls_token, L0_tok_pos_emb)
    h = h + _L0_attn_ref(_layernorm(h, axis=-1), L0_attn_Wqg, L0_attn_Wkv, L0_attn_Wout)
    h = h + _L0_ffn_ref(_layernorm(h, axis=-1), L0_ffn_shared_up, L0_ffn_shared_down, L0_ffn_routed_up, L0_ffn_routed_down, L0_ffn_router_w)
    h = h + _L1_attn_ref(_layernorm(h, axis=-1), L1_attn_Wq, L1_attn_Wk, L1_attn_Wv, L1_attn_Wo, L1_attn_bo)
    h = h + _L1_ffn_ref(_layernorm(h, axis=-1), L1_ffn_weight, L1_ffn_bias)
    return h

_drawn_inputs = setup_inputs


def setup_inputs(seed=0):
    import zlib

    import numpy as np

    out = dict(_drawn_inputs(seed))
    spreads = {'L0_tok_ln1_g': (1.0, 0.2),
     'L0_tok_ln1_b': (0.0, 0.1),
     'L0_tok_b_proj': (0.0, 0.1),
     'L0_tok_ln2_g': (1.0, 0.2),
     'L0_tok_ln2_b': (0.0, 0.1)}
    factors = {'L0_attn_Wqg': 4.574,
     'L0_attn_Wkv': 4.446,
     'L0_attn_Wout': 4.493,
     'L1_attn_Wq': 8.0,
     'L1_attn_Wk': 8.0,
     'L1_attn_bo': 4.888}
    for name, (base, spread) in spreads.items():
        noise = np.random.default_rng([zlib.crc32(name.encode()), seed]).standard_normal(out[name].shape)
        drawn = base * np.exp(spread * noise) if base else spread * noise
        out[name] = jnp.asarray(drawn.astype(out[name].dtype))
    for name, factor in factors.items():
        out[name] = (out[name] * factor).astype(out[name].dtype)
    return out
```

```python
from contextlib import ExitStack

import numpy as np

import concourse.bass as bass
from concourse import mybir

F32 = mybir.dt.float32
BF16 = mybir.dt.bfloat16
I32 = mybir.dt.int32
ALU = mybir.AluOpType
ACT = mybir.ActivationFunctionType
AX = mybir.AxisListType.X

BATCH, PATCHES, PATCH_DIM, DIM = 16, 36, 768, 256
SEQ = PATCHES + 1
HALVES = 2
IMAGES = BATCH // HALVES
TILE_IMAGES = (3, 3, 2)
TILES = len(TILE_IMAGES)
ROWS = tuple(n * SEQ for n in TILE_IMAGES)
PATCH_ROWS = tuple(n * PATCHES for n in TILE_IMAGES)
MAX_ROWS = max(ROWS)
START = tuple(sum(ROWS[:t]) for t in range(TILES))
PATCH_START = tuple(sum(PATCH_ROWS[:t]) for t in range(TILES))
TOKENS = sum(ROWS)
HEADS, DK, DV = 16, 16, 64
INNER = HEADS * DV
QK_COLS = 2 * HEADS * DK + DK
KD = DIM // 128
KP = PATCH_DIM // 128
KI = INNER // 128
SHARED, ROUTED, TOP_K, EXPERT = 2, 16, 4, 128
EXPERTS = SHARED + ROUTED
ACT_RING, GATE_RING = 4, 4
ROUND = 12582912.0
QMAX = 127.0
NEG = -3.0e38

DENSE = (0, 1)
SCORES = (2, 3)


def weave(main, fill):
    out, done = [], 0
    for i, step in enumerate(main):
        out.append(step)
        want = (i + 1) * len(fill) // len(main)
        out += fill[done:want]
        done = want
    return out


def token_steps(h):
    return [("patch_ln", h)], [("patch_t", h, c) for c in range(KP)] + [("embed", h, t) for t in range(TILES)]


def layer0_dense(h):
    steps = []
    for c in range(4):
        steps += [("qk0", h, c), ("qk0", h, 4 + c)]
        if c:
            steps += [("norm0", h, c - 1)]
    steps += [("gate0", h, 0), ("gate0", h, 1), ("norm0", h, 3), ("norms0", h), ("gate0", h, 2), ("gate0", h, 3)]
    steps += [("v0", h, t, n) for t in range(TILES) for n in range(2)]
    return steps + [("gate0", h, m) for m in range(4, KI)]


def attention0(h):
    sub = [(t, p) for t in range(TILES) for p in range(2)]
    steps = []
    for i, (t, p) in enumerate(sub):
        steps.append(("score0", h, t, p))
        if i:
            steps.append(("mix0", h) + sub[i - 1])
        if i >= 3 and i % 2 == 1:
            steps.append(("turn0", h, sub[i - 3][0]))
    steps.append(("mix0", h) + sub[-1])
    return steps + [("turn0", h, TILES - 1)]


def attention1(h):
    sub = [(t, p) for t in range(TILES) for p in range(2)]
    steps = []
    for i in range(len(sub) + 3):
        if i < len(sub):
            steps.append(("score1", h) + sub[i])
        if 1 <= i <= len(sub):
            steps.append(("prob1", h) + sub[i - 1])
        if 2 <= i <= len(sub) + 1:
            steps.append(("mix1", h) + sub[i - 2])
        if i >= 4 and i % 2 == 0:
            steps.append(("turn1", h, sub[i - 4][0]))
    return steps


def outward(layer, h):
    return [("out", layer, h, m) for m in range(KD)]


def residual(layer, h):
    return [("add", layer, h, t) for t in range(TILES)] + [("ln", layer + 1, h)]


def ffn(h):
    steps = [("up", h, 0), ("up", h, 1), ("router", h), ("up", h, 2)]
    for e in range(EXPERTS):
        if e == 0:
            steps.append(("gates", h))
        steps.append(("down", h, e))
        if e + 3 < EXPERTS:
            steps.append(("up", h, e + 3))
    return steps + [("ffn_out", h)]


def layer1_dense(h):
    qk = [("qk1", h, c) for pair in range(KI) for c in (pair, KI + pair)]
    return qk + [("v1", h, t, n) for t in range(TILES) for n in range(2)]


def make_order():
    a, b = 0, 1
    ln_a, tok_a = token_steps(a)
    ln_b, tok_b = token_steps(b)
    order = [("consts",)] + ln_a + ln_b + tok_a + [("ln", 0, a)] + tok_b + [("ln", 0, b), ("turn", 0, a)]
    order += layer0_dense(a) + [("turn", 0, b)]
    order += weave(layer0_dense(b), attention0(a))
    order += outward(0, a) + [("quant_w",)] + residual(0, a)
    order += weave([("turn", 1, a)] + ffn(a), attention0(b)[:2] + attention0(b)[2:])
    order += outward(0, b) + residual(0, b) + residual(1, a)
    order += [("turn", 1, b)]
    order += weave(ffn(b), [("turn", 2, a)] + layer1_dense(a))
    order += weave(attention1(a), residual(1, b) + [("pause",), ("turn", 2, b)] + layer1_dense(b))
    fill = outward(2, a) + residual(2, a) + [("pause",)] * 3 + [("turn", 3, a)] + [("last", a, t) for t in range(TILES)]
    order += weave(attention1(b), fill)
    order += outward(2, b) + residual(2, b) + [("turn", 3, b)] + [("last", b, t) for t in range(TILES)]
    return order


ORDER = make_order()
LN_STEPS = [step[1:] for step in ORDER if step[0] == "ln"]
LN_NTH = {at: n for n, at in enumerate(LN_STEPS)}
MIX_KEYS = [step + (1,) * (step[0] == "mix1") for step in ORDER if step[0] in ("mix0", "mix1")]
PROB_KEYS = [step + (1,) for step in ORDER if step[0] == "prob1"]
TURN_KEYS = [step + (1,) for step in ORDER if step[0] in ("turn0", "turn1")]


def banks_of(step):
    kind = step[0]
    if kind in ("patch_t", "qk0", "v0", "gate0", "out", "up", "qk1", "v1", "embed", "last"):
        return [(step, DENSE)]
    if kind in ("router", "gates"):
        return [(step, DENSE)]
    if kind == "quant_w":
        return [((kind, n), DENSE) for n in range(2)]
    if kind in ("turn", "turn1"):
        return [(step + (m,), DENSE) for m in range(2)]
    if kind == "add":
        return [(step, DENSE)]
    if kind in ("score0", "score1"):
        return [(step + (j,), (SCORES[j],)) for j in range(2)]
    if kind == "mix0":
        return [(step, (4,))]
    if kind == "turn0":
        return [(step + (u,), (5,)) for u in range(2)]
    if kind == "norm0" and step[2] == 0:
        return [(("norms0", step[1]), (6,))]
    if kind == "down" and step[2] == 0:
        return [(("ffn", step[1], m), (6 + m,)) for m in range(KD)]
    if kind == "prob1":
        return [(step + (j,), (6 + j,)) for j in range(2)]
    if kind == "mix1":
        return [(step + (j,), (4 + j,)) for j in range(2)]
    return []


def psum_plan():
    plan, used, dense = {}, [0] * 8, 0
    for step in ORDER:
        for key, ring in banks_of(step):
            bank = ring[dense % len(ring)]
            dense += ring is DENSE
            plan[key] = (bank, used[bank])
            used[bank] += 1
    return plan


PSUM = psum_plan()


def vit_tower(nc, d, out):
    with ExitStack() as ctx:
        def sb(name, shape, dt=F32):
            return ctx.enter_context(nc.sbuf_tensor(name, shape, dt))

        def sem(name):
            return ctx.enter_context(nc.semaphore(name))

        def per_half(name):
            return [sem(f"{name}_{h}") for h in range(HALVES)]

        gates_dram = nc.dram_tensor("gates_dram", [HALVES, ROUTED, TOKENS], F32).ap()

        region = sb("proj_weights", [128, KP * DIM + KD * (QK_COLS + 2 * INNER)])
        w_patch = region[:, 0:KP * DIM].rearrange("p (k n) -> p k n", k=KP)
        ends = [KP * DIM + KD * n for n in (0, QK_COLS, QK_COLS + INNER, QK_COLS + 2 * INNER)]
        w_qk, w_gate, w_val = (region[:, ends[i]:ends[i + 1]].rearrange("p (k n) -> p k n", k=KD) for i in range(3))
        w1 = [region[:, i * KD * INNER:(i + 1) * KD * INNER].rearrange("p (k n) -> p k n", k=KD) for i in range(3)]
        w_out = sb("out_weights", [128, KI, DIM])
        w_up = sb("up_weights", [128, EXPERTS, KD, EXPERT])
        w_down = sb("down_weights", [128, EXPERTS, DIM])
        w_router = sb("router_weights", [128, KD, ROUTED])
        w_last = sb("last_weights", [128, KD, DIM])
        w_last_t = sb("last_weights_t", [128, KD, DIM], BF16)
        patch_g, patch_b = sb("patch_g", [128, KP]), sb("patch_b", [128, KP])
        row_b = sb("row_b", [1, DIM])
        is_patch = sb("is_patch", [1, TOKENS])
        out_b1 = sb("out_b1", [128, KD])
        last_b = sb("last_b", [MAX_ROWS, DIM])
        last_scale = sb("last_scale", [128, DIM])
        ident, ident_b = sb("ident", [128, 128]), sb("ident_b", [128, 128], BF16)
        same_image = sb("same_image", [MAX_ROWS, MAX_ROWS])
        masked = sb("masked", [MAX_ROWS, MAX_ROWS])
        masked_b = sb("masked_b", [MAX_ROWS, MAX_ROWS], BF16)
        head_sum = sb("head_sum", [128, 8])
        power = sb("power", [128, TILES])

        h_tok = [sb(f"h{h}", [MAX_ROWS, TILES, DIM]) for h in range(HALVES)]
        xn = [sb(f"xn{t}", [MAX_ROWS, DIM]) for t in range(TILES)]
        xn_t = [sb(f"xn_t{h}", [128, KD, TOKENS]) for h in range(HALVES)]
        qk = [sb(f"qk{h}", [128, 2 * KI, TOKENS]) for h in range(HALVES)]
        flat = [q[:, :, :].rearrange("p c n -> p (c n)") for q in qk]
        patch = [[flat[h][0:PATCH_ROWS[t], t * PATCH_DIM:(t + 1) * PATCH_DIM] for t in range(TILES)]
                 for h in range(HALVES)]
        patch_t = [flat[h][:, TILES * PATCH_DIM:TILES * PATCH_DIM + KP * TOKENS].rearrange("p (k n) -> p k n", k=KP)
                   for h in range(HALVES)]
        val = [sb(f"val{h}", [MAX_ROWS, TILES, HEADS, DV + 1]) for h in range(HALVES)]
        square = [sb(f"square{i}", [128, TOKENS]) for i in range(2)]
        half_tanh = [sb(f"half_tanh{i}", [128, TOKENS]) for i in range(2)]
        raw = [sb(f"raw{i}", [MAX_ROWS, 2, 4, MAX_ROWS]) for i in range(2)]
        prob = [sb(f"prob{i}", [MAX_ROWS, 2, 4, MAX_ROWS]) for i in range(2)]
        mix = [sb(f"mix{i}", [MAX_ROWS, INNER]) for i in range(2)]
        sq_val, sq_mix = sb("sq_val", [MAX_ROWS, 8 * DV]), sb("sq_mix", [MAX_ROWS, 8 * DV])
        y_t = [sb(f"y_t{h}", [128, KD, TOKENS]) for h in range(HALVES)]
        act_t = [sb(f"act_t{i}", [128, TOKENS]) for i in range(ACT_RING)]
        gate_bc = [sb(f"gate_bc{i}", [128, TOKENS]) for i in range(GATE_RING)]
        embed_b = act_t[3][0:MAX_ROWS, 0:DIM]
        embed_g, embed_add = (gate_bc[i][0:MAX_ROWS, 0:DIM] for i in (2, 3))
        xq_t = [gate_bc[h][:, :].bitcast(BF16).rearrange("p (k n) -> p k n", k=KD) for h in range(HALVES)]
        gate_t = [sb(f"gate_t{h}", [ROUTED, TOKENS]) for h in range(HALVES)]
        result = [act_t[t][0:MAX_ROWS, 0:DIM] for t in range(TILES)]

        stats = sb("stats", [MAX_ROWS, TILES, 2, 6])
        mean_var = sb("mean_var", [MAX_ROWS, TILES, 2])
        var_eps = sb("var_eps", [MAX_ROWS, TILES])
        rstd = sb("rstd", [MAX_ROWS, TILES])
        qk_sq = [sb(f"qk_sq{h}", [MAX_ROWS, TILES, 2, HEADS]) for h in range(HALVES)]
        qk_inv = [sb(f"qk_inv{h}", [MAX_ROWS, TILES, 2, HEADS]) for h in range(HALVES)]
        v_sq, v_scale = sb("v_sq", [MAX_ROWS, HEADS]), sb("v_scale", [MAX_ROWS, HEADS])
        o_sq, o_norm = sb("o_sq", [MAX_ROWS, HEADS]), sb("o_norm", [MAX_ROWS, HEADS])
        root, root_t = sb("root", [MAX_ROWS, HEADS]), sb("root_t", [MAX_ROWS, HEADS])
        o_tanh, o_inv, o_fac = (sb(n, [MAX_ROWS, HEADS]) for n in ("o_tanh", "o_inv", "o_fac"))
        row_max = [sb(f"row_max{j}", [MAX_ROWS, 4]) for j in range(2)]
        row_inv = [sb(f"row_inv{j}", [MAX_ROWS, 4]) for j in range(2)]
        logits = sb("logits", [MAX_ROWS, TILES, ROUTED])
        exps = sb("exps", [MAX_ROWS, TILES, ROUTED])
        top_stat = sb("top_stat", [MAX_ROWS, 3, TILES])
        probs = sb("probs", [MAX_ROWS, TILES, ROUTED + 4])
        rest = sb("rest", [MAX_ROWS, TILES, ROUTED + 4])
        top8 = sb("top8", [MAX_ROWS, TILES, 8])
        pads = sb("pads", [MAX_ROWS, TILES, 4])
        gate = sb("gate", [MAX_ROWS, TILES, ROUTED])
        q_stat = sb("q_stat", [MAX_ROWS, 2, TILES])
        q_scale = [sb(f"q_scale{h}", [MAX_ROWS, TILES]) for h in range(HALVES)]
        wq_stat, wq_scale = sb("wq_stat", [128, 2, KD]), sb("wq_scale", [128, KD])

        bank = [ctx.enter_context(nc.psum_tensor(f"bank{i}", [128, 512], F32)) for i in range(8)]

        full = [sem(f"full{i}") for i in range(8)]
        free = [sem(f"free{i}") for i in range(8)]
        loads = {}
        zeroed = sem("zeroed")
        dve_chain, pool_chain = sem("dve_chain"), sem("pool_chain")
        stat_ready, rstd_ready = sem("stat_ready"), sem("rstd_ready")
        patch_normed = per_half("patch_normed")
        z_normed = per_half("z_normed")
        h_embedded = per_half("h_embedded")
        xn_ready = sem("xn_ready")
        squared, summed = sem("squared"), sem("summed")
        qk_inv_ready = per_half("qk_inv_ready")
        v_copied, v_summed = sem("v_copied"), sem("v_summed")
        v_ready = per_half("v_ready")
        tanh1_ready = sem("tanh1_ready")
        gate_ready = per_half("gate_ready")
        exp_ready = sem("exp_ready")
        prob_ready = sem("prob_ready")
        mix_copied, mix_summed = sem("mix_copied"), sem("mix_summed")
        norm_ready, norm_tanh = sem("norm_ready"), sem("norm_tanh")
        mix_ready = sem("mix_ready")
        logit_ready, expd = sem("logit_ready"), sem("expd")
        gated_rows = sem("gated_rows")
        gate_stored = sem("gate_stored")
        gate_loaded = [sem(f"gate_loaded{i}") for i in range(GATE_RING)]
        gated, act_used = sem("gated"), sem("act_used")
        wq_ready, masks_ready = sem("wq_ready"), sem("masks_ready")
        h_biased = per_half("h_biased")
        result_ready = sem("result_ready")
        stored = [sem(f"stored{t}") for t in range(TILES)]

        def loaded(eng, *names):
            for name in names:
                eng.wait_ge(loads[name], 16)

        def wait_full(eng, key):
            b, before = PSUM[key]
            eng.wait_ge(full[b], before + 1)
            return bank[b]

        def bank_read(key):
            return free[PSUM[key][0]]

        def wait_read(eng, key):
            b, before = PSUM[key]
            eng.wait_ge(free[b], before + 1)

        def spread(ap, n):
            return ap.unsqueeze(2).to_broadcast([ap.shape[0], ap.shape[1], n])

        x_dram = d["patches"]
        first = [(f"x{h}{t}", patch[h][t], x_dram[h, PATCH_START[t]:PATCH_START[t] + PATCH_ROWS[t], :])
                 for h in range(HALVES) for t in range(TILES)]
        small = [("ident", ident[:, :], d["ident"]), ("patch_g", patch_g[:, :], d["patch_g"]),
                 ("patch_b", patch_b[:, :], d["patch_b"]), ("row_b", row_b[:, :], d["row_b"]),
                 ("is_patch", is_patch[:, :], d["is_patch"]), ("embed_g", embed_g[:, :], d["embed_g"]),
                 ("embed_add", embed_add[:, :], d["embed_pos"]), ("embed_b", embed_b[:, :], d["embed_b"]),
                 ("same_image", same_image[:, :], d["same_image"]), ("masked", masked[:, :], d["masked"]),
                 ("head_sum", head_sum[:, :], d["head_sum"])]
        w_layer0 = [(name, w, d[name].rearrange("(k p) n -> p k n", p=128))
                    for name, w in (("w_qk", w_qk), ("w_val", w_val), ("w_gate", w_gate))]
        w_experts = []
        for i in range(0, EXPERTS, 6):
            w_experts += [(f"w_up{i}", w_up[:, i:i + 6, :, :], d["w_up"][:, i:i + 6, :, :]),
                          (f"w_down{i}", w_down[:, i:i + 6, :], d["w_down"][:, i:i + 6, :])]
        plan_sync = first[:TILES] + [("w_patch", w_patch, d["w_patch"].rearrange("(k p) n -> p k n", p=128))] \
            + first[TILES:] + w_layer0 + [("w_out", w_out[:, :, :], d["w_out"].rearrange("(k p) n -> p k n", p=128))] \
            + w_experts
        late = [("w_router", w_router[:, :, :], d["w_router"]),
                ("w_last", w_last[:, :, :], d["w_last"].rearrange("(k p) n -> p k n", p=128)),
                ("out_b1", out_b1[:, :], d["out_b1"]), ("last_b", last_b[:, :], d["last_b"])]
        w_layer1 = [(f"w1{i}", w1[i], d[name].rearrange("(k p) n -> p k n", p=128))
                    for i, name in enumerate(("w_q1", "w_k1", "w_v1"))]
        w_layer1_out = ("w_out1", w_out[:, :, :], d["w_out1"].rearrange("(k p) n -> p k n", p=128))
        for name, _, _ in plan_sync + small + late + w_layer1 + [w_layer1_out]:
            loads[name] = sem(f"load_{name}")

        block = ctx.enter_context(nc.Block())

        @block.sync
        def _(sp):
            for name, to, src in plan_sync:
                sp.dma_start(to, src).then_inc(loads[name], 16)
            for name, to, src in late:
                sp.dma_start(to, src).then_inc(loads[name], 16)
            for step in ORDER:
                if step[0] == "gates":
                    h = step[1]
                    wait_read(sp, ("gates", h))
                    sp.dma_start(gates_dram[h], gate_t[h][:, :]).then_inc(gate_stored, 16)
                    if h == 0:
                        wait_full(sp, ("gate0", HALVES - 1, KI - 1))
                        for name, to, src in w_layer1:
                            sp.dma_start(to, src).then_inc(loads[name], 16)
                    sp.wait_ge(gate_stored, 16 * (h + 1))
                    for r in range(ROUTED):
                        n = ROUTED * h + r
                        if n >= GATE_RING:
                            sp.wait_ge(gated, n - GATE_RING + 1)
                        sp.dma_start(gate_bc[n % GATE_RING][:, :],
                                     gates_dram[h, r:r + 1, :].to_broadcast([128, TOKENS])
                                     ).then_inc(gate_loaded[n % GATE_RING], 16)
                    if h == 0:
                        for half in range(HALVES):
                            wait_full(sp, ("out", 0, half, KD - 1))
                        name, to, src = w_layer1_out
                        sp.dma_start(to, src).then_inc(loads[name], 16)
                if step[0] == "last":
                    _, h, t = step
                    sp.wait_ge(result_ready, TILES * h + t + 1)
                    r0 = h * TOKENS + START[t]
                    sp.dma_start(out[r0:r0 + ROWS[t], :], result[t][0:ROWS[t], :]).then_inc(stored[t], 16)
            for t in range(TILES):
                sp.wait_ge(stored[t], 16 * HALVES)

        @block.tensor
        def _(pe):
            def claim(key):
                b, before = PSUM[key]
                if before:
                    pe.wait_ge(free[b], before)
                return bank[b]

            def filled(key, last):
                last.then_inc(full[PSUM[key][0]], 1)

            def patch_turn(h, c):
                key = ("patch_t", h, c)
                if c == 0:
                    loaded(pe, "ident")
                    pe.wait_ge(patch_normed[h], TILES)
                b = claim(key)
                for t in range(TILES):
                    last = pe.transpose(b[:, PATCH_START[t]:PATCH_START[t] + PATCH_ROWS[t]],
                                        patch[h][t][:, c * 128:(c + 1) * 128],
                                        ident[0:PATCH_ROWS[t], 0:PATCH_ROWS[t]])
                filled(key, last)

            def embed(h, t):
                key = ("embed", h, t)
                if t == 0:
                    loaded(pe, "w_patch", "row_b", "is_patch")
                    pe.wait_ge(zeroed, 1)
                    wait_read(pe, ("patch_t", h, KP - 1))
                b = claim(key)[0:ROWS[t], 0:DIM]
                cols = slice(START[t], START[t] + ROWS[t])
                for k in range(KP):
                    pe.matmul(b, patch_t[h][:, k, cols], w_patch[:, k, :], start=(k == 0), stop=False)
                filled(key, pe.matmul(b, is_patch[:, cols], row_b[:, :], start=False, stop=True))

            def turn(layer, h):
                pe.wait_ge(xn_ready, TILES * (LN_NTH[layer, h] + 1))
                for m in range(KD):
                    key = ("turn", layer, h, m)
                    b = claim(key)
                    for t in range(TILES):
                        last = pe.transpose(b[:, START[t]:START[t] + ROWS[t]],
                                            xn[t][0:ROWS[t], m * 128:(m + 1) * 128], ident[0:ROWS[t], 0:ROWS[t]])
                    filled(key, last)

            def dense(key, h, weights, b=None):
                b = claim(key) if b is None else b
                for k in range(KD):
                    last = pe.matmul(b[:, 0:TOKENS], weights(k), xn_t[h][:, k, :],
                                     start=(k == 0), stop=(k == KD - 1))
                filled(key, last)

            def token_product(key, h, t, weights, cols):
                b = claim(key)[0:ROWS[t], 0:cols]
                for k in range(KD):
                    last = pe.matmul(b, xn_t[h][:, k, START[t]:START[t] + ROWS[t]], weights(k),
                                     start=(k == 0), stop=(k == KD - 1))
                filled(key, last)

            def qk0(h, c):
                if c == 0:
                    loaded(pe, "w_qk")
                    wait_read(pe, ("turn", 0, h, KD - 1))
                col = 128 * (c % 4) + DK * (c // 4)
                dense(("qk0", h, c), h, lambda k: w_qk[:, k, col:col + 128])

            def norm0(h, c):
                key = ("norms0", h)
                if c == 0:
                    loaded(pe, "head_sum")
                    claim(key)
                n = 4 * h + c
                pe.wait_ge(squared, n + 1)
                b = bank[PSUM[key][0]]
                for t in range(TILES):
                    col = 32 * t + 8 * c
                    last = pe.matmul(b[0:ROWS[t], col:col + 8], square[n % 2][:, START[t]:START[t] + ROWS[t]],
                                     head_sum[:, :], start=True, stop=True)
                if c < 3:
                    last.then_inc(summed, 1)
                else:
                    filled(key, last)

            def score0(h, t, p):
                if (t, p) == (0, 0):
                    wait_read(pe, ("qk0", h, 7))
                cols = slice(START[t], START[t] + ROWS[t])
                banks = [claim(("score0", h, t, p, j)) for j in range(2)]
                last = [None, None]
                for c in range(4):
                    for j in range(2):
                        at = slice(32 * (2 * p + j), 32 * (2 * p + j) + DK)
                        last[j] = pe.matmul(banks[j][0:ROWS[t], c * ROWS[t]:(c + 1) * ROWS[t]],
                                            qk[h][at, 4 + c, cols], qk[h][at, c, cols], start=True, stop=True,
                                            tile_position=(32 * (2 * p + j), 0))
                for j in range(2):
                    filled(("score0", h, t, p, j), last[j])

            def mix0(h, t, p):
                n = 6 * h + 2 * t + p
                key = ("mix0", h, t, p)
                pe.wait_ge(prob_ready, n + 1)
                pe.wait_ge(v_ready[h], t + 1)
                b = claim(key)
                for c in range(4):
                    for j in range(2):
                        last = pe.matmul(b[0:ROWS[t], (2 * c + j) * DV:(2 * c + j + 1) * DV],
                                         prob[n % 2][0:ROWS[t], j, c, 0:ROWS[t]],
                                         val[h][0:ROWS[t], t, 4 * c + 2 * p + j, 0:DV], start=True, stop=True)
                filled(key, last)

            def turn0(h, t):
                n = 3 * h + t
                pe.wait_ge(mix_ready, n + 1)
                for u in range(2):
                    key = ("turn0", h, t, u)
                    b = claim(key)
                    for q in range(4):
                        c = 4 * u + q
                        last = pe.transpose(b[:, q * ROWS[t]:(q + 1) * ROWS[t]],
                                            mix[n % 2][0:ROWS[t], c * 128:(c + 1) * 128],
                                            ident[0:ROWS[t], 0:ROWS[t]])
                    filled(key, last)

            def out_product(layer, h, m):
                key = ("out", layer, h, m)
                if m == 0:
                    loaded(pe, "w_out" if layer == 0 else "w_out1")
                    wait_read(pe, ("turn0" if layer == 0 else "turn1", h, TILES - 1, 1))
                src = qk[h][:, KI:2 * KI, :] if layer == 0 else qk[h][:, 0:KI, :]
                b = claim(key)
                for k in range(KI):
                    last = pe.matmul(b[:, 0:TOKENS], w_out[:, k, m * 128:(m + 1) * 128], src[:, k, :],
                                     start=(k == 0), stop=(k == KI - 1))
                filled(key, last)

            def add(layer, h, t):
                key = ("add", layer, h, t)
                if t == 0:
                    wait_read(pe, ("ffn", h, KD - 1) if layer == 1 else ("out", layer, h, KD - 1))
                b = claim(key)
                for m in range(KD):
                    last = pe.transpose(b[0:ROWS[t], m * 128:(m + 1) * 128],
                                        y_t[h][:, m, START[t]:START[t] + ROWS[t]], ident[:, :])
                filled(key, last)

            def router(h):
                key = ("router", h)
                if h == 0:
                    loaded(pe, "w_router")
                b = claim(key)
                for t in range(TILES):
                    for k in range(KD):
                        last = pe.matmul(b[0:ROWS[t], ROUTED * t:ROUTED * (t + 1)],
                                         xn_t[h][:, k, START[t]:START[t] + ROWS[t]], w_router[:, k, :],
                                         start=(k == 0), stop=(k == KD - 1))
                filled(key, last)

            def gates(h):
                key = ("gates", h)
                pe.wait_ge(gated_rows, h + 1)
                b = claim(key)
                for t in range(TILES):
                    last = pe.transpose(b[0:ROUTED, START[t]:START[t] + ROWS[t]], gate[0:ROWS[t], t, :],
                                        ident[0:ROWS[t], 0:ROWS[t]])
                filled(key, last)

            def up(h, e):
                if e == 0:
                    wait_read(pe, ("turn", 1, h, KD - 1))
                if h == 0 and e % 6 == 0:
                    loaded(pe, f"w_up{e}")
                dense(("up", h, e), h, lambda k: w_up[:, e, k, :])

            def down(h, e):
                n = EXPERTS * h + e
                if h == 0 and e % 6 == 0:
                    loaded(pe, f"w_down{e}")
                if e < SHARED:
                    wait_read(pe, ("up", h, e))
                else:
                    pe.wait_ge(gated, ROUTED * h + e - SHARED + 1)
                for m in range(KD):
                    key = ("ffn", h, m)
                    b = claim(key) if e == 0 else bank[PSUM[key][0]]
                    last = pe.matmul(b[:, 0:TOKENS], w_down[:, e, m * 128:(m + 1) * 128],
                                     act_t[n % ACT_RING][:, :], start=(e == 0), stop=(e == EXPERTS - 1))
                    if e == EXPERTS - 1:
                        filled(key, last)
                if e < EXPERTS - 1:
                    last.then_inc(act_used, 1)

            def qk1(h, c):
                if c == 0:
                    wait_read(pe, ("turn", 2, h, KD - 1))
                    loaded(pe, "w10", "w11")
                w, m = (w1[0], c) if c < KI else (w1[1], c - KI)
                dense(("qk1", h, c), h, lambda k: w[:, k, m * 128:(m + 1) * 128])

            def score1(h, t, u):
                if (t, u) == (0, 0):
                    pe.wait_ge(masks_ready, 1)
                    wait_read(pe, ("qk1", h, KI - 1))
                    wait_read(pe, ("qk1", h, 2 * KI - 1))
                cols = slice(START[t], START[t] + ROWS[t])
                banks = [claim(("score1", h, t, u, j)) for j in range(2)]
                for j in range(2):
                    pe.matmul(banks[j][0:ROWS[t], 0:4 * ROWS[t]], ident_b[0:ROWS[t], 0:ROWS[t]],
                              masked_b[0:ROWS[t], 0:ROWS[t]].unsqueeze(1).to_broadcast([ROWS[t], 4, ROWS[t]]),
                              start=True, stop=False, skip_group_check=True)
                last = [None, None]
                for q in range(4):
                    for j in range(2):
                        at = slice(64 * j, 64 * j + 64)
                        last[j] = pe.matmul(banks[j][0:ROWS[t], q * ROWS[t]:(q + 1) * ROWS[t]],
                                            qk[h][at, 4 * u + q, cols], qk[h][at, KI + 4 * u + q, cols],
                                            start=False, stop=True, skip_group_check=True,
                                            tile_position=(64 * j, 0))
                for j in range(2):
                    filled(("score1", h, t, u, j), last[j])

            def prob1(h, t, u):
                n = 12 + 6 * h + 2 * t + u
                pe.wait_ge(exp_ready, n - 12 + 1)
                for j in range(2):
                    key = ("prob1", h, t, u, j)
                    b = claim(key)
                    for q in range(4):
                        last = pe.transpose(b[0:ROWS[t], q * ROWS[t]:(q + 1) * ROWS[t]],
                                            raw[n % 2][0:ROWS[t], j, q, 0:ROWS[t]], ident[0:ROWS[t], 0:ROWS[t]])
                    filled(key, last)

            def mix1(h, t, u):
                n = 12 + 6 * h + 2 * t + u
                wait_read(pe, ("prob1", h, t, u, 1))
                wait_read(pe, ("v1", h, t, 0))
                wait_read(pe, ("v1", h, t, 1))
                for j in range(2):
                    key = ("mix1", h, t, u, j)
                    b = claim(key)
                    for q in range(4):
                        last = pe.matmul(b[0:ROWS[t], q * (DV + 1):(q + 1) * (DV + 1)],
                                         prob[n % 2][0:ROWS[t], j, q, 0:ROWS[t]],
                                         val[h][0:ROWS[t], t, 2 * (4 * u + q) + j, :], start=True, stop=True)
                    filled(key, last)

            def turn1(h, t):
                n = 6 + 3 * h + t
                wait_read(pe, ("mix1", h, t, 1, 1))
                for u in range(2):
                    key = ("turn1", h, t, u)
                    b = claim(key)
                    for q in range(4):
                        c = 4 * u + q
                        last = pe.transpose(b[:, q * ROWS[t]:(q + 1) * ROWS[t]],
                                            mix[n % 2][0:ROWS[t], c * 128:(c + 1) * 128],
                                            ident[0:ROWS[t], 0:ROWS[t]])
                    filled(key, last)

            def quant_w():
                pe.wait_ge(wq_ready, 1)
                b = claim(("quant_w", 0))
                for k in range(KD):
                    for m in range(KD):
                        last = pe.transpose(b[:, k * DIM + m * 128:k * DIM + (m + 1) * 128],
                                            w_last[:, m, k * 128:(k + 1) * 128], ident[:, :])
                filled(("quant_w", 0), last)
                b = claim(("quant_w", 1))
                for m in range(KD):
                    last = pe.matmul(b[:, m * 128:(m + 1) * 128], wq_scale[:, m:m + 1].to_broadcast([128, 128]),
                                     ident[:, :], start=True, stop=True)
                filled(("quant_w", 1), last)

            def last_product(h, t):
                if t == 0:
                    wait_read(pe, ("turn", 3, h, KD - 1))
                    wait_read(pe, ("quant_w", 0))
                key = ("last", h, t)
                b = claim(key)[0:ROWS[t], 0:DIM]
                for k in range(KD):
                    last = pe.matmul(b, xq_t[h][:, k, START[t]:START[t] + ROWS[t]], w_last_t[:, k, :],
                                     start=(k == 0), stop=(k == KD - 1))
                filled(key, last)

            for step in ORDER:
                kind, at = step[0], step[1:]
                if kind == "patch_t":
                    patch_turn(*at)
                elif kind == "embed":
                    embed(*at)
                elif kind == "turn":
                    turn(*at)
                elif kind == "qk0":
                    qk0(*at)
                elif kind == "norm0":
                    norm0(*at)
                elif kind == "v0":
                    h, t, n = at
                    if (t, n) == (0, 0):
                        loaded(pe, "w_val")
                    token_product(step, h, t, lambda k: w_val[:, k, 512 * n:512 * (n + 1)], 8 * DV)
                elif kind == "gate0":
                    h, m = at
                    if m == 0:
                        loaded(pe, "w_gate")
                    dense(step, h, lambda k: w_gate[:, k, m * 128:(m + 1) * 128])
                elif kind == "score0":
                    score0(*at)
                elif kind == "mix0":
                    mix0(*at)
                elif kind == "turn0":
                    turn0(*at)
                elif kind == "out":
                    out_product(*at)
                elif kind == "add":
                    add(*at)
                elif kind == "router":
                    router(*at)
                elif kind == "gates":
                    gates(*at)
                elif kind == "up":
                    up(*at)
                elif kind == "down":
                    down(*at)
                elif kind == "qk1":
                    qk1(*at)
                elif kind == "v1":
                    h, t, n = at
                    if (t, n) == (0, 0):
                        loaded(pe, "w12")
                    token_product(step, h, t, lambda k: w1[2][:, k, 512 * n:512 * (n + 1)], 8 * DV)
                elif kind == "score1":
                    score1(*at)
                elif kind == "prob1":
                    prob1(*at)
                elif kind == "mix1":
                    mix1(*at)
                elif kind == "turn1":
                    turn1(*at)
                elif kind == "quant_w":
                    quant_w()
                elif kind == "last":
                    last_product(*at)

        @block.scalar
        def _(act):
            for name, to, src in small:
                act.dma_start(to, src).then_inc(loads[name], 16)
            act.preload_act_table(ACT.Gelu)

            def copy_out(key, to, cols, rows=128, func=ACT.Copy, **kw):
                b = wait_full(act, key)
                return act.activation(to, b[0:rows, 0:cols], func, **kw).then_inc(bank_read(key), 1)

            gate_pending = []

            def gate_tanh():
                h, m = gate_pending.pop(0)
                wait_read(act, ("gate0", h, m))
                act.activation(qk[h][:, KI + m, :], half_tanh[m % 2][:, :], ACT.Tanh, scale=0.5
                               ).then_inc(gate_ready[h], 1)

            for step in ORDER:
                kind, at = step[0], step[1:]
                if kind != "gate0" and gate_pending and len(gate_pending) > 0:
                    while gate_pending:
                        gate_tanh()
                if kind == "patch_t":
                    h, c = at
                    if c == 0:
                        loaded(act, "patch_g", "patch_b")
                    to = patch_t[h][:, c, :].rearrange("p (s n) -> p s n", n=SEQ)[:, :, 1:SEQ]
                    b = wait_full(act, step)
                    act.activation(to, b[:, 0:IMAGES * PATCHES].rearrange("p (s n) -> p s n", n=PATCHES),
                                   ACT.Identity, scale=patch_g[:, c:c + 1], bias=patch_b[:, c:c + 1]
                                   ).then_inc(bank_read(step), 1)
                elif kind == "embed":
                    h, t = at
                    copy_out(step, h_tok[h][0:ROWS[t], t, :], DIM, ROWS[t])
                elif kind == "turn":
                    layer, h = at
                    for m in range(KD):
                        key = step + (m,)
                        copy_out(key, (xq_t if layer == 3 else xn_t)[h][:, m, :], TOKENS)
                elif kind == "qk0":
                    h, c = at
                    copy_out(step, qk[h][:, c, :], TOKENS)
                elif kind in ("v0", "v1"):
                    h, t, n = at
                    if kind == "v0" or n == 0:
                        b = wait_full(act, step)
                        last = act.activation(val[h][0:ROWS[t], t, 8 * n:8 * n + 8, 0:DV],
                                              b[0:ROWS[t], :].rearrange("p (h n) -> p h n", n=DV), ACT.Copy)
                        if kind == "v0":
                            last.then_inc(v_copied, 1)
                            i = 2 * (TILES * h + t) + n
                            if i:
                                act.wait_ge(v_summed, i)
                            last = act.activation(sq_val[0:ROWS[t], :], b[0:ROWS[t], :], ACT.Square)
                        last.then_inc(bank_read(step), 1)
                elif kind == "gate0":
                    h, m = at
                    b = wait_full(act, step)
                    if m >= 2:
                        act.wait_ge(gate_ready[h], m - 1)
                    elif h:
                        act.wait_ge(gate_ready[h - 1], KI)
                    act.activation(half_tanh[m % 2][:, :], b[:, 0:TOKENS], ACT.Tanh, scale=0.5
                                   ).then_inc(tanh1_ready, 1)
                    gate_pending.append((h, m))
                    if len(gate_pending) == 2:
                        gate_tanh()
                    if m == KI - 1:
                        gate_tanh()
                elif kind == "score0":
                    h, t, p = at
                    n = 6 * h + 2 * t + p
                    wait_read(act, step + (1,))
                    if n >= 2:
                        wait_full(act, MIX_KEYS[n - 2])
                    act.activation(prob[n % 2][0:ROWS[t], :, :, 0:ROWS[t]].rearrange("p j c n -> p (j c) n"),
                                   raw[n % 2][0:ROWS[t], :, :, 0:ROWS[t]].rearrange("p j c n -> p (j c) n"),
                                   ACT.Square).then_inc(prob_ready, 1)
                elif kind == "mix0":
                    h, t, p = at
                    n = 3 * h + t
                    if n >= 2:
                        wait_full(act, TURN_KEYS[n - 2])
                    b = wait_full(act, step)
                    to = mix[n % 2][0:ROWS[t], :].rearrange("p (c n) -> p c n", c=4)[:, :, 2 * p * DV:2 * (p + 1) * DV]
                    act.activation(to, b[0:ROWS[t], :].rearrange("p (c n) -> p c n", c=4), ACT.Copy
                                   ).then_inc(mix_copied, 1)
                    if 2 * n + p:
                        act.wait_ge(mix_summed, 2 * n + p)
                    act.activation(sq_mix[0:ROWS[t], :], b[0:ROWS[t], :], ACT.Square).then_inc(bank_read(step), 1)
                    if p == 1:
                        act.wait_ge(norm_ready, n + 1)
                        act.activation(o_tanh[0:ROWS[t], :], o_norm[0:ROWS[t], :], ACT.Tanh).then_inc(norm_tanh, 1)
                elif kind == "out":
                    layer, h, m = at
                    if layer == 2:
                        loaded(act, "out_b1")
                        copy_out(step, y_t[h][:, m, :], TOKENS, func=ACT.Identity, bias=out_b1[:, m:m + 1])
                    else:
                        copy_out(step, y_t[h][:, m, :], TOKENS)
                elif kind == "router":
                    h = at[0]
                    act.wait_ge(logit_ready, h + 1)
                    act.activation(exps[:, :, :], exps[:, :, :], ACT.Exp).then_inc(expd, 1)
                elif kind == "gates":
                    h = at[0]
                    copy_out(step, gate_t[h][:, :], TOKENS, ROUTED)
                elif kind == "up":
                    h, e = at
                    n = EXPERTS * h + e
                    if n >= ACT_RING:
                        before = n - ACT_RING
                        if before % EXPERTS == EXPERTS - 1:
                            wait_full(act, ("ffn", before // EXPERTS, KD - 1))
                        else:
                            act.wait_ge(act_used, before + 1 - before // EXPERTS)
                    copy_out(step, act_t[n % ACT_RING][:, :], TOKENS, func=ACT.Gelu)
                elif kind == "ffn_out":
                    h = at[0]
                    for m in range(KD):
                        key = ("ffn", h, m)
                        copy_out(key, y_t[h][:, m, :], TOKENS)
                elif kind == "qk1":
                    h, c = at
                    if c >= KI:
                        copy_out(step, qk[h][:, c, :], TOKENS)
                elif kind == "score1":
                    h, t, u = at
                    n = 12 + 6 * h + 2 * t + u
                    wait_read(act, step + (1,))
                    view = raw[n % 2][0:ROWS[t], :, :, 0:ROWS[t]].rearrange("p j c n -> p (j c) n")
                    act.activation(view, view, ACT.Exp, scale=DV ** -0.5).then_inc(exp_ready, 1)
                elif kind == "prob1":
                    h, t, u = at
                    n = 12 + 6 * h + 2 * t + u
                    wait_full(act, MIX_KEYS[n - 2])
                    for j in range(2):
                        key = step + (j,)
                        b = wait_full(act, key)
                        act.activation(prob[n % 2][0:ROWS[t], j, :, 0:ROWS[t]],
                                       b[0:ROWS[t], 0:4 * ROWS[t]].rearrange("p (c n) -> p c n", c=4), ACT.Copy
                                       ).then_inc(bank_read(key), 1)
                elif kind == "turn1":
                    h, t = at
                    for u in range(2):
                        key = step + (u,)
                        b = wait_full(act, key)
                        act.activation(qk[h][:, 4 * u:4 * u + 4, START[t]:START[t] + ROWS[t]],
                                       b[:, 0:4 * ROWS[t]].rearrange("p (c n) -> p c n", c=4), ACT.Copy
                                       ).then_inc(bank_read(key), 1)
                elif kind == "quant_w":
                    copy_out(("quant_w", 0), w_last_t[:, :, :].rearrange("p k n -> p (k n)"), KD * DIM)
                    copy_out(("quant_w", 1), last_scale[:, :], DIM)

        @block.vector
        def _(dve):
            chained = [0]
            stat_n = [0]

            def link(ins):
                chained[0] += 1
                ins.then_inc(dve_chain, 1)
                dve.wait_ge(dve_chain, chained[0])

            def reciprocal_root(x, rows):
                y, t = root[0:rows, :], root_t[0:rows, :]
                link(dve.tensor_scalar(t.bitcast(I32), x.bitcast(I32), 1, None, ALU.logical_shift_right))
                link(dve.tensor_scalar(y.bitcast(I32), t.bitcast(I32), -1.0, float(0x5f3759df),
                                       ALU.mult, ALU.add))
                for _ in range(3):
                    link(dve.scalar_tensor_tensor(out=t, in0=y, scalar=-0.5, in1=y, op0=ALU.mult, op1=ALU.mult))
                    link(dve.tensor_tensor(t, t, x, ALU.mult))
                    link(dve.scalar_tensor_tensor(out=y, in0=t, scalar=1.5, in1=y, op0=ALU.add, op1=ALU.mult))

            def constants():
                dve.memset(mean_var[:, :, :], 1.0)
                dve.memset(logits[:, :, :], 0.0)
                for h in range(HALVES):
                    dve.memset(qk_sq[h][:, :, :, :], 1.0)
                for i in range(4):
                    dve.memset(pads[:, :, i:i + 1], -5.0 - i)
                link(dve.memset(q_stat[:, :, :], 1.0))
                for h in range(HALVES):
                    last = dve.memset(val[h][:, :, :, DV:DV + 1], 1.0)
                link(last)
                for t in range(TILES):
                    dve.tensor_copy(probs[:, t, ROUTED:], pads[:, t, :])

            def statistics(tiles, width):
                parts = -(-width // 512)
                w = width // parts
                for t, tile in enumerate(tiles):
                    for i in range(parts):
                        last = dve.bn_stats(stats[0:tile.shape[0], t, i, :], tile[:, i * w:(i + 1) * w])
                link(last)
                for t, tile in enumerate(tiles):
                    last = dve.bn_aggr(mean_var[0:tile.shape[0], t, :],
                                       stats[0:tile.shape[0], t, 0:parts, :].rearrange("p a b -> p (a b)"))
                last.then_inc(stat_ready, 1)
                stat_n[0] += 1
                dve.wait_ge(rstd_ready, stat_n[0])

            def normalise(to, tile, t):
                rows = tile.shape[0]
                return dve.tensor_scalar(to, tile, mean_var[0:rows, t, 0:1], rstd[0:rows, t:t + 1],
                                         ALU.subtract, ALU.mult)

            def quantise(tiles, stat, scale, n):
                for t, tile in enumerate(tiles):
                    last = dve.tensor_reduce(stat[0:tile.shape[0], 0, t:t + 1], tile, AX, ALU.max,
                                             apply_absolute_value=True)
                link(last)
                link(dve.tensor_scalar(scale[:, :], stat[:, 0, :], 1e-8, 1.0 / QMAX, ALU.max, ALU.mult))
                link(dve.reciprocal(stat[:, 1, :], scale[:, :]))
                for t, tile in enumerate(tiles):
                    last = dve.tensor_scalar(tile, tile, stat[0:tile.shape[0], 1, t:t + 1], ROUND,
                                             ALU.mult, ALU.add)
                link(last)
                for t, tile in enumerate(tiles):
                    last = dve.tensor_scalar(tile, tile, ROUND, None, ALU.subtract)
                    yield last

            def route(h):
                b = wait_full(dve, ("router", h))
                for t in range(TILES):
                    last = dve.tensor_copy(logits[0:ROWS[t], t, :], b[0:ROWS[t], ROUTED * t:ROUTED * (t + 1)])
                last.then_inc(bank_read(("router", h)), 1)
                wait_read(dve, ("router", h))
                link(dve.tensor_reduce(top_stat[:, 0, :], logits[:, :, :], AX, ALU.max))
                dve.tensor_tensor(exps[:, :, :], logits[:, :, :], spread(top_stat[:, 0, :], ROUTED), ALU.subtract
                                  ).then_inc(logit_ready, 1)
                dve.wait_ge(expd, h + 1)
                link(dve.tensor_reduce(top_stat[:, 1, :], exps[:, :, :], AX, ALU.add))
                link(dve.reciprocal(top_stat[:, 2, :], top_stat[:, 1, :]))
                link(dve.tensor_tensor(probs[:, :, 0:ROUTED], exps[:, :, :], spread(top_stat[:, 2, :], ROUTED),
                                       ALU.mult))
                for t in range(TILES):
                    last = dve.max(top8[:, t, :], probs[:, t, 0:ROUTED])
                link(last)
                link(dve.tensor_copy(top8[:, :, TOP_K:], pads[:, :, :]))
                for t in range(TILES):
                    last = dve.match_replace(out=rest[:, t, :], in_to_replace=top8[:, t, :],
                                             in_values=probs[:, t, :], imm_value=0.0)
                link(last)
                dve.tensor_tensor(gate[:, :, :], probs[:, :, 0:ROUTED], rest[:, :, 0:ROUTED], ALU.subtract
                                  ).then_inc(gated_rows, 1)

            for step in ORDER:
                kind, at = step[0], step[1:]
                if kind == "consts":
                    constants()
                elif kind == "patch_ln":
                    h = at[0]
                    loaded(dve, *(f"x{h}{t}" for t in range(TILES)))
                    statistics(patch[h], PATCH_DIM)
                    for t in range(TILES):
                        normalise(patch[h][t], patch[h][t], t).then_inc(patch_normed[h], 1)
                elif kind == "ln":
                    layer, h = at
                    rows = [h_tok[h][0:ROWS[t], t, :] for t in range(TILES)]
                    if layer == 0:
                        wait_read(dve, ("embed", h, TILES - 1))
                        statistics(rows, DIM)
                        for t in range(TILES):
                            normalise(rows[t], rows[t], t).then_inc(z_normed[h], 1)
                        dve.wait_ge(h_embedded[h], TILES)
                    else:
                        wait_read(dve, ("add", layer - 1, h, TILES - 1))
                    statistics(rows, DIM)
                    if LN_NTH[layer, h]:
                        wait_full(dve, ("turn",) + LN_STEPS[LN_NTH[layer, h] - 1] + (KD - 1,))
                    tiles = [xn[t][0:ROWS[t], :] for t in range(TILES)]
                    if layer < 3:
                        for t in range(TILES):
                            normalise(tiles[t], rows[t], t).then_inc(xn_ready, 1)
                    else:
                        for t in range(TILES):
                            last = normalise(tiles[t], rows[t], t)
                        link(last)
                        for ins in quantise(tiles, q_stat, q_scale[h], TILES):
                            ins.then_inc(xn_ready, 1)
                elif kind == "norms0":
                    h = at[0]
                    b = wait_full(dve, step)
                    for t in range(TILES):
                        last = dve.tensor_scalar(
                            qk_sq[h][0:ROWS[t], t, :, :].rearrange("p a (c i) -> p c a i", i=4),
                            b[0:ROWS[t], 32 * t:32 * (t + 1)].rearrange("p (c a i) -> p c a i", a=2, i=4),
                            1e-24, None, ALU.max)
                    last.then_inc(bank_read(step), 1)
                    wait_read(dve, step)
                    dve.reciprocal(qk_inv[h][:, :, :, :], qk_sq[h][:, :, :, :]).then_inc(qk_inv_ready[h], 1)
                elif kind == "v0":
                    h, t, n = at
                    r = slice(0, ROWS[t])
                    wait_read(dve, step)
                    dve.tensor_reduce(v_sq[r, 8 * n:8 * n + 8], sq_val[r, :].rearrange("p (h n) -> p h n", n=DV),
                                      AX, ALU.add).then_inc(v_summed, 1)
                    if n == 1:
                        dve.wait_ge(v_summed, 2 * (TILES * h + t + 1))
                        link(dve.tensor_scalar(v_scale[r, :], v_sq[r, :], 1e-24, None, ALU.max))
                        reciprocal_root(v_scale[r, :], ROWS[t])
                        dve.wait_ge(qk_inv_ready[h], 1)
                        link(dve.tensor_tensor(v_scale[r, :], root[r, :], qk_inv[h][r, t, 1, :], ALU.mult))
                        dve.wait_ge(v_copied, 2 * (TILES * h + t + 1))
                        v = val[h][r, t, :, 0:DV]
                        dve.tensor_tensor(v, v, spread(v_scale[r, :], DV), ALU.mult).then_inc(v_ready[h], 1)
                elif kind == "gate0":
                    h, m = at
                    dve.wait_ge(tanh1_ready, KI * h + m + 1)
                    b = wait_full(dve, step)
                    dve.scalar_tensor_tensor(out=half_tanh[m % 2][:, :], in0=half_tanh[m % 2][:, :], scalar=1.0,
                                             in1=b[:, 0:TOKENS], op0=ALU.add, op1=ALU.mult
                                             ).then_inc(bank_read(step), 1)
                elif kind == "score0":
                    h, t, p = at
                    n = 6 * h + 2 * t + p
                    if n >= 2:
                        dve.wait_ge(prob_ready, n - 1)
                    if n == 0:
                        loaded(dve, "same_image")
                    mask = same_image[0:ROWS[t], 0:ROWS[t]].unsqueeze(1).to_broadcast([ROWS[t], 4, ROWS[t]])
                    for j in range(2):
                        key = step + (j,)
                        b = wait_full(dve, key)
                        dve.scalar_tensor_tensor(out=raw[n % 2][0:ROWS[t], j, :, 0:ROWS[t]],
                                                 in0=b[0:ROWS[t], 0:4 * ROWS[t]].rearrange("p (c n) -> p c n", c=4),
                                                 scalar=0.0, in1=mask, op0=ALU.max, op1=ALU.mult
                                                 ).then_inc(bank_read(key), 1)
                elif kind == "mix0":
                    h, t, p = at
                    n = TILES * h + t
                    r = slice(0, ROWS[t])
                    wait_read(dve, step)
                    dve.tensor_reduce(o_sq[r, :].rearrange("p (c i) -> p c i", c=4)[:, :, 2 * p:2 * p + 2],
                                      sq_mix[r, :].rearrange("p (c i n) -> p c i n", c=4, i=2), AX, ALU.add
                                      ).then_inc(mix_summed, 1)
                    if p == 1:
                        dve.wait_ge(mix_summed, 2 * (n + 1))
                        inv_q = qk_inv[h][r, t, 0, :]
                        link(dve.tensor_scalar(o_sq[r, :], o_sq[r, :], 1.2e-38, None, ALU.max))
                        reciprocal_root(o_sq[r, :], ROWS[t])
                        link(dve.tensor_tensor(o_norm[r, :], o_sq[r, :], root[r, :], ALU.mult))
                        dve.tensor_tensor(o_norm[r, :], o_norm[r, :], inv_q, ALU.mult).then_inc(norm_ready, 1)
                        dve.wait_ge(norm_ready, n + 1)
                        link(dve.tensor_scalar(o_inv[r, :], o_norm[r, :], 1e-12, None, ALU.max))
                        link(dve.reciprocal(o_inv[r, :], o_inv[r, :]))
                        link(dve.tensor_tensor(o_fac[r, :], o_inv[r, :], inv_q, ALU.mult))
                        dve.wait_ge(norm_tanh, n + 1)
                        link(dve.tensor_tensor(o_fac[r, :], o_fac[r, :], o_tanh[r, :], ALU.mult))
                        view = mix[n % 2][r, :].rearrange("p (h n) -> p h n", n=DV)
                        dve.wait_ge(mix_copied, 2 * (n + 1))
                        dve.tensor_tensor(view, view, spread(o_fac[r, :], DV), ALU.mult).then_inc(mix_ready, 1)
                elif kind == "turn0":
                    h, t = at
                    if t == 0:
                        dve.wait_ge(gate_ready[h], KI)
                    for u in range(2):
                        key = step + (u,)
                        b = wait_full(dve, key)
                        to = qk[h][:, KI + 4 * u:KI + 4 * u + 4, START[t]:START[t] + ROWS[t]]
                        dve.tensor_tensor(to, b[:, 0:4 * ROWS[t]].rearrange("p (c n) -> p c n", c=4), to, ALU.mult
                                          ).then_inc(bank_read(key), 1)
                elif kind == "add":
                    layer, h, t = at
                    b = wait_full(dve, step)
                    rows = h_tok[h][0:ROWS[t], t, :]
                    dve.tensor_tensor(rows, b[0:ROWS[t], 0:DIM], rows, ALU.add).then_inc(bank_read(step), 1)
                elif kind == "router":
                    route(at[0])
                elif kind == "qk1":
                    h, c = at
                    if c < KI:
                        b = wait_full(dve, step)
                        dve.tensor_copy(qk[h][:, c, :], b[:, 0:TOKENS]).then_inc(bank_read(step), 1)
                elif kind == "v1":
                    h, t, n = at
                    if n == 1:
                        b = wait_full(dve, step)
                        dve.tensor_copy(val[h][0:ROWS[t], t, 8 * n:8 * n + 8, 0:DV],
                                        b[0:ROWS[t], :].rearrange("p (h n) -> p h n", n=DV)
                                        ).then_inc(bank_read(step), 1)
                elif kind == "score1":
                    h, t, u = at
                    n = 12 + 6 * h + 2 * t + u
                    r = slice(0, ROWS[t])
                    if n < 14:
                        dve.wait_ge(prob_ready, n - 1)
                    else:
                        wait_full(dve, PROB_KEYS[n - 14])
                    for j in range(2):
                        key = step + (j,)
                        b = wait_full(dve, key)[r, 0:4 * ROWS[t]].rearrange("p (c n) -> p c n", c=4)
                        link(dve.tensor_reduce(row_max[j][r, :], b, AX, ALU.max))
                        dve.tensor_tensor(raw[n % 2][r, j, :, 0:ROWS[t]], b, spread(row_max[j][r, :], ROWS[t]),
                                          ALU.subtract).then_inc(bank_read(key), 1)
                elif kind == "mix1":
                    h, t, u = at
                    n = 6 + 3 * h + t
                    r = slice(0, ROWS[t])
                    if n >= 2 and u == 0:
                        wait_full(dve, TURN_KEYS[n - 2])
                    to = mix[n % 2][r, :].rearrange("p (c n) -> p c n", c=KI)
                    for j in range(2):
                        key = step + (j,)
                        b = wait_full(dve, key)[r, 0:4 * (DV + 1)].rearrange("p (c n) -> p c n", n=DV + 1)
                        link(dve.reciprocal(row_inv[j][r, :], b[:, :, DV]))
                        dve.tensor_tensor(to[:, 4 * u:4 * u + 4, j * DV:(j + 1) * DV], b[:, :, 0:DV],
                                          spread(row_inv[j][r, :], DV), ALU.mult).then_inc(bank_read(key), 1)
                elif kind == "quant_w":
                    loaded(dve, "ident", "masked", "w_last")
                    dve.tensor_copy(ident_b[:, :], ident[:, :])
                    dve.tensor_copy(masked_b[:, :], masked[:, :]).then_inc(masks_ready, 1)
                    tiles = [w_last[:, k, :] for k in range(KD)]
                    for ins in quantise(tiles, wq_stat, wq_scale, KD):
                        last = ins
                    last.then_inc(wq_ready, 1)
                elif kind == "last":
                    h, t = at
                    r = slice(0, ROWS[t])
                    if t == 0:
                        wait_read(dve, ("quant_w", 1))
                    if h == 1:
                        dve.wait_ge(stored[t], 16)
                    b = wait_full(dve, step)
                    dve.scalar_tensor_tensor(out=result[t][r, :], in0=b[r, 0:DIM], scalar=q_scale[h][r, t:t + 1],
                                             in1=last_scale[r, :], op0=ALU.mult, op1=ALU.mult
                                             ).then_inc(bank_read(step), 1)

        @block.gpsimd
        def _(pool):
            chained = [0]
            stat_n = [0]

            def link(ins):
                chained[0] += 1
                ins.then_inc(pool_chain, 1)
                pool.wait_ge(pool_chain, chained[0])

            def reciprocal_std():
                stat_n[0] += 1
                pool.wait_ge(stat_ready, stat_n[0])
                link(pool.tensor_scalar(var_eps[:, :], mean_var[:, :, 1], 1e-5, None, ALU.add))
                pool.tensor_tensor(rstd[:, :], var_eps[:, :], power[0:MAX_ROWS, :], ALU.pow
                                   ).then_inc(rstd_ready, 1)

            for step in ORDER:
                kind, at = step[0], step[1:]
                if kind == "consts":
                    for h in range(HALVES):
                        pool.memset(patch_t[h].rearrange("p k (s n) -> p k s n", n=SEQ)[:, :, :, 0:1], 0.0)
                    pool.memset(power[:, :], -0.5).then_inc(zeroed, 1)
                    pool.wait_ge(zeroed, 1)
                elif kind == "patch_ln":
                    reciprocal_std()
                elif kind == "ln":
                    layer, h = at
                    reciprocal_std()
                    if layer == 0:
                        if h == 0:
                            loaded(pool, "embed_g", "embed_add", "embed_b")
                            link(pool.tensor_tensor(embed_add[:, :], embed_add[:, :], embed_b[:, :], ALU.add))
                        for t in range(TILES):
                            rows = h_tok[h][0:ROWS[t], t, :]
                            pool.wait_ge(z_normed[h], t + 1)
                            link(pool.tensor_tensor(rows, rows, embed_g[0:ROWS[t], :], ALU.mult))
                            pool.tensor_tensor(rows, rows, embed_add[0:ROWS[t], :], ALU.add
                                               ).then_inc(h_embedded[h], 1)
                        reciprocal_std()
                    if layer == 3:
                        pool.wait_ge(xn_ready, TILES * (LN_NTH[layer, h] + 1))
                        loaded(pool, "last_b")
                        for t in range(TILES):
                            rows = h_tok[h][0:ROWS[t], t, :]
                            last = pool.tensor_tensor(rows, rows, last_b[0:ROWS[t], :], ALU.add)
                        last.then_inc(h_biased[h], 1)
                elif kind == "qk0":
                    h, c = at
                    if c >= 4:
                        continue
                    n = 4 * h + c
                    wait_read(pool, step)
                    before = n - 2
                    if before >= 0 and before % 4 == 3:
                        wait_full(pool, ("norms0", before // 4))
                    elif before >= 0:
                        pool.wait_ge(summed, before + 1 - before // 4)
                    pool.tensor_tensor(square[n % 2][:, :], qk[h][:, c, :], qk[h][:, c, :], ALU.mult
                                       ).then_inc(squared, 1)
                elif kind == "up":
                    h, e = at
                    if e >= SHARED:
                        n = EXPERTS * h + e
                        i = ROUTED * h + e - SHARED
                        a = act_t[n % ACT_RING]
                        wait_read(pool, step)
                        pool.wait_ge(gate_loaded[i % GATE_RING], 16 * (i // GATE_RING + 1))
                        pool.tensor_tensor(a[:, :], a[:, :], gate_bc[i % GATE_RING][:, :], ALU.mult
                                           ).then_inc(gated, 1)
                elif kind == "last":
                    h, t = at
                    r = slice(0, ROWS[t])
                    pool.wait_ge(h_biased[h], 1)
                    wait_read(pool, step)
                    pool.tensor_tensor(result[t][r, :], result[t][r, :], h_tok[h][r, t, :], ALU.add
                                       ).then_inc(result_ready, 1)


def _layouts(x):
    f = lambda name: np.ascontiguousarray(x[name])
    split = lambda a: np.ascontiguousarray(a.reshape(-1, 128).T)
    images = max(TILE_IMAGES)
    side = 6
    img = f("x").reshape(BATCH, 3, side, 16, side, 16).transpose(0, 2, 4, 3, 5, 1)
    rows = lambda a: np.ascontiguousarray(np.broadcast_to(a.reshape(1, DIM), (MAX_ROWS, DIM)))
    shift = np.concatenate([f("L0_tok_cls_token").reshape(1, DIM),
                            np.broadcast_to(f("L0_tok_ln2_b").reshape(1, DIM), (PATCHES, DIM))])
    token = np.arange(MAX_ROWS)
    same = (token[:, None] // SEQ) == (token[None, :] // SEQ)
    seen = same & (token[None, :] <= token[:, None])
    feature = np.arange(128)
    of_head = 4 * (feature % 32 // DK) + feature // 32
    qg, kv = (f(name).reshape(DIM, HEADS, DK + DV) for name in ("L0_attn_Wqg", "L0_attn_Wkv"))
    up = np.concatenate([f("L0_ffn_shared_up"), f("L0_ffn_routed_up")])
    down = np.concatenate([f("L0_ffn_shared_down"), f("L0_ffn_routed_down")])
    return {
        "patches": np.ascontiguousarray(img.reshape(HALVES, IMAGES * PATCHES, PATCH_DIM)),
        "patch_g": split(f("L0_tok_ln1_g")), "patch_b": split(f("L0_tok_ln1_b")),
        "w_patch": f("L0_tok_W_proj"), "row_b": f("L0_tok_b_proj").reshape(1, DIM),
        "is_patch": (np.arange(TOKENS) % SEQ != 0).astype(np.float32).reshape(1, TOKENS),
        "embed_g": rows(f("L0_tok_ln2_g")),
        "embed_b": np.ascontiguousarray(np.tile(shift, (images, 1))),
        "embed_pos": np.ascontiguousarray(np.tile(f("L0_tok_pos_emb").reshape(SEQ, DIM), (images, 1))),
        "w_qk": np.concatenate([np.stack([qg[:, :, :DK], kv[:, :, :DK]], 2).reshape(DIM, -1),
                                np.zeros((DIM, DK), np.float32)], 1),
        "w_gate": np.ascontiguousarray(qg[:, :, DK:].reshape(DIM, INNER)),
        "w_val": np.ascontiguousarray(kv[:, :, DK:].reshape(DIM, INNER)), "w_out": f("L0_attn_Wout"),
        "w_up": np.ascontiguousarray(up.transpose(2, 0, 1).reshape(KD, 128, EXPERTS, EXPERT).transpose(1, 2, 0, 3)),
        "w_down": np.ascontiguousarray(down.transpose(2, 0, 1)),
        "w_router": np.ascontiguousarray(f("L0_ffn_router_w").T.reshape(KD, 128, ROUTED).transpose(1, 0, 2)),
        "w_q1": f("L1_attn_Wq"), "w_k1": f("L1_attn_Wk"), "w_v1": f("L1_attn_Wv"), "w_out1": f("L1_attn_Wo"),
        "out_b1": split(f("L1_attn_bo")), "w_last": f("L1_ffn_weight"), "last_b": rows(f("L1_ffn_bias")),
        "ident": np.eye(128, dtype=np.float32),
        "same_image": same.astype(np.float32),
        "masked": np.where(seen, 0.0, NEG).astype(np.float32),
        "head_sum": (of_head[:, None] == np.arange(8)[None, :]).astype(np.float32),
    }


def kernel(**inputs):
    import concourse.bacc as bacc
    from concourse.bass_utils import run_bass_kernel_spmd

    arrays = _layouts({k: np.asarray(v) for k, v in inputs.items()})
    nc = bacc.Bacc("TRN2", target_bir_lowering=False, num_devices=1)
    dram = {name: nc.dram_tensor(name + "_dram", a.shape, mybir.dt.from_np(a.dtype), kind="ExternalInput").ap()
            for name, a in arrays.items()}
    out = nc.dram_tensor("out_dram", (BATCH * SEQ, DIM), F32, kind="ExternalOutput").ap()
    vit_tower(nc, dram, out)
    r = run_bass_kernel_spmd(nc, [{name + "_dram": a for name, a in arrays.items()}], core_ids=[0])
    return r.results[0]["out_dram"].reshape(BATCH, SEQ, DIM)
```

```python
from contextlib import ExitStack

import numpy as np

import concourse.bass as bass
from concourse import mybir

F32 = mybir.dt.float32
BF16 = mybir.dt.bfloat16
I32 = mybir.dt.int32
ALU = mybir.AluOpType
ACT = mybir.ActivationFunctionType
AX = mybir.AxisListType.X

BATCH, PATCHES, PATCH_DIM, DIM = 16, 36, 768, 256
SEQ = PATCHES + 1
HALVES = 2
IMAGES = BATCH // HALVES
TILE_IMAGES = (3, 3, 2)
TILES = len(TILE_IMAGES)
ROWS = tuple(n * SEQ for n in TILE_IMAGES)
PATCH_ROWS = tuple(n * PATCHES for n in TILE_IMAGES)
MAX_ROWS = max(ROWS)
START = tuple(sum(ROWS[:t]) for t in range(TILES))
PATCH_START = tuple(sum(PATCH_ROWS[:t]) for t in range(TILES))
TOKENS = sum(ROWS)
HEADS, DK, DV = 16, 16, 64
INNER = HEADS * DV
QK_COLS = 2 * HEADS * DK + DK
KD = DIM // 128
KP = PATCH_DIM // 128
KI = INNER // 128
SHARED, ROUTED, TOP_K, EXPERT = 2, 16, 4, 128
EXPERTS = SHARED + ROUTED
ACT_RING, GATE_RING = 4, 4
WARM_UP = 24
ROUND = 12582912.0
QMAX = 127.0
NEG = -3.0e38

DENSE = (0, 1)
SCORES = (2, 3)


def token_steps(h):
    steps = []
    for c in range(KP + 1):
        if c < KP:
            steps.append(("patch_t", h, c))
        if c:
            steps.append(("embed", h, c - 1))
    return [("patch_stats", h), ("patch_norm", h)] + steps + [("embed_t", h)]


def layer0_dense(h):
    steps = []
    for c in range(4):
        steps += [("qk0", h, c), ("qk0", h, 4 + c)]
        if c:
            steps += [("norm0", h, c - 1)]
    gates = []
    for m in range(KI):
        gates += [("gate0", h, m)] + [("gate_tanh", h, m - 1)] * (m > 0)
    gates.append(("gate_tanh", h, KI - 1))
    values = []
    for t in range(TILES):
        values += [("v0", h, t, 0), ("v0", h, t, 1)] + [("v_scale", h, t)]
    return steps + gates[:3] + [("norm0", h, 3), ("norms0", h)] + gates[3:7] + values + gates[7:]


def attention0(h):
    sub = [(t, p) for t in range(TILES) for p in range(2)]
    steps = []
    for i, (t, p) in enumerate(sub):
        steps += [("score0", h, t, p), ("prob0", h, t, p)]
        if i:
            steps.append(("mix0", h) + sub[i - 1])
        if i >= 2 and i % 2 == 0:
            steps += [("mix_norm", h, sub[i - 1][0]), ("mix_scale", h, sub[i - 1][0])]
        if i >= 3 and i % 2 == 1:
            steps.append(("turn0", h, sub[i - 3][0]))
    steps += [("mix0", h) + sub[-1], ("mix_norm", h, TILES - 1), ("mix_scale", h, TILES - 1)]
    return steps + [("turn0", h, TILES - 1)]


def attention1(h):
    sub = [(t, p) for t in range(TILES) for p in range(2)]
    steps = []
    for i in range(len(sub) + 3):
        if i < len(sub):
            steps += [("score1", h) + sub[i], ("exp1", h) + sub[i]]
        if 1 <= i <= len(sub):
            steps.append(("prob1", h) + sub[i - 1])
        if 2 <= i <= len(sub) + 1:
            steps.append(("mix1", h) + sub[i - 2])
        if i >= 4 and i % 2 == 0:
            steps.append(("turn1", h, sub[i - 4][0]))
    return steps


def layer_norm(layer, h):
    return [("stats", layer, h), ("norm", layer, h)]


def outward(layer, h):
    return [("out", layer, h, m) for m in range(KD)]


def residual(layer, h):
    return [("add", layer, h, t) for t in range(TILES)] + layer_norm(layer + 1, h)


def ffn(h):
    steps = [("up", h, 0), ("up", h, 1), ("router", h), ("route", h), ("up", h, 2)]
    for e in range(EXPERTS):
        if e == 0:
            steps.append(("gates", h))
        steps.append(("down", h, e))
        if e + 3 < EXPERTS:
            steps.append(("up", h, e + 3))
    return steps + [("ffn_out", h)]


def layer1_dense(h):
    qk = [("qk1", h, c) for pair in range(KI) for c in (pair, KI + pair)]
    return qk + [("v1", h, t, n) for t in range(TILES) for n in range(2)]


def last_steps(h):
    return [("turn_q", h, 0), ("turn_q", h, 1), ("last", h, 0), ("turn_q", h, 2), ("last", h, 1), ("last", h, 2)]


def half_steps(h):
    steps = token_steps(h) + [("embed_stats", h), ("embed_norm", h)] + layer_norm(0, h) + [("turn", 0, h)]
    steps += layer0_dense(h) + attention0(h) + outward(0, h) + residual(0, h)
    steps += [("turn", 1, h)] + ffn(h) + residual(1, h)
    steps += [("turn", 2, h)] + layer1_dense(h) + attention1(h) + outward(2, h) + residual(2, h) + last_steps(h)
    by_kind = {}
    for step in steps:
        by_kind.setdefault(step[0], []).append(step)
    return by_kind


SCHEDULE = """
    -: consts |  a: patch_stats patch_t patch_norm patch_t embed |  b: patch_stats |  a: patch_t embed |  b:
    patch_norm |  a: 2*patch_t 2*embed patch_t 2*embed |  b: 2*patch_t |  a: embed_t |  b: patch_t |  a:
    embed_stats |  b: 2*embed patch_t embed patch_t embed patch_t 2*embed |  a: embed_norm stats |  b: embed_t
    |  a: norm turn qk0 |  b: embed_stats |  a: 3*qk0 |  b: embed_norm |  a: qk0 gate0 norm0 2*qk0 norm0 gate0
    |  b: stats |  a: norm0 qk0 gate_tanh gate0 |  b: norm |  a: gate_tanh v0 gate0 norm0 gate_tanh v0 norms0
    v_scale 2*v0 |  b: turn |  a: gate0 gate_tanh v_scale v0 gate_tanh v0 gate0 score0 |  b: qk0 |  a: score0
    gate_tanh prob0 mix0 |  b: qk0 |  a: gate0 |  b: 2*qk0 |  a: prob0 gate0 |  b: qk0 norm0 2*qk0 |  a:
    2*gate_tanh v_scale |  b: gate0 |  a: mix0 |  b: qk0 norm0 |  a: mix_norm |  b: gate_tanh gate0 |  a:
    score0 |  b: gate_tanh 2*norm0 |  a: prob0 mix_scale |  b: norms0 2*v0 |  a: score0 |  b: gate0 |  a: mix0
    turn0 score0 |  b: gate_tanh |  a: prob0 mix0 mix_norm score0 prob0 |  b: v_scale |  a: mix_scale prob0 |
    b: v0 gate0 v0 score0 v_scale |  a: mix0 |  b: gate0 v0 |  a: mix0 |  b: gate_tanh |  a: turn0 mix_norm
    mix_scale |  b: gate_tanh 2*gate0 prob0 |  a: turn0 |  b: v0 |  a: 2*out |  -: quant_w |  a: 3*add stats |
    b: gate_tanh gate0 |  a: norm turn |  b: mix0 |  a: 2*up router up route gates |  b: prob0 |  a: down |
    b: gate_tanh v_scale |  a: up |  b: 2*score0 |  a: 2*up down |  b: gate_tanh mix0 mix_norm |  a: down up
    down |  b: mix_scale score0 prob0 |  a: up 3*down |  b: score0 prob0 |  a: up |  b: turn0 |  a: 2*up down
    |  b: mix0 prob0 |  a: down up 2*down up |  b: mix0 |  a: up |  b: mix_norm |  a: down |  b: score0
    mix_scale |  a: down 3*up |  b: mix0 prob0 turn0 mix0 mix_norm |  a: 3*down up down |  b: mix_scale |  a:
    down |  b: turn0 out |  a: ffn_out |  b: out 3*add stats |  a: 3*add |  b: norm |  a: stats |  b: turn up
    |  a: norm turn |  b: router |  a: 2*qk1 |  b: up down route |  a: 2*qk1 |  b: 2*up gates down |  a: 4*qk1
    |  b: up down 3*up down up 2*down 3*up 3*down |  a: qk1 v1 |  b: down up |  a: v1 2*qk1 |  b: down |  a:
    v1 qk1 |  b: 2*up 2*down |  a: 3*qk1 |  b: up |  a: qk1 score1 |  b: up 3*down |  a: v1 |  b: up |  a:
    score1 v1 |  b: 2*down ffn_out 3*add stats |  a: v1 exp1 |  b: norm |  a: exp1 2*prob1 |  b: turn |  a:
    score1 exp1 |  b: 6*qk1 |  a: score1 mix1 |  b: qk1 |  a: prob1 exp1 |  b: qk1 |  a: mix1 score1 prob1 |
    b: qk1 |  a: mix1 |  b: qk1 |  a: exp1 |  b: v1 |  a: mix1 |  b: qk1 |  a: score1 |  b: qk1 v1 qk1 |  a:
    prob1 |  b: qk1 v1 qk1 |  a: exp1 |  b: qk1 |  a: turn1 prob1 mix1 turn1 mix1 |  b: score1 |  a: turn1 |
    b: 2*v1 |  a: out |  b: score1 2*exp1 v1 prob1 score1 |  a: out 2*add |  b: prob1 exp1 |  a: add stats |
    b: score1 mix1 prob1 exp1 |  a: norm |  b: mix1 score1 prob1 exp1 mix1 turn1 score1 |  a: turn_q |  b:
    prob1 mix1 |  a: last turn_q |  b: mix1 exp1 prob1 turn1 mix1 |  a: turn_q last |  b: turn1 2*out |  a:
    last |  b: 3*add 2*turn_q stats norm turn_q 3*last
"""


def make_order():
    steps = [half_steps(h) for h in range(HALVES)] + [{"consts": [("consts",)], "quant_w": [("quant_w",)]}]
    order = []
    for part in SCHEDULE.split("|"):
        owner, kinds = part.split(":")
        of = steps["ab-".index(owner.strip())]
        for item in kinds.split():
            count, kind = item.split("*") if "*" in item else (1, item)
            order += [of[kind].pop(0) for _ in range(int(count))]
    assert not any(left for of in steps for left in of.values())
    return order


ORDER = make_order()
LN_STEPS = [step[1:] for step in ORDER if step[0] == "norm"]
STATS = [step for step in ORDER if step[0] in ("patch_stats", "embed_stats", "stats")]
LN_NTH = {at: n for n, at in enumerate(LN_STEPS)}
TURNED = [("turn", layer, h, KD - 1) if layer < 3 else ("turn_q", h, TILES - 1) for layer, h in LN_STEPS]
MIX_KEYS = [step + (1,) * (step[0] == "mix1") for step in ORDER if step[0] in ("mix0", "mix1")]
PROB_KEYS = [step + (1,) for step in ORDER if step[0] == "prob1"]
TURN_KEYS = [step + (1,) for step in ORDER if step[0] in ("turn0", "turn1")]


def banks_of(step):
    kind = step[0]
    if kind in ("patch_t", "qk0", "v0", "gate0", "out", "up", "qk1", "v1", "last"):
        return [(step, DENSE)]
    if kind in ("router", "gates"):
        return [(step, DENSE)]
    if kind == "quant_w":
        return [((kind, n), DENSE) for n in range(2)]
    if kind in ("turn", "turn1"):
        return [(step + (m,), DENSE) for m in range(2)]
    if kind == "add":
        return [(step, DENSE)]
    if kind in ("score0", "score1"):
        return [(step + (j,), (SCORES[j],)) for j in range(2)]
    if kind == "mix0":
        return [(step, (4,))]
    if kind == "turn0":
        return [(step + (u,), (5,)) for u in range(2)]
    if kind == "embed" and step[2] == 0:
        return [(("embedded", step[1], m), (6 + m,)) for m in range(KD)]
    if kind == "embed_t":
        return [(step + (t,), (2 + t,)) for t in range(TILES)]
    if kind == "turn_q":
        return [(step, DENSE)]
    if kind == "norm0" and step[2] == 0:
        return [(("norms0", step[1]), (6,))]
    if kind == "down" and step[2] == 0:
        return [(("ffn", step[1], m), (6 + m,)) for m in range(KD)]
    if kind == "prob1":
        return [(step + (j,), (6 + j,)) for j in range(2)]
    if kind == "mix1":
        return [(step + (j,), (4 + j,)) for j in range(2)]
    return []


def psum_plan():
    plan, used, dense = {}, [0] * 8, 0
    for step in ORDER:
        for key, ring in banks_of(step):
            bank = ring[dense % len(ring)]
            dense += ring is DENSE
            plan[key] = (bank, used[bank])
            used[bank] += 1
    return plan


PSUM = psum_plan()


def vit_tower(nc, d, out):
    with ExitStack() as ctx:
        def sb(name, shape, dt=F32):
            return ctx.enter_context(nc.sbuf_tensor(name, shape, dt))

        def sem(name):
            return ctx.enter_context(nc.semaphore(name))

        def per_half(name):
            return [sem(f"{name}_{h}") for h in range(HALVES)]

        gates_dram = nc.dram_tensor("gates_dram", [HALVES, ROUTED, TOKENS], F32).ap()

        region = sb("proj_weights", [128, KP * DIM + KD * (QK_COLS + 2 * INNER)])
        w_patch = region[:, 0:KP * DIM].rearrange("p (k n) -> p k n", k=KP)
        ends = [KP * DIM + KD * n for n in (0, QK_COLS, QK_COLS + INNER, QK_COLS + 2 * INNER)]
        w_qk, w_gate, w_val = (region[:, ends[i]:ends[i + 1]].rearrange("p (k n) -> p k n", k=KD) for i in range(3))
        w1 = [region[:, i * KD * INNER:(i + 1) * KD * INNER].rearrange("p (k n) -> p k n", k=KD) for i in range(3)]
        w_out = sb("out_weights", [128, KI, DIM])
        w_up = sb("up_weights", [128, EXPERTS, KD, EXPERT])
        w_down = sb("down_weights", [128, EXPERTS, DIM])
        w_router = sb("router_weights", [128, KD, ROUTED])
        w_last = sb("last_weights", [128, KD, DIM])
        w_last_t = sb("last_weights_t", [128, KD, DIM], BF16)
        patch_g, patch_b = sb("patch_g", [128, KP]), sb("patch_b", [128, KP])
        embed_bias = sb("embed_bias", [128, KD])
        minus_round = sb("minus_round", [128, 1])
        out_b1 = sb("out_b1", [128, KD])
        last_b = sb("last_b", [MAX_ROWS, DIM])
        last_scale = sb("last_scale", [128, DIM])
        ident, ident_b = sb("ident", [128, 128]), sb("ident_b", [128, 128], BF16)
        same_image = sb("same_image", [MAX_ROWS, MAX_ROWS])
        masked = sb("masked", [MAX_ROWS, MAX_ROWS])
        masked_b = sb("masked_b", [MAX_ROWS, MAX_ROWS], BF16)
        head_sum = sb("head_sum", [128, 8])
        power = sb("power", [128, TILES])

        h_tok = [sb(f"h{h}", [MAX_ROWS, TILES, DIM]) for h in range(HALVES)]
        xn = [sb(f"xn{t}", [MAX_ROWS, DIM]) for t in range(TILES)]
        xn_t = [sb(f"xn_t{h}", [128, KD, TOKENS]) for h in range(HALVES)]
        qk = [sb(f"qk{h}", [128, 2 * KI, TOKENS]) for h in range(HALVES)]
        flat = [q[:, :, :].rearrange("p c n -> p (c n)") for q in qk]
        patch = [[flat[h][0:PATCH_ROWS[t], t * PATCH_DIM:(t + 1) * PATCH_DIM] for t in range(TILES)]
                 for h in range(HALVES)]
        patch_t = [flat[h][:, TILES * PATCH_DIM:TILES * PATCH_DIM + KP * IMAGES * PATCHES].rearrange("p (k n) -> p k n", k=KP)
                   for h in range(HALVES)]
        val = [sb(f"val{h}", [MAX_ROWS, TILES, HEADS, DV + 1]) for h in range(HALVES)]
        square = [sb(f"square{i}", [128, TOKENS]) for i in range(2)]
        half_tanh = [sb(f"half_tanh{i}", [128, TOKENS]) for i in range(2)]
        raw = [sb(f"raw{i}", [MAX_ROWS, 2, 4, MAX_ROWS]) for i in range(2)]
        prob = [sb(f"prob{i}", [MAX_ROWS, 2, 4, MAX_ROWS]) for i in range(2)]
        mix = [sb(f"mix{i}", [MAX_ROWS, INNER]) for i in range(2)]
        sq_val, sq_mix = sb("sq_val", [MAX_ROWS, 8 * DV]), sb("sq_mix", [MAX_ROWS, 8 * DV])
        y_t = [sb(f"y_t{h}", [128, KD, TOKENS]) for h in range(HALVES)]
        act_t = [sb(f"act_t{i}", [128, TOKENS]) for i in range(ACT_RING)]
        gate_bc = [sb(f"gate_bc{i}", [128, TOKENS]) for i in range(GATE_RING)]
        embed_b = act_t[3][0:MAX_ROWS, 0:DIM]
        embed_g, embed_add = (gate_bc[i][0:MAX_ROWS, 0:DIM] for i in (2, 3))
        xq_t = [gate_bc[h][:, :].bitcast(BF16).rearrange("p (k n) -> p k n", k=KD) for h in range(HALVES)]
        gate_t = [sb(f"gate_t{h}", [ROUTED, TOKENS]) for h in range(HALVES)]
        result = [act_t[t][0:MAX_ROWS, 0:DIM] for t in range(TILES)]

        partial = sb("partial", [MAX_ROWS, TILES, 2, 6])
        mean_var = [sb(f"mean_var{h}", [MAX_ROWS, TILES, 2]) for h in range(HALVES)]
        var_eps = sb("var_eps", [MAX_ROWS, TILES])
        rstd = [sb(f"rstd{h}", [MAX_ROWS, TILES]) for h in range(HALVES)]
        qk_sq = [sb(f"qk_sq{h}", [MAX_ROWS, TILES, 2, HEADS]) for h in range(HALVES)]
        qk_inv = [sb(f"qk_inv{h}", [MAX_ROWS, TILES, 2, HEADS]) for h in range(HALVES)]
        v_sq, v_scale = sb("v_sq", [MAX_ROWS, HEADS]), sb("v_scale", [MAX_ROWS, HEADS])
        o_sq, o_norm = sb("o_sq", [MAX_ROWS, HEADS]), sb("o_norm", [MAX_ROWS, HEADS])
        root, root_t = sb("root", [MAX_ROWS, HEADS]), sb("root_t", [MAX_ROWS, HEADS])
        o_tanh, o_inv, o_fac = (sb(n, [MAX_ROWS, HEADS]) for n in ("o_tanh", "o_inv", "o_fac"))
        row_max = [sb(f"row_max{j}", [MAX_ROWS, 4]) for j in range(2)]
        row_inv = [sb(f"row_inv{j}", [MAX_ROWS, 4]) for j in range(2)]
        logits = sb("logits", [MAX_ROWS, TILES, ROUTED])
        exps = sb("exps", [MAX_ROWS, TILES, ROUTED])
        top_stat = sb("top_stat", [MAX_ROWS, 3, TILES])
        probs = sb("probs", [MAX_ROWS, TILES, ROUTED + 4])
        rest = sb("rest", [MAX_ROWS, TILES, ROUTED + 4])
        top8 = sb("top8", [MAX_ROWS, TILES, 8])
        pads = sb("pads", [MAX_ROWS, TILES, 4])
        gate = sb("gate", [MAX_ROWS, TILES, ROUTED])
        q_stat = sb("q_stat", [MAX_ROWS, 2, TILES])
        q_scale = [sb(f"q_scale{h}", [MAX_ROWS, TILES]) for h in range(HALVES)]
        wq_stat, wq_scale = sb("wq_stat", [128, 2, KD]), sb("wq_scale", [128, KD])

        bank = [ctx.enter_context(nc.psum_tensor(f"bank{i}", [128, 512], F32)) for i in range(8)]

        full = [sem(f"full{i}") for i in range(8)]
        free = [sem(f"free{i}") for i in range(8)]
        loads = {}
        warm_ready = sem("warm_ready")
        zeroed = sem("zeroed")
        dve_chain, pool_chain = sem("dve_chain"), sem("pool_chain")
        stat_ready, rstd_ready = sem("stat_ready"), sem("rstd_ready")
        patch_normed = per_half("patch_normed")
        xn_ready = sem("xn_ready")
        squared, summed = sem("squared"), sem("summed")
        qk_inv_ready = per_half("qk_inv_ready")
        v_copied, v_summed = sem("v_copied"), sem("v_summed")
        v_ready = per_half("v_ready")
        tanh1_ready = sem("tanh1_ready")
        gate_ready = per_half("gate_ready")
        exp_ready = sem("exp_ready")
        prob_ready = sem("prob_ready")
        mix_copied, mix_summed = sem("mix_copied"), sem("mix_summed")
        norm_ready, norm_tanh = sem("norm_ready"), sem("norm_tanh")
        mix_ready = sem("mix_ready")
        logit_ready, expd = sem("logit_ready"), sem("expd")
        gated_rows = sem("gated_rows")
        gate_stored = sem("gate_stored")
        gate_loaded = [sem(f"gate_loaded{i}") for i in range(GATE_RING)]
        gated, act_used = sem("gated"), sem("act_used")
        wq_ready, masks_ready = sem("wq_ready"), sem("masks_ready")
        h_biased = per_half("h_biased")
        result_ready = sem("result_ready")
        stored = [sem(f"stored{t}") for t in range(TILES)]

        def loaded(eng, *names):
            for name in names:
                eng.wait_ge(loads[name], 16)

        def wait_full(eng, key):
            b, before = PSUM[key]
            eng.wait_ge(full[b], before + 1)
            return bank[b]

        def bank_read(key):
            return free[PSUM[key][0]]

        def wait_read(eng, key):
            b, before = PSUM[key]
            eng.wait_ge(free[b], before + 1)

        def spread(ap, n):
            return ap.unsqueeze(2).to_broadcast([ap.shape[0], ap.shape[1], n])

        x_dram = d["patches"]
        first = [(f"x{h}{t}", patch[h][t], x_dram[h, PATCH_START[t]:PATCH_START[t] + PATCH_ROWS[t], :])
                 for h in range(HALVES) for t in range(TILES)]
        small = [("ident", ident[:, :], d["ident"]), ("patch_g", patch_g[:, :], d["patch_g"]),
                 ("patch_b", patch_b[:, :], d["patch_b"]), ("embed_bias", embed_bias[:, :], d["embed_bias"]),
                 ("embed_g", embed_g[:, :], d["embed_g"]),
                 ("embed_add", embed_add[:, :], d["embed_pos"]), ("embed_b", embed_b[:, :], d["embed_b"]),
                 ("same_image", same_image[:, :], d["same_image"]), ("masked", masked[:, :], d["masked"]),
                 ("head_sum", head_sum[:, :], d["head_sum"])]
        w_layer0 = [(name, w, d[name].rearrange("(k p) n -> p k n", p=128))
                    for name, w in (("w_qk", w_qk), ("w_val", w_val), ("w_gate", w_gate))]
        w_experts = []
        for i in range(0, EXPERTS, 6):
            w_experts += [(f"w_up{i}", w_up[:, i:i + 6, :, :], d["w_up"][:, i:i + 6, :, :]),
                          (f"w_down{i}", w_down[:, i:i + 6, :], d["w_down"][:, i:i + 6, :])]
        plan_sync = first[:TILES] + [("w_patch", w_patch, d["w_patch"].rearrange("(k p) n -> p k n", p=128))] \
            + first[TILES:] + w_layer0 + [("w_out", w_out[:, :, :], d["w_out"].rearrange("(k p) n -> p k n", p=128))] \
            + w_experts
        late = [("w_router", w_router[:, :, :], d["w_router"]),
                ("w_last", w_last[:, :, :], d["w_last"].rearrange("(k p) n -> p k n", p=128)),
                ("out_b1", out_b1[:, :], d["out_b1"]), ("last_b", last_b[:, :], d["last_b"])]
        w_layer1 = [(f"w1{i}", w1[i], d[name].rearrange("(k p) n -> p k n", p=128))
                    for i, name in enumerate(("w_q1", "w_k1", "w_v1"))]
        w_layer1_out = ("w_out1", w_out[:, :, :], d["w_out1"].rearrange("(k p) n -> p k n", p=128))
        for name, _, _ in plan_sync + small + late + w_layer1 + [w_layer1_out]:
            loads[name] = sem(f"load_{name}")

        block = ctx.enter_context(nc.Block())

        @block.sync
        def _(sp):
            for name, to, src in plan_sync:
                sp.dma_start(to, src).then_inc(loads[name], 16)
            for name, to, src in late:
                sp.dma_start(to, src).then_inc(loads[name], 16)
            for step in ORDER:
                if step[0] == "gates":
                    h = step[1]
                    wait_read(sp, ("gates", h))
                    sp.dma_start(gates_dram[h], gate_t[h][:, :]).then_inc(gate_stored, 16)
                    if h == 0:
                        wait_full(sp, ("gate0", HALVES - 1, KI - 1))
                        for name, to, src in w_layer1:
                            sp.dma_start(to, src).then_inc(loads[name], 16)
                    sp.wait_ge(gate_stored, 16 * (h + 1))
                    for r in range(ROUTED):
                        n = ROUTED * h + r
                        if n >= GATE_RING:
                            sp.wait_ge(gated, n - GATE_RING + 1)
                        sp.dma_start(gate_bc[n % GATE_RING][:, :],
                                     gates_dram[h, r:r + 1, :].to_broadcast([128, TOKENS])
                                     ).then_inc(gate_loaded[n % GATE_RING], 16)
                    if h == 0:
                        for half in range(HALVES):
                            wait_full(sp, ("out", 0, half, KD - 1))
                        name, to, src = w_layer1_out
                        sp.dma_start(to, src).then_inc(loads[name], 16)
                if step[0] == "last":
                    _, h, t = step
                    sp.wait_ge(result_ready, TILES * h + t + 1)
                    r0 = h * TOKENS + START[t]
                    sp.dma_start(out[r0:r0 + ROWS[t], :], result[t][0:ROWS[t], :]).then_inc(stored[t], 16)
            for t in range(TILES):
                sp.wait_ge(stored[t], 16 * HALVES)

        @block.tensor
        def _(pe):
            def claim(key):
                b, before = PSUM[key]
                if before:
                    pe.wait_ge(free[b], before)
                return bank[b]

            def filled(key, last):
                last.then_inc(full[PSUM[key][0]], 1)

            def warm_up():
                pe.wait_ge(warm_ready, 1)
                for _ in range(WARM_UP):
                    pe.matmul(bank[0][:, :], w_last_t[:, 0, 0:128], w_last_t[:, :, :].rearrange("p k n -> p (k n)"),
                              start=True, stop=True)

            def patch_turn(h, c):
                key = ("patch_t", h, c)
                if c == 0:
                    loaded(pe, "ident")
                    pe.wait_ge(patch_normed[h], TILES)
                b = claim(key)
                for t in range(TILES):
                    last = pe.transpose(b[:, PATCH_START[t]:PATCH_START[t] + PATCH_ROWS[t]],
                                        patch[h][t][:, c * 128:(c + 1) * 128],
                                        ident[0:PATCH_ROWS[t], 0:PATCH_ROWS[t]])
                filled(key, last)

            def embed(h, k):
                if k == 0:
                    loaded(pe, "w_patch")
                wait_read(pe, ("patch_t", h, k))
                for m in range(KD):
                    key = ("embedded", h, m)
                    b = claim(key) if k == 0 else bank[PSUM[key][0]]
                    last = pe.matmul(b[:, 0:IMAGES * PATCHES], w_patch[:, k, m * 128:(m + 1) * 128],
                                     patch_t[h][:, k, :], start=(k == 0), stop=(k == KP - 1))
                    if k == KP - 1:
                        filled(key, last)

            def embed_turn(h):
                wait_read(pe, ("embedded", h, KD - 1))
                for t in range(TILES):
                    key = ("embed_t", h, t)
                    b = claim(key)
                    for m in range(KD):
                        last = pe.transpose(b[0:ROWS[t], m * 128:(m + 1) * 128],
                                            y_t[h][:, m, START[t]:START[t] + ROWS[t]], ident[:, :])
                    filled(key, last)

            def turn(layer, h):
                for m in range(KD):
                    key = ("turn", layer, h, m)
                    b = claim(key)
                    for t in range(TILES):
                        if m == 0:
                            pe.wait_ge(xn_ready, TILES * LN_NTH[layer, h] + t + 1)
                        last = pe.transpose(b[:, START[t]:START[t] + ROWS[t]],
                                            xn[t][0:ROWS[t], m * 128:(m + 1) * 128], ident[0:ROWS[t], 0:ROWS[t]])
                    filled(key, last)

            def turn_quantised(h, t):
                key = ("turn_q", h, t)
                pe.wait_ge(xn_ready, TILES * LN_NTH[3, h] + t + 1)
                b = claim(key)
                for m in range(KD):
                    last = pe.transpose(b[:, m * ROWS[t]:(m + 1) * ROWS[t]],
                                        xn[t][0:ROWS[t], m * 128:(m + 1) * 128], ident[0:ROWS[t], 0:ROWS[t]])
                filled(key, last)

            def dense(key, h, weights, b=None):
                b = claim(key) if b is None else b
                for k in range(KD):
                    last = pe.matmul(b[:, 0:TOKENS], weights(k), xn_t[h][:, k, :],
                                     start=(k == 0), stop=(k == KD - 1))
                filled(key, last)

            def token_product(key, h, t, weights, cols):
                b = claim(key)[0:ROWS[t], 0:cols]
                for k in range(KD):
                    last = pe.matmul(b, xn_t[h][:, k, START[t]:START[t] + ROWS[t]], weights(k),
                                     start=(k == 0), stop=(k == KD - 1))
                filled(key, last)

            def qk0(h, c):
                if c == 0:
                    loaded(pe, "w_qk")
                    wait_read(pe, ("turn", 0, h, KD - 1))
                col = 128 * (c % 4) + DK * (c // 4)
                dense(("qk0", h, c), h, lambda k: w_qk[:, k, col:col + 128])

            def norm0(h, c):
                key = ("norms0", h)
                if c == 0:
                    loaded(pe, "head_sum")
                    claim(key)
                n = 4 * h + c
                pe.wait_ge(squared, n + 1)
                b = bank[PSUM[key][0]]
                for t in range(TILES):
                    col = 32 * t + 8 * c
                    last = pe.matmul(b[0:ROWS[t], col:col + 8], square[n % 2][:, START[t]:START[t] + ROWS[t]],
                                     head_sum[:, :], start=True, stop=True)
                if c < 3:
                    last.then_inc(summed, 1)
                else:
                    filled(key, last)

            def score0(h, t, p):
                if (t, p) == (0, 0):
                    wait_read(pe, ("qk0", h, 7))
                cols = slice(START[t], START[t] + ROWS[t])
                banks = [claim(("score0", h, t, p, j)) for j in range(2)]
                last = [None, None]
                for c in range(4):
                    for j in range(2):
                        at = slice(32 * (2 * p + j), 32 * (2 * p + j) + DK)
                        last[j] = pe.matmul(banks[j][0:ROWS[t], c * ROWS[t]:(c + 1) * ROWS[t]],
                                            qk[h][at, 4 + c, cols], qk[h][at, c, cols], start=True, stop=True,
                                            tile_position=(32 * (2 * p + j), 0))
                for j in range(2):
                    filled(("score0", h, t, p, j), last[j])

            def mix0(h, t, p):
                n = 6 * h + 2 * t + p
                key = ("mix0", h, t, p)
                pe.wait_ge(prob_ready, n + 1)
                pe.wait_ge(v_ready[h], t + 1)
                b = claim(key)
                for c in range(4):
                    for j in range(2):
                        last = pe.matmul(b[0:ROWS[t], (2 * c + j) * DV:(2 * c + j + 1) * DV],
                                         prob[n % 2][0:ROWS[t], j, c, 0:ROWS[t]],
                                         val[h][0:ROWS[t], t, 4 * c + 2 * p + j, 0:DV], start=True, stop=True)
                filled(key, last)

            def turn0(h, t):
                n = 3 * h + t
                pe.wait_ge(mix_ready, n + 1)
                for u in range(2):
                    key = ("turn0", h, t, u)
                    b = claim(key)
                    for q in range(4):
                        c = 4 * u + q
                        last = pe.transpose(b[:, q * ROWS[t]:(q + 1) * ROWS[t]],
                                            mix[n % 2][0:ROWS[t], c * 128:(c + 1) * 128],
                                            ident[0:ROWS[t], 0:ROWS[t]])
                    filled(key, last)

            def out_product(layer, h, m):
                key = ("out", layer, h, m)
                if m == 0:
                    loaded(pe, "w_out" if layer == 0 else "w_out1")
                    wait_read(pe, ("turn0" if layer == 0 else "turn1", h, TILES - 1, 1))
                src = qk[h][:, KI:2 * KI, :] if layer == 0 else qk[h][:, 0:KI, :]
                b = claim(key)
                for k in range(KI):
                    last = pe.matmul(b[:, 0:TOKENS], w_out[:, k, m * 128:(m + 1) * 128], src[:, k, :],
                                     start=(k == 0), stop=(k == KI - 1))
                filled(key, last)

            def add(layer, h, t):
                key = ("add", layer, h, t)
                if t == 0:
                    wait_read(pe, ("ffn", h, KD - 1) if layer == 1 else ("out", layer, h, KD - 1))
                b = claim(key)
                for m in range(KD):
                    last = pe.transpose(b[0:ROWS[t], m * 128:(m + 1) * 128],
                                        y_t[h][:, m, START[t]:START[t] + ROWS[t]], ident[:, :])
                filled(key, last)

            def router(h):
                key = ("router", h)
                if h == 0:
                    loaded(pe, "w_router")
                b = claim(key)
                for t in range(TILES):
                    for k in range(KD):
                        last = pe.matmul(b[0:ROWS[t], ROUTED * t:ROUTED * (t + 1)],
                                         xn_t[h][:, k, START[t]:START[t] + ROWS[t]], w_router[:, k, :],
                                         start=(k == 0), stop=(k == KD - 1))
                filled(key, last)

            def gates(h):
                key = ("gates", h)
                pe.wait_ge(gated_rows, h + 1)
                b = claim(key)
                for t in range(TILES):
                    last = pe.transpose(b[0:ROUTED, START[t]:START[t] + ROWS[t]], gate[0:ROWS[t], t, :],
                                        ident[0:ROWS[t], 0:ROWS[t]])
                filled(key, last)

            def up(h, e):
                if e == 0:
                    wait_read(pe, ("turn", 1, h, KD - 1))
                if h == 0 and e % 6 == 0:
                    loaded(pe, f"w_up{e}")
                dense(("up", h, e), h, lambda k: w_up[:, e, k, :])

            def down(h, e):
                n = EXPERTS * h + e
                if h == 0 and e % 6 == 0:
                    loaded(pe, f"w_down{e}")
                if e < SHARED:
                    wait_read(pe, ("up", h, e))
                else:
                    pe.wait_ge(gated, ROUTED * h + e - SHARED + 1)
                for m in range(KD):
                    key = ("ffn", h, m)
                    b = claim(key) if e == 0 else bank[PSUM[key][0]]
                    last = pe.matmul(b[:, 0:TOKENS], w_down[:, e, m * 128:(m + 1) * 128],
                                     act_t[n % ACT_RING][:, :], start=(e == 0), stop=(e == EXPERTS - 1))
                    if e == EXPERTS - 1:
                        filled(key, last)
                if e < EXPERTS - 1:
                    last.then_inc(act_used, 1)

            def qk1(h, c):
                if c == 0:
                    wait_read(pe, ("turn", 2, h, KD - 1))
                    loaded(pe, "w10", "w11")
                w, m = (w1[0], c) if c < KI else (w1[1], c - KI)
                dense(("qk1", h, c), h, lambda k: w[:, k, m * 128:(m + 1) * 128])

            def score1(h, t, u):
                if (t, u) == (0, 0):
                    pe.wait_ge(masks_ready, 1)
                    wait_read(pe, ("qk1", h, KI - 1))
                    wait_read(pe, ("qk1", h, 2 * KI - 1))
                cols = slice(START[t], START[t] + ROWS[t])
                banks = [claim(("score1", h, t, u, j)) for j in range(2)]
                for j in range(2):
                    pe.matmul(banks[j][0:ROWS[t], 0:4 * ROWS[t]], ident_b[0:ROWS[t], 0:ROWS[t]],
                              masked_b[0:ROWS[t], 0:ROWS[t]].unsqueeze(1).to_broadcast([ROWS[t], 4, ROWS[t]]),
                              start=True, stop=False, skip_group_check=True)
                last = [None, None]
                for q in range(4):
                    for j in range(2):
                        at = slice(64 * j, 64 * j + 64)
                        last[j] = pe.matmul(banks[j][0:ROWS[t], q * ROWS[t]:(q + 1) * ROWS[t]],
                                            qk[h][at, 4 * u + q, cols], qk[h][at, KI + 4 * u + q, cols],
                                            start=False, stop=True, skip_group_check=True,
                                            tile_position=(64 * j, 0))
                for j in range(2):
                    filled(("score1", h, t, u, j), last[j])

            def prob1(h, t, u):
                n = 12 + 6 * h + 2 * t + u
                pe.wait_ge(exp_ready, n - 12 + 1)
                for j in range(2):
                    key = ("prob1", h, t, u, j)
                    b = claim(key)
                    for q in range(4):
                        last = pe.transpose(b[0:ROWS[t], q * ROWS[t]:(q + 1) * ROWS[t]],
                                            raw[n % 2][0:ROWS[t], j, q, 0:ROWS[t]], ident[0:ROWS[t], 0:ROWS[t]])
                    filled(key, last)

            def mix1(h, t, u):
                n = 12 + 6 * h + 2 * t + u
                wait_read(pe, ("prob1", h, t, u, 1))
                wait_read(pe, ("v1", h, t, 0))
                wait_read(pe, ("v1", h, t, 1))
                for j in range(2):
                    key = ("mix1", h, t, u, j)
                    b = claim(key)
                    for q in range(4):
                        last = pe.matmul(b[0:ROWS[t], q * (DV + 1):(q + 1) * (DV + 1)],
                                         prob[n % 2][0:ROWS[t], j, q, 0:ROWS[t]],
                                         val[h][0:ROWS[t], t, 2 * (4 * u + q) + j, :], start=True, stop=True)
                    filled(key, last)

            def turn1(h, t):
                n = 6 + 3 * h + t
                wait_read(pe, ("mix1", h, t, 1, 1))
                for u in range(2):
                    key = ("turn1", h, t, u)
                    b = claim(key)
                    for q in range(4):
                        c = 4 * u + q
                        last = pe.transpose(b[:, q * ROWS[t]:(q + 1) * ROWS[t]],
                                            mix[n % 2][0:ROWS[t], c * 128:(c + 1) * 128],
                                            ident[0:ROWS[t], 0:ROWS[t]])
                    filled(key, last)

            def quant_w():
                pe.wait_ge(wq_ready, 1)
                b = claim(("quant_w", 0))
                for k in range(KD):
                    for m in range(KD):
                        last = pe.transpose(b[:, k * DIM + m * 128:k * DIM + (m + 1) * 128],
                                            w_last[:, m, k * 128:(k + 1) * 128], ident[:, :])
                filled(("quant_w", 0), last)
                b = claim(("quant_w", 1))
                for m in range(KD):
                    last = pe.matmul(b[:, m * 128:(m + 1) * 128], wq_scale[:, m:m + 1].to_broadcast([128, 128]),
                                     ident[:, :], start=True, stop=True)
                filled(("quant_w", 1), last)

            def last_product(h, t):
                wait_read(pe, ("turn_q", h, t))
                if (h, t) == (0, 0):
                    wait_read(pe, ("quant_w", 0))
                key = ("last", h, t)
                b = claim(key)[0:ROWS[t], 0:DIM]
                for k in range(KD):
                    last = pe.matmul(b, xq_t[h][:, k, START[t]:START[t] + ROWS[t]], w_last_t[:, k, :],
                                     start=(k == 0), stop=(k == KD - 1))
                filled(key, last)

            for step in ORDER:
                kind, at = step[0], step[1:]
                if kind == "consts":
                    warm_up()
                elif kind == "patch_t":
                    patch_turn(*at)
                elif kind == "embed":
                    embed(*at)
                elif kind == "embed_t":
                    embed_turn(*at)
                elif kind == "turn_q":
                    turn_quantised(*at)
                elif kind == "turn":
                    turn(*at)
                elif kind == "qk0":
                    qk0(*at)
                elif kind == "norm0":
                    norm0(*at)
                elif kind == "v0":
                    h, t, n = at
                    if (t, n) == (0, 0):
                        loaded(pe, "w_val")
                    token_product(step, h, t, lambda k: w_val[:, k, 512 * n:512 * (n + 1)], 8 * DV)
                elif kind == "gate0":
                    h, m = at
                    if m == 0:
                        loaded(pe, "w_gate")
                    dense(step, h, lambda k: w_gate[:, k, m * 128:(m + 1) * 128])
                elif kind == "score0":
                    score0(*at)
                elif kind == "mix0":
                    mix0(*at)
                elif kind == "turn0":
                    turn0(*at)
                elif kind == "out":
                    out_product(*at)
                elif kind == "add":
                    add(*at)
                elif kind == "router":
                    router(*at)
                elif kind == "gates":
                    gates(*at)
                elif kind == "up":
                    up(*at)
                elif kind == "down":
                    down(*at)
                elif kind == "qk1":
                    qk1(*at)
                elif kind == "v1":
                    h, t, n = at
                    if (t, n) == (0, 0):
                        loaded(pe, "w12")
                    token_product(step, h, t, lambda k: w1[2][:, k, 512 * n:512 * (n + 1)], 8 * DV)
                elif kind == "score1":
                    score1(*at)
                elif kind == "prob1":
                    prob1(*at)
                elif kind == "mix1":
                    mix1(*at)
                elif kind == "turn1":
                    turn1(*at)
                elif kind == "quant_w":
                    quant_w()
                elif kind == "last":
                    last_product(*at)

        @block.scalar
        def _(act):
            for name, to, src in small:
                act.dma_start(to, src).then_inc(loads[name], 16)
            act.preload_act_table(ACT.Gelu)

            def copy_out(key, to, cols, rows=128, func=ACT.Copy, **kw):
                b = wait_full(act, key)
                return act.activation(to, b[0:rows, 0:cols], func, **kw).then_inc(bank_read(key), 1)

            for step in ORDER:
                kind, at = step[0], step[1:]
                if kind == "patch_t":
                    h, c = at
                    if c == 0:
                        loaded(act, "patch_g", "patch_b")
                    copy_out(step, patch_t[h][:, c, :], IMAGES * PATCHES, func=ACT.Identity,
                             scale=patch_g[:, c:c + 1], bias=patch_b[:, c:c + 1])
                elif kind == "embed_t":
                    h = at[0]
                    if h == 0:
                        act.wait_ge(zeroed, 1)
                        loaded(act, "embed_bias")
                    for m in range(KD):
                        key = ("embedded", h, m)
                        b = wait_full(act, key)
                        act.activation(y_t[h][:, m, :].rearrange("p (s n) -> p s n", n=SEQ)[:, :, 1:SEQ],
                                       b[:, 0:IMAGES * PATCHES].rearrange("p (s n) -> p s n", n=PATCHES),
                                       ACT.Identity, bias=embed_bias[:, m:m + 1]).then_inc(bank_read(key), 1)
                elif kind == "turn":
                    layer, h = at
                    for m in range(KD):
                        copy_out(step + (m,), xn_t[h][:, m, :], TOKENS)
                elif kind == "turn_q":
                    h, t = at
                    b = wait_full(act, step)
                    act.activation(xq_t[h][:, :, START[t]:START[t] + ROWS[t]],
                                   b[:, 0:KD * ROWS[t]].rearrange("p (k n) -> p k n", k=KD),
                                   ACT.Identity, bias=minus_round[:, :]).then_inc(bank_read(step), 1)
                elif kind == "qk0":
                    h, c = at
                    copy_out(step, qk[h][:, c, :], TOKENS)
                elif kind in ("v0", "v1"):
                    h, t, n = at
                    if kind == "v0" or n == 0:
                        b = wait_full(act, step)
                        last = act.activation(val[h][0:ROWS[t], t, 8 * n:8 * n + 8, 0:DV],
                                              b[0:ROWS[t], :].rearrange("p (h n) -> p h n", n=DV), ACT.Copy)
                        if kind == "v0":
                            last.then_inc(v_copied, 1)
                            i = 2 * (TILES * h + t) + n
                            if i:
                                act.wait_ge(v_summed, i)
                            last = act.activation(sq_val[0:ROWS[t], :], b[0:ROWS[t], :], ACT.Square)
                        last.then_inc(bank_read(step), 1)
                elif kind == "gate0":
                    h, m = at
                    b = wait_full(act, step)
                    if m >= 2:
                        act.wait_ge(gate_ready[h], m - 1)
                    elif h:
                        act.wait_ge(gate_ready[h - 1], KI)
                    act.activation(half_tanh[m % 2][:, :], b[:, 0:TOKENS], ACT.Tanh, scale=0.5
                                   ).then_inc(tanh1_ready, 1)
                elif kind == "gate_tanh":
                    h, m = at
                    wait_read(act, ("gate0", h, m))
                    act.activation(qk[h][:, KI + m, :], half_tanh[m % 2][:, :], ACT.Tanh, scale=0.5
                                   ).then_inc(gate_ready[h], 1)
                elif kind == "prob0":
                    h, t, p = at
                    n = 6 * h + 2 * t + p
                    wait_read(act, ("score0", h, t, p, 1))
                    if n >= 2:
                        wait_full(act, MIX_KEYS[n - 2])
                    act.activation(prob[n % 2][0:ROWS[t], :, :, 0:ROWS[t]].rearrange("p j c n -> p (j c) n"),
                                   raw[n % 2][0:ROWS[t], :, :, 0:ROWS[t]].rearrange("p j c n -> p (j c) n"),
                                   ACT.Square).then_inc(prob_ready, 1)
                elif kind == "mix0":
                    h, t, p = at
                    n = 3 * h + t
                    if n >= 2:
                        wait_full(act, TURN_KEYS[n - 2])
                    b = wait_full(act, step)
                    to = mix[n % 2][0:ROWS[t], :].rearrange("p (c n) -> p c n", c=4)[:, :, 2 * p * DV:2 * (p + 1) * DV]
                    act.activation(to, b[0:ROWS[t], :].rearrange("p (c n) -> p c n", c=4), ACT.Copy
                                   ).then_inc(mix_copied, 1)
                    if 2 * n + p:
                        act.wait_ge(mix_summed, 2 * n + p)
                    act.activation(sq_mix[0:ROWS[t], :], b[0:ROWS[t], :], ACT.Square).then_inc(bank_read(step), 1)
                elif kind == "mix_norm":
                    h, t = at
                    n = 3 * h + t
                    act.wait_ge(norm_ready, n + 1)
                    act.activation(o_tanh[0:ROWS[t], :], o_norm[0:ROWS[t], :], ACT.Tanh).then_inc(norm_tanh, 1)
                elif kind == "out":
                    layer, h, m = at
                    if layer == 2:
                        loaded(act, "out_b1")
                        copy_out(step, y_t[h][:, m, :], TOKENS, func=ACT.Identity, bias=out_b1[:, m:m + 1])
                    else:
                        copy_out(step, y_t[h][:, m, :], TOKENS)
                elif kind == "router":
                    h = at[0]
                    act.wait_ge(logit_ready, h + 1)
                    act.activation(exps[:, :, :], exps[:, :, :], ACT.Exp).then_inc(expd, 1)
                elif kind == "gates":
                    h = at[0]
                    copy_out(step, gate_t[h][:, :], TOKENS, ROUTED)
                elif kind == "up":
                    h, e = at
                    n = EXPERTS * h + e
                    if n >= ACT_RING:
                        before = n - ACT_RING
                        if before % EXPERTS == EXPERTS - 1:
                            wait_full(act, ("ffn", before // EXPERTS, KD - 1))
                        else:
                            act.wait_ge(act_used, before + 1 - before // EXPERTS)
                    copy_out(step, act_t[n % ACT_RING][:, :], TOKENS, func=ACT.Gelu)
                elif kind == "ffn_out":
                    h = at[0]
                    for m in range(KD):
                        key = ("ffn", h, m)
                        copy_out(key, y_t[h][:, m, :], TOKENS)
                elif kind == "qk1":
                    h, c = at
                    if c >= KI:
                        copy_out(step, qk[h][:, c, :], TOKENS)
                elif kind == "exp1":
                    h, t, u = at
                    n = 12 + 6 * h + 2 * t + u
                    wait_read(act, ("score1", h, t, u, 1))
                    view = raw[n % 2][0:ROWS[t], :, :, 0:ROWS[t]].rearrange("p j c n -> p (j c) n")
                    act.activation(view, view, ACT.Exp, scale=DV ** -0.5).then_inc(exp_ready, 1)
                elif kind == "prob1":
                    h, t, u = at
                    n = 12 + 6 * h + 2 * t + u
                    wait_full(act, MIX_KEYS[n - 2])
                    for j in range(2):
                        key = step + (j,)
                        b = wait_full(act, key)
                        act.activation(prob[n % 2][0:ROWS[t], j, :, 0:ROWS[t]],
                                       b[0:ROWS[t], 0:4 * ROWS[t]].rearrange("p (c n) -> p c n", c=4), ACT.Copy
                                       ).then_inc(bank_read(key), 1)
                elif kind == "turn1":
                    h, t = at
                    for u in range(2):
                        key = step + (u,)
                        b = wait_full(act, key)
                        act.activation(qk[h][:, 4 * u:4 * u + 4, START[t]:START[t] + ROWS[t]],
                                       b[:, 0:4 * ROWS[t]].rearrange("p (c n) -> p c n", c=4), ACT.Copy
                                       ).then_inc(bank_read(key), 1)
                elif kind == "quant_w":
                    copy_out(("quant_w", 0), w_last_t[:, :, :].rearrange("p k n -> p (k n)"), KD * DIM,
                             func=ACT.Identity, bias=minus_round[:, :])
                    copy_out(("quant_w", 1), last_scale[:, :], DIM)

        @block.vector
        def _(dve):
            chained = [0]

            def link(ins):
                chained[0] += 1
                ins.then_inc(dve_chain, 1)
                dve.wait_ge(dve_chain, chained[0])

            def reciprocal_root(x, rows):
                y, t = root[0:rows, :], root_t[0:rows, :]
                link(dve.tensor_scalar(t.bitcast(I32), x.bitcast(I32), 1, None, ALU.logical_shift_right))
                link(dve.tensor_scalar(y.bitcast(I32), t.bitcast(I32), -1.0, float(0x5f3759df),
                                       ALU.mult, ALU.add))
                for _ in range(3):
                    link(dve.scalar_tensor_tensor(out=t, in0=y, scalar=-0.5, in1=y, op0=ALU.mult, op1=ALU.mult))
                    link(dve.tensor_tensor(t, t, x, ALU.mult))
                    link(dve.scalar_tensor_tensor(out=y, in0=t, scalar=1.5, in1=y, op0=ALU.add, op1=ALU.mult))

            def constants():
                for h in range(HALVES):
                    dve.memset(mean_var[h][:, :, :], 1.0)
                dve.memset(logits[:, :, :], 0.0)
                for h in range(HALVES):
                    dve.memset(qk_sq[h][:, :, :, :], 1.0)
                for i in range(4):
                    dve.memset(pads[:, :, i:i + 1], -5.0 - i)
                link(dve.memset(q_stat[:, :, :], 1.0))
                for h in range(HALVES):
                    last = dve.memset(val[h][:, :, :, DV:DV + 1], 1.0)
                link(last)
                for t in range(TILES):
                    dve.tensor_copy(probs[:, t, ROUTED:], pads[:, t, :])

            def statistics(h, tiles, width, wait=None):
                parts = -(-width // 512)
                w = width // parts
                for t, tile in enumerate(tiles):
                    if wait:
                        wait(t)
                    for i in range(parts):
                        last = dve.bn_stats(partial[0:tile.shape[0], t, i, :], tile[:, i * w:(i + 1) * w])
                link(last)
                for t, tile in enumerate(tiles):
                    last = dve.bn_aggr(mean_var[h][0:tile.shape[0], t, :],
                                       partial[0:tile.shape[0], t, 0:parts, :].rearrange("p a b -> p (a b)"))
                last.then_inc(stat_ready, 1)

            def wait_rstd(*stats_step):
                dve.wait_ge(rstd_ready, STATS.index(stats_step) + 1)

            def normalise(h, to, tile, t):
                rows = tile.shape[0]
                return dve.tensor_scalar(to, tile, mean_var[h][0:rows, t, 0:1], rstd[h][0:rows, t:t + 1],
                                         ALU.subtract, ALU.mult)

            def quantise(tiles, stat, scale, n):
                for t, tile in enumerate(tiles):
                    last = dve.tensor_reduce(stat[0:tile.shape[0], 0, t:t + 1], tile, AX, ALU.max,
                                             apply_absolute_value=True)
                link(last)
                link(dve.tensor_scalar(scale[:, :], stat[:, 0, :], 1e-8, 1.0 / QMAX, ALU.max, ALU.mult))
                link(dve.reciprocal(stat[:, 1, :], scale[:, :]))
                for t, tile in enumerate(tiles):
                    yield dve.tensor_scalar(tile, tile, stat[0:tile.shape[0], 1, t:t + 1], ROUND,
                                            ALU.mult, ALU.add)

            def start_softmax(h):
                b = wait_full(dve, ("router", h))
                for t in range(TILES):
                    last = dve.tensor_copy(logits[0:ROWS[t], t, :], b[0:ROWS[t], ROUTED * t:ROUTED * (t + 1)])
                last.then_inc(bank_read(("router", h)), 1)
                wait_read(dve, ("router", h))
                link(dve.tensor_reduce(top_stat[:, 0, :], logits[:, :, :], AX, ALU.max))
                dve.tensor_tensor(exps[:, :, :], logits[:, :, :], spread(top_stat[:, 0, :], ROUTED), ALU.subtract
                                  ).then_inc(logit_ready, 1)

            def route(h):
                dve.wait_ge(expd, h + 1)
                link(dve.tensor_reduce(top_stat[:, 1, :], exps[:, :, :], AX, ALU.add))
                link(dve.reciprocal(top_stat[:, 2, :], top_stat[:, 1, :]))
                link(dve.tensor_tensor(probs[:, :, 0:ROUTED], exps[:, :, :], spread(top_stat[:, 2, :], ROUTED),
                                       ALU.mult))
                for t in range(TILES):
                    last = dve.max(top8[:, t, :], probs[:, t, 0:ROUTED])
                link(last)
                link(dve.tensor_copy(top8[:, :, TOP_K:], pads[:, :, :]))
                for t in range(TILES):
                    last = dve.match_replace(out=rest[:, t, :], in_to_replace=top8[:, t, :],
                                             in_values=probs[:, t, :], imm_value=0.0)
                link(last)
                dve.tensor_tensor(gate[:, :, :], probs[:, :, 0:ROUTED], rest[:, :, 0:ROUTED], ALU.subtract
                                  ).then_inc(gated_rows, 1)

            for step in ORDER:
                kind, at = step[0], step[1:]
                if kind == "consts":
                    constants()
                elif kind == "patch_stats":
                    h = at[0]
                    statistics(h, patch[h], PATCH_DIM, lambda t: loaded(dve, f"x{h}{t}"))
                elif kind == "patch_norm":
                    h = at[0]
                    wait_rstd("patch_stats", h)
                    for t in range(TILES):
                        normalise(h, patch[h][t], patch[h][t], t).then_inc(patch_normed[h], 1)
                elif kind == "embed_stats":
                    h = at[0]
                    statistics(h, [bank[PSUM["embed_t", h, t][0]][0:ROWS[t], 0:DIM] for t in range(TILES)], DIM,
                               lambda t: wait_full(dve, ("embed_t", h, t)))
                    dve.wait_ge(stat_ready, STATS.index(step) + 1)
                elif kind == "embed_norm":
                    h = at[0]
                    if h == 0:
                        loaded(dve, "embed_g", "embed_add", "embed_b")
                        dve.tensor_tensor(embed_add[:, :], embed_add[:, :], embed_b[:, :], ALU.add)
                    rows = [h_tok[h][0:ROWS[t], t, :] for t in range(TILES)]
                    keys = [("embed_t", h, t) for t in range(TILES)]
                    for t in range(TILES):
                        dve.scalar_tensor_tensor(out=rows[t], in0=wait_full(dve, keys[t])[0:ROWS[t], 0:DIM],
                                                 scalar=mean_var[h][0:ROWS[t], t, 0:1],
                                                 in1=embed_g[0:ROWS[t], :], op0=ALU.subtract, op1=ALU.mult
                                                 ).then_inc(bank_read(keys[t]), 1)
                    wait_rstd("embed_stats", h)
                    for t in range(TILES):
                        wait_read(dve, keys[t])
                        last = dve.scalar_tensor_tensor(out=rows[t], in0=rows[t], scalar=rstd[h][0:ROWS[t], t:t + 1],
                                                        in1=embed_add[0:ROWS[t], :], op0=ALU.mult, op1=ALU.add)
                    link(last)
                elif kind == "stats":
                    layer, h = at
                    if layer:
                        wait_read(dve, ("add", layer - 1, h, TILES - 1))
                    statistics(h, [h_tok[h][0:ROWS[t], t, :] for t in range(TILES)], DIM)
                elif kind == "norm":
                    layer, h = at
                    wait_rstd("stats", layer, h)
                    if LN_NTH[layer, h]:
                        wait_full(dve, TURNED[LN_NTH[layer, h] - 1])
                    tiles = [xn[t][0:ROWS[t], :] for t in range(TILES)]
                    for t in range(TILES):
                        last = normalise(h, tiles[t], h_tok[h][0:ROWS[t], t, :], t)
                        if layer < 3:
                            last.then_inc(xn_ready, 1)
                    if layer == 3:
                        link(last)
                        for ins in quantise(tiles, q_stat, q_scale[h], TILES):
                            ins.then_inc(xn_ready, 1)
                elif kind == "norms0":
                    h = at[0]
                    b = wait_full(dve, step)
                    for t in range(TILES):
                        last = dve.tensor_scalar(
                            qk_sq[h][0:ROWS[t], t, :, :].rearrange("p a (c i) -> p c a i", i=4),
                            b[0:ROWS[t], 32 * t:32 * (t + 1)].rearrange("p (c a i) -> p c a i", a=2, i=4),
                            1e-24, None, ALU.max)
                    last.then_inc(bank_read(step), 1)
                    wait_read(dve, step)
                    dve.reciprocal(qk_inv[h][:, :, :, :], qk_sq[h][:, :, :, :]).then_inc(qk_inv_ready[h], 1)
                elif kind == "v0":
                    h, t, n = at
                    r = slice(0, ROWS[t])
                    wait_read(dve, step)
                    dve.tensor_reduce(v_sq[r, 8 * n:8 * n + 8], sq_val[r, :].rearrange("p (h n) -> p h n", n=DV),
                                      AX, ALU.add).then_inc(v_summed, 1)
                elif kind == "v_scale":
                    h, t = at
                    r = slice(0, ROWS[t])
                    dve.wait_ge(v_summed, 2 * (TILES * h + t + 1))
                    link(dve.tensor_scalar(v_scale[r, :], v_sq[r, :], 1e-24, None, ALU.max))
                    reciprocal_root(v_scale[r, :], ROWS[t])
                    dve.wait_ge(qk_inv_ready[h], 1)
                    link(dve.tensor_tensor(v_scale[r, :], root[r, :], qk_inv[h][r, t, 1, :], ALU.mult))
                    dve.wait_ge(v_copied, 2 * (TILES * h + t + 1))
                    v = val[h][r, t, :, 0:DV]
                    dve.tensor_tensor(v, v, spread(v_scale[r, :], DV), ALU.mult).then_inc(v_ready[h], 1)
                elif kind == "gate0":
                    h, m = at
                    dve.wait_ge(tanh1_ready, KI * h + m + 1)
                    b = wait_full(dve, step)
                    dve.scalar_tensor_tensor(out=half_tanh[m % 2][:, :], in0=half_tanh[m % 2][:, :], scalar=1.0,
                                             in1=b[:, 0:TOKENS], op0=ALU.add, op1=ALU.mult
                                             ).then_inc(bank_read(step), 1)
                elif kind == "score0":
                    h, t, p = at
                    n = 6 * h + 2 * t + p
                    if n >= 2:
                        dve.wait_ge(prob_ready, n - 1)
                    if n == 0:
                        loaded(dve, "same_image")
                    mask = same_image[0:ROWS[t], 0:ROWS[t]].unsqueeze(1).to_broadcast([ROWS[t], 4, ROWS[t]])
                    for j in range(2):
                        key = step + (j,)
                        b = wait_full(dve, key)
                        dve.scalar_tensor_tensor(out=raw[n % 2][0:ROWS[t], j, :, 0:ROWS[t]],
                                                 in0=b[0:ROWS[t], 0:4 * ROWS[t]].rearrange("p (c n) -> p c n", c=4),
                                                 scalar=0.0, in1=mask, op0=ALU.max, op1=ALU.mult
                                                 ).then_inc(bank_read(key), 1)
                elif kind == "mix0":
                    h, t, p = at
                    r = slice(0, ROWS[t])
                    wait_read(dve, step)
                    dve.tensor_reduce(o_sq[r, :].rearrange("p (c i) -> p c i", c=4)[:, :, 2 * p:2 * p + 2],
                                      sq_mix[r, :].rearrange("p (c i n) -> p c i n", c=4, i=2), AX, ALU.add
                                      ).then_inc(mix_summed, 1)
                elif kind == "mix_norm":
                    h, t = at
                    n = TILES * h + t
                    r = slice(0, ROWS[t])
                    dve.wait_ge(mix_summed, 2 * (n + 1))
                    link(dve.tensor_scalar(o_sq[r, :], o_sq[r, :], 1.2e-38, None, ALU.max))
                    reciprocal_root(o_sq[r, :], ROWS[t])
                    link(dve.tensor_tensor(o_norm[r, :], o_sq[r, :], root[r, :], ALU.mult))
                    dve.tensor_tensor(o_norm[r, :], o_norm[r, :], qk_inv[h][r, t, 0, :], ALU.mult
                                      ).then_inc(norm_ready, 1)
                    dve.wait_ge(norm_ready, n + 1)
                    link(dve.tensor_scalar(o_inv[r, :], o_norm[r, :], 1e-12, None, ALU.max))
                    link(dve.reciprocal(o_inv[r, :], o_inv[r, :]))
                    link(dve.tensor_tensor(o_fac[r, :], o_inv[r, :], qk_inv[h][r, t, 0, :], ALU.mult))
                elif kind == "mix_scale":
                    h, t = at
                    n = TILES * h + t
                    r = slice(0, ROWS[t])
                    dve.wait_ge(norm_tanh, n + 1)
                    link(dve.tensor_tensor(o_fac[r, :], o_fac[r, :], o_tanh[r, :], ALU.mult))
                    view = mix[n % 2][r, :].rearrange("p (h n) -> p h n", n=DV)
                    dve.wait_ge(mix_copied, 2 * (n + 1))
                    dve.tensor_tensor(view, view, spread(o_fac[r, :], DV), ALU.mult).then_inc(mix_ready, 1)
                elif kind == "turn0":
                    h, t = at
                    if t == 0:
                        dve.wait_ge(gate_ready[h], KI)
                    for u in range(2):
                        key = step + (u,)
                        b = wait_full(dve, key)
                        to = qk[h][:, KI + 4 * u:KI + 4 * u + 4, START[t]:START[t] + ROWS[t]]
                        dve.tensor_tensor(to, b[:, 0:4 * ROWS[t]].rearrange("p (c n) -> p c n", c=4), to, ALU.mult
                                          ).then_inc(bank_read(key), 1)
                elif kind == "add":
                    layer, h, t = at
                    b = wait_full(dve, step)
                    rows = h_tok[h][0:ROWS[t], t, :]
                    dve.tensor_tensor(rows, b[0:ROWS[t], 0:DIM], rows, ALU.add).then_inc(bank_read(step), 1)
                elif kind == "router":
                    start_softmax(at[0])
                elif kind == "route":
                    route(at[0])
                elif kind == "qk1":
                    h, c = at
                    if c < KI:
                        b = wait_full(dve, step)
                        dve.tensor_copy(qk[h][:, c, :], b[:, 0:TOKENS]).then_inc(bank_read(step), 1)
                elif kind == "v1":
                    h, t, n = at
                    if n == 1:
                        b = wait_full(dve, step)
                        dve.tensor_copy(val[h][0:ROWS[t], t, 8 * n:8 * n + 8, 0:DV],
                                        b[0:ROWS[t], :].rearrange("p (h n) -> p h n", n=DV)
                                        ).then_inc(bank_read(step), 1)
                elif kind == "score1":
                    h, t, u = at
                    n = 12 + 6 * h + 2 * t + u
                    r = slice(0, ROWS[t])
                    if n < 14:
                        dve.wait_ge(prob_ready, n - 1)
                    else:
                        wait_full(dve, PROB_KEYS[n - 14])
                    for j in range(2):
                        key = step + (j,)
                        b = wait_full(dve, key)[r, 0:4 * ROWS[t]].rearrange("p (c n) -> p c n", c=4)
                        link(dve.tensor_reduce(row_max[j][r, :], b, AX, ALU.max))
                        dve.tensor_tensor(raw[n % 2][r, j, :, 0:ROWS[t]], b, spread(row_max[j][r, :], ROWS[t]),
                                          ALU.subtract).then_inc(bank_read(key), 1)
                elif kind == "mix1":
                    h, t, u = at
                    n = 6 + 3 * h + t
                    r = slice(0, ROWS[t])
                    if n >= 2 and u == 0:
                        wait_full(dve, TURN_KEYS[n - 2])
                    to = mix[n % 2][r, :].rearrange("p (c n) -> p c n", c=KI)
                    for j in range(2):
                        key = step + (j,)
                        b = wait_full(dve, key)[r, 0:4 * (DV + 1)].rearrange("p (c n) -> p c n", n=DV + 1)
                        link(dve.reciprocal(row_inv[j][r, :], b[:, :, DV]))
                        dve.tensor_tensor(to[:, 4 * u:4 * u + 4, j * DV:(j + 1) * DV], b[:, :, 0:DV],
                                          spread(row_inv[j][r, :], DV), ALU.mult).then_inc(bank_read(key), 1)
                elif kind == "quant_w":
                    loaded(dve, "ident", "masked", "w_last")
                    dve.tensor_copy(ident_b[:, :], ident[:, :])
                    dve.tensor_copy(masked_b[:, :], masked[:, :]).then_inc(masks_ready, 1)
                    tiles = [w_last[:, k, :] for k in range(KD)]
                    for ins in quantise(tiles, wq_stat, wq_scale, KD):
                        last = ins
                    last.then_inc(wq_ready, 1)
                elif kind == "last":
                    h, t = at
                    r = slice(0, ROWS[t])
                    if t == 0:
                        wait_read(dve, ("quant_w", 1))
                    if h == 1:
                        dve.wait_ge(stored[t], 16)
                    b = wait_full(dve, step)
                    dve.scalar_tensor_tensor(out=result[t][r, :], in0=b[r, 0:DIM], scalar=q_scale[h][r, t:t + 1],
                                             in1=last_scale[r, :], op0=ALU.mult, op1=ALU.mult
                                             ).then_inc(bank_read(step), 1)

        @block.gpsimd
        def _(pool):
            chained = [0]

            def link(ins):
                chained[0] += 1
                ins.then_inc(pool_chain, 1)
                pool.wait_ge(pool_chain, chained[0])

            def reciprocal_std(step, h):
                pool.wait_ge(stat_ready, STATS.index(step) + 1)
                link(pool.tensor_scalar(var_eps[:, :], mean_var[h][:, :, 1], 1e-5, None, ALU.add))
                pool.tensor_tensor(rstd[h][:, :], var_eps[:, :], power[0:MAX_ROWS, :], ALU.pow
                                   ).then_inc(rstd_ready, 1)

            for step in ORDER:
                kind, at = step[0], step[1:]
                if kind == "consts":
                    pool.memset(w_last_t[:, :, :], 0.0).then_inc(warm_ready, 1)
                    for h in range(HALVES):
                        pool.memset(y_t[h][:, :, :].rearrange("p k (s n) -> p k s n", n=SEQ)[:, :, :, 0:1], 0.0)
                    pool.memset(minus_round[:, :], -ROUND)
                    pool.memset(power[:, :], -0.5).then_inc(zeroed, 1)
                    pool.wait_ge(zeroed, 1)
                elif kind in ("patch_stats", "embed_stats", "stats"):
                    reciprocal_std(step, at[-1])
                elif kind == "norm":
                    layer, h = at
                    if layer == 3:
                        pool.wait_ge(xn_ready, TILES * (LN_NTH[layer, h] + 1))
                        loaded(pool, "last_b")
                        for t in range(TILES):
                            rows = h_tok[h][0:ROWS[t], t, :]
                            last = pool.tensor_tensor(rows, rows, last_b[0:ROWS[t], :], ALU.add)
                        last.then_inc(h_biased[h], 1)
                elif kind == "qk0":
                    h, c = at
                    if c >= 4:
                        continue
                    n = 4 * h + c
                    wait_read(pool, step)
                    before = n - 2
                    if before >= 0 and before % 4 == 3:
                        wait_full(pool, ("norms0", before // 4))
                    elif before >= 0:
                        pool.wait_ge(summed, before + 1 - before // 4)
                    pool.tensor_tensor(square[n % 2][:, :], qk[h][:, c, :], qk[h][:, c, :], ALU.mult
                                       ).then_inc(squared, 1)
                elif kind == "up":
                    h, e = at
                    if e >= SHARED:
                        n = EXPERTS * h + e
                        i = ROUTED * h + e - SHARED
                        a = act_t[n % ACT_RING]
                        wait_read(pool, step)
                        pool.wait_ge(gate_loaded[i % GATE_RING], 16 * (i // GATE_RING + 1))
                        pool.tensor_tensor(a[:, :], a[:, :], gate_bc[i % GATE_RING][:, :], ALU.mult
                                           ).then_inc(gated, 1)
                elif kind == "last":
                    h, t = at
                    r = slice(0, ROWS[t])
                    pool.wait_ge(h_biased[h], 1)
                    wait_read(pool, step)
                    pool.tensor_tensor(result[t][r, :], result[t][r, :], h_tok[h][r, t, :], ALU.add
                                       ).then_inc(result_ready, 1)


def _layouts(x):
    f = lambda name: np.ascontiguousarray(x[name])
    split = lambda a: np.ascontiguousarray(a.reshape(-1, 128).T)
    images = max(TILE_IMAGES)
    side = 6
    img = f("x").reshape(BATCH, 3, side, 16, side, 16).transpose(0, 2, 4, 3, 5, 1)
    rows = lambda a: np.ascontiguousarray(np.broadcast_to(a.reshape(1, DIM), (MAX_ROWS, DIM)))
    shift = np.concatenate([f("L0_tok_cls_token").reshape(1, DIM),
                            np.broadcast_to(f("L0_tok_ln2_b").reshape(1, DIM), (PATCHES, DIM))])
    token = np.arange(MAX_ROWS)
    same = (token[:, None] // SEQ) == (token[None, :] // SEQ)
    seen = same & (token[None, :] <= token[:, None])
    feature = np.arange(128)
    of_head = 4 * (feature % 32 // DK) + feature // 32
    qg, kv = (f(name).reshape(DIM, HEADS, DK + DV) for name in ("L0_attn_Wqg", "L0_attn_Wkv"))
    up = np.concatenate([f("L0_ffn_shared_up"), f("L0_ffn_routed_up")])
    down = np.concatenate([f("L0_ffn_shared_down"), f("L0_ffn_routed_down")])
    return {
        "patches": np.ascontiguousarray(img.reshape(HALVES, IMAGES * PATCHES, PATCH_DIM)),
        "patch_g": split(f("L0_tok_ln1_g")), "patch_b": split(f("L0_tok_ln1_b")),
        "w_patch": f("L0_tok_W_proj"), "embed_bias": split(f("L0_tok_b_proj")),
        "embed_g": rows(f("L0_tok_ln2_g")),
        "embed_b": np.ascontiguousarray(np.tile(shift, (images, 1))),
        "embed_pos": np.ascontiguousarray(np.tile(f("L0_tok_pos_emb").reshape(SEQ, DIM), (images, 1))),
        "w_qk": np.concatenate([np.stack([qg[:, :, :DK], kv[:, :, :DK]], 2).reshape(DIM, -1),
                                np.zeros((DIM, DK), np.float32)], 1),
        "w_gate": np.ascontiguousarray(qg[:, :, DK:].reshape(DIM, INNER)),
        "w_val": np.ascontiguousarray(kv[:, :, DK:].reshape(DIM, INNER)), "w_out": f("L0_attn_Wout"),
        "w_up": np.ascontiguousarray(up.transpose(2, 0, 1).reshape(KD, 128, EXPERTS, EXPERT).transpose(1, 2, 0, 3)),
        "w_down": np.ascontiguousarray(down.transpose(2, 0, 1)),
        "w_router": np.ascontiguousarray(f("L0_ffn_router_w").T.reshape(KD, 128, ROUTED).transpose(1, 0, 2)),
        "w_q1": f("L1_attn_Wq"), "w_k1": f("L1_attn_Wk"), "w_v1": f("L1_attn_Wv"), "w_out1": f("L1_attn_Wo"),
        "out_b1": split(f("L1_attn_bo")), "w_last": f("L1_ffn_weight"), "last_b": rows(f("L1_ffn_bias")),
        "ident": np.eye(128, dtype=np.float32),
        "same_image": same.astype(np.float32),
        "masked": np.where(seen, 0.0, NEG).astype(np.float32),
        "head_sum": (of_head[:, None] == np.arange(8)[None, :]).astype(np.float32),
    }


def kernel(**inputs):
    import concourse.bacc as bacc
    from concourse.bass_utils import run_bass_kernel_spmd

    arrays = _layouts({k: np.asarray(v) for k, v in inputs.items()})
    nc = bacc.Bacc("TRN2", target_bir_lowering=False, num_devices=1)
    dram = {name: nc.dram_tensor(name + "_dram", a.shape, mybir.dt.from_np(a.dtype), kind="ExternalInput").ap()
            for name, a in arrays.items()}
    out = nc.dram_tensor("out_dram", (BATCH * SEQ, DIM), F32, kind="ExternalOutput").ap()
    vit_tower(nc, dram, out)
    r = run_bass_kernel_spmd(nc, [{name + "_dram": a for name, a in arrays.items()}], core_ids=[0])
    return r.results[0]["out_dram"].reshape(BATCH, SEQ, DIM)
```

```python
from contextlib import ExitStack

import numpy as np

import concourse.bass as bass
from concourse import mybir

F32 = mybir.dt.float32
BF16 = mybir.dt.bfloat16
ALU = mybir.AluOpType
ACT = mybir.ActivationFunctionType
AX = mybir.AxisListType.X

BATCH, PATCHES, PATCH_DIM, DIM = 16, 36, 768, 256
SEQ = PATCHES + 1
HALVES = 2
IMAGES = BATCH // HALVES
TILE_IMAGES = (3, 3, 2)
TILES = len(TILE_IMAGES)
ROWS = tuple(n * SEQ for n in TILE_IMAGES)
PATCH_ROWS = tuple(n * PATCHES for n in TILE_IMAGES)
MAX_ROWS = max(ROWS)
START = tuple(sum(ROWS[:t]) for t in range(TILES))
PATCH_START = tuple(sum(PATCH_ROWS[:t]) for t in range(TILES))
TOKENS = sum(ROWS)
HEADS, DK, DV = 16, 16, 64
INNER = HEADS * DV
QK_COLS = 2 * HEADS * DK + DK
KD = DIM // 128
KP = PATCH_DIM // 128
KI = INNER // 128
SHARED, ROUTED, TOP_K, EXPERT = 2, 16, 4, 128
EXPERTS = SHARED + ROUTED
ACT_RING, GATE_RING = 4, 4
WARM_UP = 20
ROUND = 12582912.0
QMAX = 127.0
NEG = -3.0e38


def half_steps(h):
    half = [(h,)]
    tiles = [(h, t) for t in range(TILES)]
    parts = [(h, t, p) for t in range(TILES) for p in range(2)]
    experts = [(h, e) for e in range(EXPERTS)]
    by_tile = h == HALVES - 1
    added = (0, 1) if by_tile else (0, 1, 2)
    norms = [(layer, h) for layer in (0,) + tuple(layer + 1 for layer in added)]
    args = {
        "patch_stats": tiles, "patch_norm": tiles, "patch_t": [(h, c) for c in range(KP)],
        "embed": [(h, c) for c in range(KP)], "embed_t": half, "embed_stats": half, "embed_norm": half,
        "stats": norms, "norm": norms, "turn": [(layer, h) for layer in range(3)],
        "qk0": [(h, c) for i in range(4) for c in (i, 4 + i)], "norm0": [(h, c) for c in range(4)],
        "norms0": half, "v0": parts, "v_root": tiles, "v_scale": tiles,
        "gate0": [(h, m) for m in range(KI)], "gate_tanh": [(h, m) for m in range(KI)],
        "score0": parts, "prob0": parts, "mix0": parts, "mix_root": parts, "mix_tanh": tiles,
        "mix_scale": tiles, "turn0": tiles,
        "out": [(layer, h, m) for layer in added if layer != 1 for m in range(KD)],
        "add": [(layer, h, t) for layer in added for t in range(TILES)],
        "up": experts, "router": half, "route": half, "gates": half, "down": experts, "ffn_out": half,
        "qk1": [(h, c) for i in range(KI) for c in (i, KI + i)], "v1": parts, "score1": parts, "exp1": parts,
        "sum1": parts, "scale1": parts, "prob1": parts, "mix1": parts,
        "turn_q": tiles, "last": tiles,
    }
    if by_tile:
        args.update(out_rows=tiles, tile_stats=tiles, tile_norm=tiles)
    return {kind: [(kind,) + at for at in values] for kind, values in args.items()}


SCHEDULE = """
    -: consts |  a: patch_stats patch_norm patch_stats 2*patch_t patch_stats embed 2*patch_norm patch_t embed
    |  b: patch_stats |  a: patch_t embed patch_t embed patch_t embed |  b: patch_t |  a: embed embed_t |  b:
    embed patch_stats 3*patch_t 2*patch_norm patch_stats patch_norm |  a: embed_stats embed_norm stats |  b:
    patch_t |  a: norm |  b: 2*embed patch_t 3*embed embed_t embed_stats embed_norm |  a: turn qk0 |  b: stats
    norm |  a: 2*qk0 gate0 qk0 gate0 gate_tanh qk0 2*norm0 qk0 |  b: turn |  a: qk0 norm0 gate0 norm0 qk0 |
    b: 2*qk0 |  a: norms0 2*v0 v_root prob0 score0 v_scale v0 gate_tanh |  b: qk0 |  a: gate_tanh gate0
    gate_tanh v0 score0 gate0 |  b: norm0 |  a: gate_tanh gate0 mix0 prob0 mix_root score0 v0 mix0 score0
    v_root gate_tanh |  b: qk0 |  a: mix_root |  b: qk0 |  a: gate0 v0 gate_tanh v_root prob0 v_scale gate0 |
    b: v0 qk0 |  a: v_scale mix_scale mix_tanh gate_tanh |  b: gate0 qk0 v_root norm0 gate_tanh |  a: mix0 |
    b: 2*norm0 gate0 v0 |  a: score0 |  b: norms0 gate_tanh 2*gate0 |  a: prob0 turn0 prob0 score0 mix0 |  b:
    gate_tanh |  a: mix_root prob0 mix0 mix_root |  b: gate_tanh gate0 |  a: mix_tanh mix_scale 2*mix_root
    mix0 |  b: gate0 v0 v_scale |  a: mix_scale mix_tanh |  b: qk0 gate_tanh v0 |  a: turn0 |  b: score0 |  a:
    turn0 |  b: v_root v0 score0 |  a: 2*out |  -: quant_w |  a: 3*add |  b: prob0 gate_tanh |  a: stats norm
    |  b: score0 mix0 gate0 v0 |  a: turn |  b: v_root gate0 |  a: up router |  b: prob0 |  a: route |  b:
    gate_tanh v_scale 2*score0 |  a: up gates |  b: prob0 mix_root v_scale mix_root prob0 mix0 |  a: 2*down
    8*up |  b: mix_tanh prob0 mix_scale |  a: 2*up |  b: mix_root |  a: 3*down |  b: mix0 |  a: down |  b:
    prob0 score0 mix0 |  a: down |  b: mix_scale |  a: 3*down up |  b: mix_root |  a: down |  b: mix0 mix_tanh
    gate_tanh |  a: up |  b: turn0 |  a: down 2*up |  b: 2*mix_root mix0 mix_scale |  a: down up |  b:
    mix_tanh |  a: 3*down up |  b: turn0 |  a: ffn_out |  b: turn0 |  a: 2*down |  b: out |  a: 3*add stats
    norm |  b: out |  a: turn |  b: 3*add stats norm |  a: 4*qk1 |  b: turn |  a: qk1 |  b: up router 2*up
    route down |  a: v1 |  b: gates |  a: 2*qk1 |  b: 3*up down up 4*down up |  a: 2*qk1 v1 4*qk1 |  b: up
    down |  a: v1 |  b: down 5*up 2*down up 4*down |  a: qk1 |  b: 2*up down |  a: 2*qk1 |  b: up down |  a:
    score1 v1 |  b: down ffn_out down |  a: exp1 |  b: 3*add stats |  a: v1 sum1 2*scale1 |  b: norm |  a:
    score1 v1 |  b: turn |  a: sum1 exp1 score1 |  b: qk1 |  a: prob1 |  b: 5*qk1 |  a: prob1 score1 exp1 mix1
    |  b: qk1 v1 |  a: sum1 |  b: 2*v1 |  a: prob1 mix1 sum1 score1 exp1 |  b: qk1 |  a: 2*scale1 |  b: 2*qk1
    |  a: mix1 score1 sum1 scale1 prob1 |  b: qk1 |  a: scale1 exp1 |  b: scale1 3*qk1 |  a: exp1 sum1 |  b:
    2*qk1 |  a: prob1 mix1 prob1 |  b: score1 |  a: 2*mix1 |  b: exp1 sum1 score1 exp1 sum1 score1 |  a: out |
    b: scale1 prob1 score1 exp1 prob1 exp1 scale1 sum1 scale1 |  a: out |  b: v1 sum1 |  a: 2*add |  b: mix1 |
    a: add stats |  b: prob1 mix1 score1 |  a: norm |  b: exp1 score1 out_rows prob1 exp1 mix1 scale1 sum1 v1
    |  a: 2*turn_q |  b: sum1 v1 prob1 mix1 scale1 |  a: turn_q |  b: tile_stats prob1 |  a: 2*last |  b:
    tile_norm 2*mix1 out_rows tile_stats tile_norm out_rows tile_stats |  a: last |  b: turn_q last turn_q
    tile_norm last turn_q last
"""


def make_order():
    steps = [half_steps(h) for h in range(HALVES)] + [{"consts": [("consts",)], "quant_w": [("quant_w",)]}]
    order = []
    for part in SCHEDULE.split("|"):
        owner, kinds = part.split(":")
        of = steps["ab-".index(owner.strip())]
        for item in kinds.split():
            count, kind = item.split("*") if "*" in item else (1, item)
            order += [of[kind].pop(0) for _ in range(int(count))]
    assert not any(left for of in steps for left in of.values())
    return order


ORDER = make_order()
LN_STEPS = [step[1:] for step in ORDER if step[0] == "norm"] + [(3, HALVES - 1)]
STATS = [step for step in ORDER if step[0] in ("patch_stats", "embed_stats", "stats", "tile_stats")]
LN_NTH = {at: n for n, at in enumerate(LN_STEPS)}
TURNED = [("turn", layer, h, KD - 1) if layer < 3 else ("turn_q", h, TILES - 1) for layer, h in LN_STEPS]
MIX_KEYS = [step for step in ORDER if step[0] in ("mix0", "mix1")]
PROB_KEYS = [step + (1,) for step in ORDER if step[0] == "prob1"]
TURN_KEYS = [step + (1,) for step in ORDER if step[0] == "turn0"]


def banks_of(step):
    kind = step[0]
    if kind in ("patch_t", "qk0", "v0", "gate0", "out", "add", "out_rows", "up", "router", "gates", "qk1", "v1",
                "mix0", "mix1", "turn_q", "last"):
        return [step]
    if kind == "quant_w":
        return [(kind, n) for n in range(2)]
    if kind in ("turn", "turn0", "score0", "score1", "prob1"):
        return [step + (j,) for j in range(2)]
    if kind == "embed_t":
        return [step + (t,) for t in range(TILES)]
    if kind == "norm0" and step[2] == 0:
        return [("norms0", step[1])]
    if kind == "embed" and step[2] == 0:
        return [("embedded", step[1], m) for m in range(KD)]
    if kind == "down" and step[2] == 0:
        return [("ffn", step[1], m) for m in range(KD)]
    return []


READ_BY = {"norms0": "norms0", "embedded": "embed_t", "embed_t": "embed_norm", "ffn": "ffn_out"}


def psum_plan():
    plan, used, held, waiting = {}, [0] * 8, {}, list(range(8))
    for step in ORDER:
        for key in banks_of(step):
            bank = waiting.pop(0)
            plan[key] = (bank, used[bank])
            used[bank] += 1
            if key[0] in READ_BY:
                held.setdefault((READ_BY[key[0]], key[1]), []).append(bank)
            else:
                waiting.append(bank)
        waiting += held.pop(step, [])
    return plan


PSUM = psum_plan()


def vit_tower(nc, d, out):
    with ExitStack() as ctx:
        def sb(name, shape, dt=F32):
            return ctx.enter_context(nc.sbuf_tensor(name, shape, dt))

        def sem(name):
            return ctx.enter_context(nc.semaphore(name))

        def per_half(name):
            return [sem(f"{name}_{h}") for h in range(HALVES)]

        gates_dram = nc.dram_tensor("gates_dram", [HALVES, ROUTED, TOKENS], F32).ap()

        region = sb("proj_weights", [128, KP * DIM + KD * (QK_COLS + 2 * INNER)])
        w_patch = region[:, 0:KP * DIM].rearrange("p (k n) -> p k n", k=KP)
        ends = [KP * DIM + KD * n for n in (0, QK_COLS, QK_COLS + INNER, QK_COLS + 2 * INNER)]
        w_qk, w_gate, w_val = (region[:, ends[i]:ends[i + 1]].rearrange("p (k n) -> p k n", k=KD)
                               for i in range(3))
        w1 = [region[:, i * KD * INNER:(i + 1) * KD * INNER].rearrange("p (k n) -> p k n", k=KD)
              for i in range(3)]
        w_out = sb("out_weights", [128, KI, DIM])
        w_up = sb("up_weights", [128, EXPERTS, KD, EXPERT])
        w_down = sb("down_weights", [128, EXPERTS, DIM])
        w_router = sb("router_weights", [128, KD, ROUTED])
        w_last = sb("last_weights", [128, KD, DIM])
        w_last_t = sb("last_weights_t", [128, KD, DIM], BF16)
        patch_g, patch_b = sb("patch_g", [128, KP]), sb("patch_b", [128, KP])
        embed_bias = sb("embed_bias", [128, KD])
        minus_round = sb("minus_round", [128, 1])
        bias = {2: sb("out_b1", [MAX_ROWS, DIM]), 3: sb("last_b", [MAX_ROWS, DIM])}
        last_scale = sb("last_scale", [128, DIM])
        ident, ident_b = sb("ident", [128, 128]), sb("ident_b", [128, 128], BF16)
        same_image = sb("same_image", [MAX_ROWS, MAX_ROWS])
        masked = sb("masked", [MAX_ROWS, MAX_ROWS])
        masked_b = sb("masked_b", [MAX_ROWS, MAX_ROWS], BF16)
        head_sum = sb("head_sum", [128, 8])
        minus_half, half = sb("minus_half", [128, HEADS]), sb("half", [128, HEADS // 2])

        h_tok = [sb(f"h{h}", [MAX_ROWS, TILES, DIM]) for h in range(HALVES)]
        xn = [sb(f"xn{t}", [MAX_ROWS, DIM]) for t in range(TILES)]
        xn_t = [sb(f"xn_t{h}", [128, KD, TOKENS]) for h in range(HALVES)]
        qk = [sb(f"qk{h}", [128, 2 * KI, TOKENS]) for h in range(HALVES)]
        flat = [q[:, :, :].rearrange("p c n -> p (c n)") for q in qk]
        patch = [[flat[h][0:PATCH_ROWS[t], t * PATCH_DIM:(t + 1) * PATCH_DIM] for t in range(TILES)]
                 for h in range(HALVES)]
        patch_end = TILES * PATCH_DIM
        patch_t = [flat[h][:, patch_end:patch_end + KP * IMAGES * PATCHES].rearrange("p (k n) -> p k n", k=KP)
                   for h in range(HALVES)]
        val = [sb(f"val{h}", [MAX_ROWS, TILES, HEADS, DV]) for h in range(HALVES)]
        square = [sb(f"square{i}", [128, TOKENS]) for i in range(2)]
        half_tanh = [sb(f"half_tanh{i}", [128, TOKENS]) for i in range(2)]
        raw = [sb(f"raw{i}", [MAX_ROWS, 2, 4, MAX_ROWS]) for i in range(2)]
        prob = [sb(f"prob{i}", [MAX_ROWS, 2, 4, MAX_ROWS]) for i in range(2)]
        mix = [sb(f"mix{i}", [MAX_ROWS, INNER]) for i in range(2)]
        sq_val, sq_mix = sb("sq_val", [MAX_ROWS, 8 * DV]), sb("sq_mix", [MAX_ROWS, 8 * DV])
        y_t = [sb(f"y_t{h}", [128, KD, TOKENS]) for h in range(HALVES)]
        act_t = [sb(f"act_t{i}", [128, TOKENS]) for i in range(ACT_RING)]
        gate_bc = [sb(f"gate_bc{i}", [128, TOKENS]) for i in range(GATE_RING)]
        embed_b = act_t[3][0:MAX_ROWS, 0:DIM]
        embed_g, embed_add = (gate_bc[i][0:MAX_ROWS, 0:DIM] for i in (2, 3))
        xq_t = [gate_bc[h][:, :].bitcast(BF16).rearrange("p (k n) -> p k n", k=KD) for h in range(HALVES)]
        gate_t = [sb(f"gate_t{h}", [ROUTED, TOKENS]) for h in range(HALVES)]
        result = [act_t[t][0:MAX_ROWS, 0:DIM] for t in range(TILES)]

        partial = sb("partial", [MAX_ROWS, TILES, 2, 6])
        mean_var = [sb(f"mean_var{h}", [MAX_ROWS, TILES, 2]) for h in range(HALVES)]
        var_eps = sb("var_eps", [MAX_ROWS, TILES])
        rstd = [sb(f"rstd{h}", [MAX_ROWS, TILES]) for h in range(HALVES)]
        qk_sq = [sb(f"qk_sq{h}", [MAX_ROWS, TILES, 2, HEADS]) for h in range(HALVES)]
        qk_inv = [sb(f"qk_inv{h}", [MAX_ROWS, TILES, 2, HEADS]) for h in range(HALVES)]
        v_sq, v_scale, o_norm = ([sb(f"{name}{i}", [MAX_ROWS, HEADS]) for i in range(2)]
                                 for name in ("v_sq", "v_scale", "o_norm"))
        o_sq = sb("o_sq", [MAX_ROWS, HEADS])
        o_tanh, o_inv, o_fac = (sb(n, [MAX_ROWS, HEADS]) for n in ("o_tanh", "o_inv", "o_fac"))
        row_max = [sb(f"row_max{j}", [MAX_ROWS, 4]) for j in range(2)]
        row_sum = sb("row_sum", [MAX_ROWS, 8])
        row_inv = [sb(f"row_inv{i}", [MAX_ROWS, 8]) for i in range(2)]
        logits = sb("logits", [MAX_ROWS, TILES, ROUTED])
        exps = sb("exps", [MAX_ROWS, TILES, ROUTED])
        top_stat = sb("top_stat", [MAX_ROWS, 3, TILES])
        probs = sb("probs", [MAX_ROWS, TILES, ROUTED + 4])
        rest = sb("rest", [MAX_ROWS, TILES, ROUTED + 4])
        top8 = sb("top8", [MAX_ROWS, TILES, 8])
        pads = sb("pads", [MAX_ROWS, TILES, 4])
        gate = sb("gate", [MAX_ROWS, TILES, ROUTED])
        q_stat = sb("q_stat", [MAX_ROWS, 2, TILES])
        q_scale = [sb(f"q_scale{h}", [MAX_ROWS, TILES]) for h in range(HALVES)]
        wq_stat, wq_scale = sb("wq_stat", [128, 2, KD]), sb("wq_scale", [128, KD])

        bank = [ctx.enter_context(nc.psum_tensor(f"bank{i}", [128, 512], F32)) for i in range(8)]

        full = [sem(f"full{i}") for i in range(8)]
        free = [sem(f"free{i}") for i in range(8)]
        loads = {}
        warm_ready = sem("warm_ready")
        zeroed = sem("zeroed")
        dve_chain, pool_chain = sem("dve_chain"), sem("pool_chain")
        stat_ready, rstd_ready = sem("stat_ready"), sem("rstd_ready")
        patch_normed = per_half("patch_normed")
        xn_ready = sem("xn_ready")
        squared, summed = sem("squared"), sem("summed")
        qk_inv_ready = per_half("qk_inv_ready")
        v_copied, v_summed, v_rooted = sem("v_copied"), sem("v_summed"), sem("v_rooted")
        v_ready = per_half("v_ready")
        tanh1_ready = sem("tanh1_ready")
        gate_ready = per_half("gate_ready")
        exp_ready, inv_ready, exp_scaled = sem("exp_ready"), sem("inv_ready"), sem("exp_scaled")
        prob_ready = sem("prob_ready")
        mix_copied, mix_summed = sem("mix_copied"), sem("mix_summed")
        norm_ready, norm_tanh = sem("norm_ready"), sem("norm_tanh")
        mix_ready = sem("mix_ready")
        logit_ready, expd = sem("logit_ready"), sem("expd")
        gated_rows = sem("gated_rows")
        gate_stored = sem("gate_stored")
        gate_loaded = [sem(f"gate_loaded{i}") for i in range(GATE_RING)]
        gated, act_used = sem("gated"), sem("act_used")
        wq_ready, masks_ready = sem("wq_ready"), sem("masks_ready")
        h_biased = per_half("h_biased")
        result_ready = sem("result_ready")
        stored = [sem(f"stored{t}") for t in range(TILES)]

        def loaded(eng, *names):
            for name in names:
                eng.wait_ge(loads[name], 16)

        def wait_full(eng, key):
            b, before = PSUM[key]
            eng.wait_ge(full[b], before + 1)
            return bank[b]

        def bank_read(key):
            return free[PSUM[key][0]]

        def wait_read(eng, key):
            b, before = PSUM[key]
            eng.wait_ge(free[b], before + 1)

        def of_part(ap, p):
            return ap.rearrange("p (c i) -> p c i", c=4)[:, :, 2 * p:2 * p + 2]

        def spread(ap, n):
            return ap.unsqueeze(2).to_broadcast([ap.shape[0], ap.shape[1], n])

        x_dram = d["patches"]
        first = [(f"x{h}{t}", patch[h][t], x_dram[h, PATCH_START[t]:PATCH_START[t] + PATCH_ROWS[t], :])
                 for h in range(HALVES) for t in range(TILES)]
        small = [("ident", ident[:, :], d["ident"]), ("patch_g", patch_g[:, :], d["patch_g"]),
                 ("patch_b", patch_b[:, :], d["patch_b"]), ("embed_bias", embed_bias[:, :], d["embed_bias"]),
                 ("embed_g", embed_g[:, :], d["embed_g"]),
                 ("embed_add", embed_add[:, :], d["embed_pos"]), ("embed_b", embed_b[:, :], d["embed_b"]),
                 ("same_image", same_image[:, :], d["same_image"]), ("masked", masked[:, :], d["masked"]),
                 ("head_sum", head_sum[:, :], d["head_sum"])]
        w_layer0 = [(name, w, d[name].rearrange("(k p) n -> p k n", p=128))
                    for name, w in (("w_qk", w_qk), ("w_val", w_val), ("w_gate", w_gate))]
        w_experts = []
        for i in range(0, EXPERTS, 6):
            w_experts += [(f"w_up{i}", w_up[:, i:i + 6, :, :], d["w_up"][:, i:i + 6, :, :]),
                          (f"w_down{i}", w_down[:, i:i + 6, :], d["w_down"][:, i:i + 6, :])]
        plan_sync = first[:TILES] + [("w_patch", w_patch, d["w_patch"].rearrange("(k p) n -> p k n", p=128))] \
            + first[TILES:] + w_layer0 + [("w_out", w_out[:, :, :], d["w_out"].rearrange("(k p) n -> p k n", p=128))] \
            + w_experts
        late = [("w_router", w_router[:, :, :], d["w_router"]),
                ("w_last", w_last[:, :, :], d["w_last"].rearrange("(k p) n -> p k n", p=128)),
                ("bias2", bias[2][:, :], d["out_b1"]), ("bias3", bias[3][:, :], d["last_b"])]
        w_layer1 = [(f"w1{i}", w1[i], d[name].rearrange("(k p) n -> p k n", p=128))
                    for i, name in enumerate(("w_q1", "w_k1", "w_v1"))]
        w_layer1_out = ("w_out1", w_out[:, :, :], d["w_out1"].rearrange("(k p) n -> p k n", p=128))
        for name, _, _ in plan_sync + small + late + w_layer1 + [w_layer1_out]:
            loads[name] = sem(f"load_{name}")

        block = ctx.enter_context(nc.Block())

        @block.sync
        def _(sp):
            for name, to, src in plan_sync:
                sp.dma_start(to, src).then_inc(loads[name], 16)
            for name, to, src in late:
                sp.dma_start(to, src).then_inc(loads[name], 16)
            for step in ORDER:
                if step[0] == "gates":
                    h = step[1]
                    wait_read(sp, ("gates", h))
                    sp.dma_start(gates_dram[h], gate_t[h][:, :]).then_inc(gate_stored, 16)
                    if h == 0:
                        wait_full(sp, ("gate0", HALVES - 1, KI - 1))
                        for name, to, src in w_layer1:
                            sp.dma_start(to, src).then_inc(loads[name], 16)
                    sp.wait_ge(gate_stored, 16 * (h + 1))
                    for r in range(ROUTED):
                        n = ROUTED * h + r
                        if n >= GATE_RING:
                            sp.wait_ge(gated, n - GATE_RING + 1)
                        sp.dma_start(gate_bc[n % GATE_RING][:, :],
                                     gates_dram[h, r:r + 1, :].to_broadcast([128, TOKENS])
                                     ).then_inc(gate_loaded[n % GATE_RING], 16)
                    if h == 0:
                        for half in range(HALVES):
                            wait_full(sp, ("out", 0, half, KD - 1))
                        name, to, src = w_layer1_out
                        sp.dma_start(to, src).then_inc(loads[name], 16)
                if step[0] == "last":
                    _, h, t = step
                    sp.wait_ge(result_ready, TILES * h + t + 1)
                    r0 = h * TOKENS + START[t]
                    sp.dma_start(out[r0:r0 + ROWS[t], :], result[t][0:ROWS[t], :]).then_inc(stored[t], 16)
            for t in range(TILES):
                sp.wait_ge(stored[t], 16 * HALVES)

        @block.tensor
        def _(pe):
            def claim(key):
                b, before = PSUM[key]
                if before:
                    pe.wait_ge(free[b], before)
                return bank[b]

            def filled(key, last):
                last.then_inc(full[PSUM[key][0]], 1)

            def warm_up():
                pe.wait_ge(warm_ready, 1)
                for _ in range(WARM_UP):
                    pe.matmul(bank[0][:, :], w_last_t[:, 0, 0:128], w_last_t[:, :, :].rearrange("p k n -> p (k n)"),
                              start=True, stop=True)

            def patch_turn(h, c):
                key = ("patch_t", h, c)
                if c == 0:
                    loaded(pe, "ident")
                b = claim(key)
                for t in range(TILES):
                    if c == 0:
                        pe.wait_ge(patch_normed[h], t + 1)
                    last = pe.transpose(b[:, PATCH_START[t]:PATCH_START[t] + PATCH_ROWS[t]],
                                        patch[h][t][:, c * 128:(c + 1) * 128],
                                        ident[0:PATCH_ROWS[t], 0:PATCH_ROWS[t]])
                filled(key, last)

            def embed(h, k):
                if k == 0:
                    loaded(pe, "w_patch")
                wait_read(pe, ("patch_t", h, k))
                for m in range(KD):
                    key = ("embedded", h, m)
                    b = claim(key) if k == 0 else bank[PSUM[key][0]]
                    last = pe.matmul(b[:, 0:IMAGES * PATCHES], w_patch[:, k, m * 128:(m + 1) * 128],
                                     patch_t[h][:, k, :], start=(k == 0), stop=(k == KP - 1))
                    if k == KP - 1:
                        filled(key, last)

            def embed_turn(h):
                wait_read(pe, ("embedded", h, KD - 1))
                for t in range(TILES):
                    key = ("embed_t", h, t)
                    b = claim(key)
                    for m in range(KD):
                        last = pe.transpose(b[0:ROWS[t], m * 128:(m + 1) * 128],
                                            y_t[h][:, m, START[t]:START[t] + ROWS[t]], ident[:, :])
                    filled(key, last)

            def turn(layer, h):
                for m in range(KD):
                    key = ("turn", layer, h, m)
                    b = claim(key)
                    for t in range(TILES):
                        if m == 0:
                            pe.wait_ge(xn_ready, TILES * LN_NTH[layer, h] + t + 1)
                        last = pe.transpose(b[:, START[t]:START[t] + ROWS[t]],
                                            xn[t][0:ROWS[t], m * 128:(m + 1) * 128], ident[0:ROWS[t], 0:ROWS[t]])
                    filled(key, last)

            def turn_quantised(h, t):
                key = ("turn_q", h, t)
                pe.wait_ge(xn_ready, TILES * LN_NTH[3, h] + t + 1)
                b = claim(key)
                for m in range(KD):
                    last = pe.transpose(b[:, m * ROWS[t]:(m + 1) * ROWS[t]],
                                        xn[t][0:ROWS[t], m * 128:(m + 1) * 128], ident[0:ROWS[t], 0:ROWS[t]])
                filled(key, last)

            def dense(key, h, weights, b=None):
                b = claim(key) if b is None else b
                for k in range(KD):
                    last = pe.matmul(b[:, 0:TOKENS], weights(k), xn_t[h][:, k, :],
                                     start=(k == 0), stop=(k == KD - 1))
                filled(key, last)

            def token_product(key, h, t, weights, cols):
                b = claim(key)[0:ROWS[t], 0:cols]
                for k in range(KD):
                    last = pe.matmul(b, xn_t[h][:, k, START[t]:START[t] + ROWS[t]], weights(k),
                                     start=(k == 0), stop=(k == KD - 1))
                filled(key, last)

            def qk0(h, c):
                if c == 0:
                    loaded(pe, "w_qk")
                    wait_read(pe, ("turn", 0, h, KD - 1))
                col = 128 * (c % 4) + DK * (c // 4)
                dense(("qk0", h, c), h, lambda k: w_qk[:, k, col:col + 128])

            def norm0(h, c):
                key = ("norms0", h)
                if c == 0:
                    loaded(pe, "head_sum")
                    claim(key)
                n = 4 * h + c
                pe.wait_ge(squared, n + 1)
                b = bank[PSUM[key][0]]
                for t in range(TILES):
                    col = 32 * t + 8 * c
                    last = pe.matmul(b[0:ROWS[t], col:col + 8], square[n % 2][:, START[t]:START[t] + ROWS[t]],
                                     head_sum[:, :], start=True, stop=True)
                if c < 3:
                    last.then_inc(summed, 1)
                else:
                    filled(key, last)

            def score0(h, t, p):
                if (t, p) == (0, 0):
                    wait_read(pe, ("qk0", h, 7))
                cols = slice(START[t], START[t] + ROWS[t])
                banks = [claim(("score0", h, t, p, j)) for j in range(2)]
                last = [None, None]
                for c in range(4):
                    for j in range(2):
                        at = slice(32 * (2 * p + j), 32 * (2 * p + j) + DK)
                        last[j] = pe.matmul(banks[j][0:ROWS[t], c * ROWS[t]:(c + 1) * ROWS[t]],
                                            qk[h][at, 4 + c, cols], qk[h][at, c, cols], start=True, stop=True,
                                            tile_position=(32 * (2 * p + j), 0))
                for j in range(2):
                    filled(("score0", h, t, p, j), last[j])

            def mix0(h, t, p):
                n = 6 * h + 2 * t + p
                key = ("mix0", h, t, p)
                pe.wait_ge(prob_ready, n + 1)
                pe.wait_ge(v_ready[h], t + 1)
                b = claim(key)
                for c in range(4):
                    for j in range(2):
                        last = pe.matmul(b[0:ROWS[t], (2 * c + j) * DV:(2 * c + j + 1) * DV],
                                         prob[n % 2][0:ROWS[t], j, c, 0:ROWS[t]],
                                         val[h][0:ROWS[t], t, 4 * c + 2 * p + j, 0:DV], start=True, stop=True)
                filled(key, last)

            def turn0(h, t):
                n = 3 * h + t
                pe.wait_ge(mix_ready, n + 1)
                for u in range(2):
                    key = ("turn0", h, t, u)
                    b = claim(key)
                    for q in range(4):
                        c = 4 * u + q
                        last = pe.transpose(b[:, q * ROWS[t]:(q + 1) * ROWS[t]],
                                            mix[n % 2][0:ROWS[t], c * 128:(c + 1) * 128],
                                            ident[0:ROWS[t], 0:ROWS[t]])
                    filled(key, last)

            def out_product(layer, h, m):
                key = ("out", layer, h, m)
                if m == 0:
                    loaded(pe, "w_out" if layer == 0 else "w_out1")
                    wait_read(pe, ("turn0", h, TILES - 1, 1) if layer == 0 else ("mix1", h, TILES - 1, 1))
                src = qk[h][:, KI:2 * KI, :] if layer == 0 else qk[h][:, 0:KI, :]
                b = claim(key)
                for k in range(KI):
                    last = pe.matmul(b[:, 0:TOKENS], w_out[:, k, m * 128:(m + 1) * 128], src[:, k, :],
                                     start=(k == 0), stop=(k == KI - 1))
                filled(key, last)

            def out_rows(h, t):
                key = ("out_rows", h, t)
                loaded(pe, "w_out1")
                wait_read(pe, ("mix1", h, t, 1))
                b = claim(key)[0:ROWS[t], 0:DIM]
                for k in range(KI):
                    last = pe.matmul(b, qk[h][:, k, START[t]:START[t] + ROWS[t]], w_out[:, k, :],
                                     start=(k == 0), stop=(k == KI - 1))
                filled(key, last)

            def add(layer, h, t):
                key = ("add", layer, h, t)
                if t == 0:
                    wait_read(pe, ("ffn", h, KD - 1) if layer == 1 else ("out", layer, h, KD - 1))
                b = claim(key)
                for m in range(KD):
                    last = pe.transpose(b[0:ROWS[t], m * 128:(m + 1) * 128],
                                        y_t[h][:, m, START[t]:START[t] + ROWS[t]], ident[:, :])
                filled(key, last)

            def router(h):
                key = ("router", h)
                if h == 0:
                    loaded(pe, "w_router")
                b = claim(key)
                for t in range(TILES):
                    for k in range(KD):
                        last = pe.matmul(b[0:ROWS[t], ROUTED * t:ROUTED * (t + 1)],
                                         xn_t[h][:, k, START[t]:START[t] + ROWS[t]], w_router[:, k, :],
                                         start=(k == 0), stop=(k == KD - 1))
                filled(key, last)

            def gates(h):
                key = ("gates", h)
                pe.wait_ge(gated_rows, h + 1)
                b = claim(key)
                for t in range(TILES):
                    last = pe.transpose(b[0:ROUTED, START[t]:START[t] + ROWS[t]], gate[0:ROWS[t], t, :],
                                        ident[0:ROWS[t], 0:ROWS[t]])
                filled(key, last)

            def up(h, e):
                if e == 0:
                    wait_read(pe, ("turn", 1, h, KD - 1))
                if h == 0 and e % 6 == 0:
                    loaded(pe, f"w_up{e}")
                dense(("up", h, e), h, lambda k: w_up[:, e, k, :])

            def down(h, e):
                n = EXPERTS * h + e
                if h == 0 and e % 6 == 0:
                    loaded(pe, f"w_down{e}")
                if e < SHARED:
                    wait_read(pe, ("up", h, e))
                else:
                    pe.wait_ge(gated, ROUTED * h + e - SHARED + 1)
                for m in range(KD):
                    key = ("ffn", h, m)
                    b = claim(key) if e == 0 else bank[PSUM[key][0]]
                    last = pe.matmul(b[:, 0:TOKENS], w_down[:, e, m * 128:(m + 1) * 128],
                                     act_t[n % ACT_RING][:, :], start=(e == 0), stop=(e == EXPERTS - 1))
                    if e == EXPERTS - 1:
                        filled(key, last)
                if e < EXPERTS - 1:
                    last.then_inc(act_used, 1)

            def qk1(h, c):
                if c == 0:
                    wait_read(pe, ("turn", 2, h, KD - 1))
                    loaded(pe, "w10", "w11")
                w, m = (w1[0], c) if c < KI else (w1[1], c - KI)
                dense(("qk1", h, c), h, lambda k: w[:, k, m * 128:(m + 1) * 128])

            def score1(h, t, u):
                if (t, u) == (0, 0):
                    pe.wait_ge(masks_ready, 1)
                    wait_read(pe, ("qk1", h, KI - 1))
                    wait_read(pe, ("qk1", h, 2 * KI - 1))
                cols = slice(START[t], START[t] + ROWS[t])
                banks = [claim(("score1", h, t, u, j)) for j in range(2)]
                for j in range(2):
                    pe.matmul(banks[j][0:ROWS[t], 0:4 * ROWS[t]], ident_b[0:ROWS[t], 0:ROWS[t]],
                              masked_b[0:ROWS[t], 0:ROWS[t]].unsqueeze(1).to_broadcast([ROWS[t], 4, ROWS[t]]),
                              start=True, stop=False, skip_group_check=True)
                last = [None, None]
                for q in range(4):
                    for j in range(2):
                        at = slice(64 * j, 64 * j + 64)
                        last[j] = pe.matmul(banks[j][0:ROWS[t], q * ROWS[t]:(q + 1) * ROWS[t]],
                                            qk[h][at, 4 * u + q, cols], qk[h][at, KI + 4 * u + q, cols],
                                            start=False, stop=True, skip_group_check=True,
                                            tile_position=(64 * j, 0))
                for j in range(2):
                    filled(("score1", h, t, u, j), last[j])

            def prob1(h, t, u):
                n = 12 + 6 * h + 2 * t + u
                pe.wait_ge(exp_scaled, n - 12 + 1)
                for j in range(2):
                    key = ("prob1", h, t, u, j)
                    b = claim(key)
                    for q in range(4):
                        last = pe.transpose(b[0:ROWS[t], q * ROWS[t]:(q + 1) * ROWS[t]],
                                            raw[n % 2][0:ROWS[t], j, q, 0:ROWS[t]], ident[0:ROWS[t], 0:ROWS[t]])
                    filled(key, last)

            def mix1(h, t, u):
                n = 12 + 6 * h + 2 * t + u
                wait_read(pe, ("prob1", h, t, u, 1))
                wait_read(pe, ("v1", h, t, 0))
                wait_read(pe, ("v1", h, t, 1))
                key = ("mix1", h, t, u)
                b = claim(key)
                for q in range(4):
                    for j in range(2):
                        last = pe.matmul(b[j * DV:(j + 1) * DV, q * ROWS[t]:(q + 1) * ROWS[t]],
                                         val[h][0:ROWS[t], t, 2 * (4 * u + q) + j, :],
                                         prob[n % 2][0:ROWS[t], j, q, 0:ROWS[t]], start=True, stop=True,
                                         tile_position=(0, j * DV))
                filled(key, last)

            def quant_w():
                pe.wait_ge(wq_ready, 1)
                b = claim(("quant_w", 0))
                for k in range(KD):
                    for m in range(KD):
                        last = pe.transpose(b[:, k * DIM + m * 128:k * DIM + (m + 1) * 128],
                                            w_last[:, m, k * 128:(k + 1) * 128], ident[:, :])
                filled(("quant_w", 0), last)
                b = claim(("quant_w", 1))
                for m in range(KD):
                    last = pe.matmul(b[:, m * 128:(m + 1) * 128], wq_scale[:, m:m + 1].to_broadcast([128, 128]),
                                     ident[:, :], start=True, stop=True)
                filled(("quant_w", 1), last)

            def last_product(h, t):
                wait_read(pe, ("turn_q", h, t))
                if (h, t) == (0, 0):
                    wait_read(pe, ("quant_w", 0))
                key = ("last", h, t)
                b = claim(key)[0:ROWS[t], 0:DIM]
                for k in range(KD):
                    last = pe.matmul(b, xq_t[h][:, k, START[t]:START[t] + ROWS[t]], w_last_t[:, k, :],
                                     start=(k == 0), stop=(k == KD - 1))
                filled(key, last)

            for step in ORDER:
                kind, at = step[0], step[1:]
                if kind == "consts":
                    warm_up()
                elif kind == "patch_t":
                    patch_turn(*at)
                elif kind == "embed":
                    embed(*at)
                elif kind == "embed_t":
                    embed_turn(*at)
                elif kind == "turn_q":
                    turn_quantised(*at)
                elif kind == "turn":
                    turn(*at)
                elif kind == "qk0":
                    qk0(*at)
                elif kind == "norm0":
                    norm0(*at)
                elif kind == "v0":
                    h, t, n = at
                    if (t, n) == (0, 0):
                        loaded(pe, "w_val")
                    token_product(step, h, t, lambda k: w_val[:, k, 512 * n:512 * (n + 1)], 8 * DV)
                elif kind == "gate0":
                    h, m = at
                    if m == 0:
                        loaded(pe, "w_gate")
                    dense(step, h, lambda k: w_gate[:, k, m * 128:(m + 1) * 128])
                elif kind == "score0":
                    score0(*at)
                elif kind == "mix0":
                    mix0(*at)
                elif kind == "turn0":
                    turn0(*at)
                elif kind == "out":
                    out_product(*at)
                elif kind == "out_rows":
                    out_rows(*at)
                elif kind == "add":
                    add(*at)
                elif kind == "router":
                    router(*at)
                elif kind == "gates":
                    gates(*at)
                elif kind == "up":
                    up(*at)
                elif kind == "down":
                    down(*at)
                elif kind == "qk1":
                    qk1(*at)
                elif kind == "v1":
                    h, t, n = at
                    if (t, n) == (0, 0):
                        loaded(pe, "w12")
                    token_product(step, h, t, lambda k: w1[2][:, k, 512 * n:512 * (n + 1)], 8 * DV)
                elif kind == "score1":
                    score1(*at)
                elif kind == "prob1":
                    prob1(*at)
                elif kind == "mix1":
                    mix1(*at)
                elif kind == "quant_w":
                    quant_w()
                elif kind == "last":
                    last_product(*at)

        @block.scalar
        def _(act):
            act.preload_act_table(ACT.Gelu)
            for name, to, src in small:
                act.dma_start(to, src).then_inc(loads[name], 16)

            def copy_out(key, to, cols, rows=128, func=ACT.Copy, **kw):
                b = wait_full(act, key)
                return act.activation(to, b[0:rows, 0:cols], func, **kw).then_inc(bank_read(key), 1)

            for step in ORDER:
                kind, at = step[0], step[1:]
                if kind == "patch_t":
                    h, c = at
                    if c == 0:
                        loaded(act, "patch_g", "patch_b")
                    copy_out(step, patch_t[h][:, c, :], IMAGES * PATCHES, func=ACT.Identity,
                             scale=patch_g[:, c:c + 1], bias=patch_b[:, c:c + 1])
                elif kind == "embed_t":
                    h = at[0]
                    if h == 0:
                        act.wait_ge(zeroed, 1)
                        loaded(act, "embed_bias")
                    for m in range(KD):
                        key = ("embedded", h, m)
                        b = wait_full(act, key)
                        act.activation(y_t[h][:, m, :].rearrange("p (s n) -> p s n", n=SEQ)[:, :, 1:SEQ],
                                       b[:, 0:IMAGES * PATCHES].rearrange("p (s n) -> p s n", n=PATCHES),
                                       ACT.Identity, bias=embed_bias[:, m:m + 1]).then_inc(bank_read(key), 1)
                elif kind == "turn":
                    layer, h = at
                    for m in range(KD):
                        copy_out(step + (m,), xn_t[h][:, m, :], TOKENS)
                elif kind == "turn_q":
                    h, t = at
                    b = wait_full(act, step)
                    act.activation(xq_t[h][:, :, START[t]:START[t] + ROWS[t]],
                                   b[:, 0:KD * ROWS[t]].rearrange("p (k n) -> p k n", k=KD),
                                   ACT.Identity, bias=minus_round[:, :]).then_inc(bank_read(step), 1)
                elif kind == "qk0":
                    h, c = at
                    copy_out(step, qk[h][:, c, :], TOKENS)
                elif kind in ("v0", "v1"):
                    h, t, n = at
                    if kind == "v0" or n == 0:
                        b = wait_full(act, step)
                        last = act.activation(val[h][0:ROWS[t], t, 8 * n:8 * n + 8, 0:DV],
                                              b[0:ROWS[t], :].rearrange("p (h n) -> p h n", n=DV), ACT.Copy)
                        if kind == "v0":
                            last.then_inc(v_copied, 1)
                            i = 2 * (TILES * h + t) + n
                            if i:
                                act.wait_ge(v_summed, i)
                            last = act.activation(sq_val[0:ROWS[t], :], b[0:ROWS[t], :], ACT.Square)
                        last.then_inc(bank_read(step), 1)
                elif kind == "gate0":
                    h, m = at
                    b = wait_full(act, step)
                    if m >= 2:
                        act.wait_ge(gate_ready[h], m - 1)
                    elif h:
                        act.wait_ge(gate_ready[h - 1], KI)
                    act.activation(half_tanh[m % 2][:, :], b[:, 0:TOKENS], ACT.Tanh, scale=0.5
                                   ).then_inc(tanh1_ready, 1)
                elif kind == "gate_tanh":
                    h, m = at
                    wait_read(act, ("gate0", h, m))
                    act.activation(qk[h][:, KI + m, :], half_tanh[m % 2][:, :], ACT.Tanh, scale=0.5
                                   ).then_inc(gate_ready[h], 1)
                elif kind == "prob0":
                    h, t, p = at
                    n = 6 * h + 2 * t + p
                    wait_read(act, ("score0", h, t, p, 1))
                    if n >= 2:
                        wait_full(act, MIX_KEYS[n - 2])
                    act.activation(prob[n % 2][0:ROWS[t], :, :, 0:ROWS[t]].rearrange("p j c n -> p (j c) n"),
                                   raw[n % 2][0:ROWS[t], :, :, 0:ROWS[t]].rearrange("p j c n -> p (j c) n"),
                                   ACT.Square).then_inc(prob_ready, 1)
                elif kind == "mix0":
                    h, t, p = at
                    n = 3 * h + t
                    if n >= 2:
                        wait_full(act, TURN_KEYS[n - 2])
                    b = wait_full(act, step)
                    to = mix[n % 2][0:ROWS[t], :].rearrange("p (c n) -> p c n", c=4)[:, :, 2 * p * DV:2 * (p + 1) * DV]
                    act.activation(to, b[0:ROWS[t], :].rearrange("p (c n) -> p c n", c=4), ACT.Copy
                                   ).then_inc(mix_copied, 1)
                    if 2 * n + p:
                        act.wait_ge(mix_summed, 2 * n + p)
                    act.activation(sq_mix[0:ROWS[t], :], b[0:ROWS[t], :], ACT.Square).then_inc(bank_read(step), 1)
                elif kind == "mix_tanh":
                    h, t = at
                    n = 3 * h + t
                    act.wait_ge(norm_ready, 2 * (n + 1))
                    if n:
                        act.wait_ge(mix_ready, n)
                    act.activation(o_tanh[0:ROWS[t], :], o_norm[n % 2][0:ROWS[t], :], ACT.Tanh).then_inc(norm_tanh, 1)
                elif kind == "out":
                    layer, h, m = at
                    copy_out(step, y_t[h][:, m, :], TOKENS)
                elif kind == "router":
                    h = at[0]
                    act.wait_ge(logit_ready, h + 1)
                    act.activation(exps[:, :, :], exps[:, :, :], ACT.Exp).then_inc(expd, 1)
                elif kind == "gates":
                    h = at[0]
                    copy_out(step, gate_t[h][:, :], TOKENS, ROUTED)
                elif kind == "up":
                    h, e = at
                    n = EXPERTS * h + e
                    if n >= ACT_RING:
                        before = n - ACT_RING
                        if before % EXPERTS == EXPERTS - 1:
                            wait_full(act, ("ffn", before // EXPERTS, KD - 1))
                        else:
                            act.wait_ge(act_used, before + 1 - before // EXPERTS)
                    copy_out(step, act_t[n % ACT_RING][:, :], TOKENS, func=ACT.Gelu)
                elif kind == "ffn_out":
                    h = at[0]
                    for m in range(KD):
                        key = ("ffn", h, m)
                        copy_out(key, y_t[h][:, m, :], TOKENS)
                elif kind == "qk1":
                    h, c = at
                    if c >= KI:
                        copy_out(step, qk[h][:, c, :], TOKENS)
                elif kind == "exp1":
                    h, t, u = at
                    n = 12 + 6 * h + 2 * t + u
                    wait_read(act, ("score1", h, t, u, 1))
                    view = raw[n % 2][0:ROWS[t], :, :, 0:ROWS[t]].rearrange("p j c n -> p (j c) n")
                    act.activation(view, view, ACT.Exp, scale=DV ** -0.5).then_inc(exp_ready, 1)
                elif kind == "prob1":
                    h, t, u = at
                    n = 12 + 6 * h + 2 * t + u
                    wait_full(act, MIX_KEYS[n - 2])
                    for j in range(2):
                        key = step + (j,)
                        b = wait_full(act, key)
                        act.activation(prob[n % 2][0:ROWS[t], j, :, 0:ROWS[t]],
                                       b[0:ROWS[t], 0:4 * ROWS[t]].rearrange("p (c n) -> p c n", c=4), ACT.Copy
                                       ).then_inc(bank_read(key), 1)
                elif kind == "mix1":
                    h, t, u = at
                    b = wait_full(act, step)
                    act.activation(qk[h][:, 4 * u:4 * u + 4, START[t]:START[t] + ROWS[t]],
                                   b[:, 0:4 * ROWS[t]].rearrange("p (c n) -> p c n", c=4), ACT.Copy
                                   ).then_inc(bank_read(step), 1)
                elif kind == "quant_w":
                    copy_out(("quant_w", 0), w_last_t[:, :, :].rearrange("p k n -> p (k n)"), KD * DIM,
                             func=ACT.Identity, bias=minus_round[:, :])
                    copy_out(("quant_w", 1), last_scale[:, :], DIM)

        @block.vector
        def _(dve):
            chained = [0]

            def link(ins):
                chained[0] += 1
                ins.then_inc(dve_chain, 1)
                dve.wait_ge(dve_chain, chained[0])

            def constants():
                for h in range(HALVES):
                    dve.memset(mean_var[h][:, :, :], 1.0)
                dve.memset(logits[:, :, :], 0.0)
                for h in range(HALVES):
                    dve.memset(qk_sq[h][:, :, :, :], 1.0)
                for i in range(4):
                    dve.memset(pads[:, :, i:i + 1], -5.0 - i)
                link(dve.memset(q_stat[:, :, :], 1.0))
                for t in range(TILES):
                    dve.tensor_copy(probs[:, t, ROUTED:], pads[:, t, :])

            def statistics(h, tiles, width, wait=None):
                parts = -(-width // 512)
                w = width // parts
                for t, tile in tiles.items():
                    if wait:
                        wait(t)
                    for i in range(parts):
                        last = dve.bn_stats(partial[0:tile.shape[0], t, i, :], tile[:, i * w:(i + 1) * w])
                link(last)
                for t, tile in tiles.items():
                    last = dve.bn_aggr(mean_var[h][0:tile.shape[0], t, :],
                                       partial[0:tile.shape[0], t, 0:parts, :].rearrange("p a b -> p (a b)"))
                last.then_inc(stat_ready, 1)

            def wait_rstd(*stats_step):
                dve.wait_ge(rstd_ready, STATS.index(stats_step) + 1)

            def normalise(h, to, tile, t):
                rows = tile.shape[0]
                return dve.tensor_scalar(to, tile, mean_var[h][0:rows, t, 0:1], rstd[h][0:rows, t:t + 1],
                                         ALU.subtract, ALU.mult)

            def quantise(tiles, stat, scale):
                at = slice(min(tiles), max(tiles) + 1)
                for t, tile in tiles.items():
                    last = dve.tensor_reduce(stat[0:tile.shape[0], 0, t:t + 1], tile, AX, ALU.max,
                                             apply_absolute_value=True)
                link(last)
                link(dve.tensor_scalar(scale[:, at], stat[:, 0, at], 1e-8, 1.0 / QMAX, ALU.max, ALU.mult))
                link(dve.reciprocal(stat[:, 1, at], scale[:, at]))
                for t, tile in tiles.items():
                    yield dve.tensor_scalar(tile, tile, stat[0:tile.shape[0], 1, t:t + 1], ROUND,
                                            ALU.mult, ALU.add)

            def start_softmax(h):
                b = wait_full(dve, ("router", h))
                for t in range(TILES):
                    last = dve.tensor_copy(logits[0:ROWS[t], t, :], b[0:ROWS[t], ROUTED * t:ROUTED * (t + 1)])
                last.then_inc(bank_read(("router", h)), 1)
                wait_read(dve, ("router", h))
                link(dve.tensor_reduce(top_stat[:, 0, :], logits[:, :, :], AX, ALU.max))
                dve.tensor_tensor(exps[:, :, :], logits[:, :, :], spread(top_stat[:, 0, :], ROUTED), ALU.subtract
                                  ).then_inc(logit_ready, 1)

            def route(h):
                dve.wait_ge(expd, h + 1)
                link(dve.tensor_reduce(top_stat[:, 1, :], exps[:, :, :], AX, ALU.add))
                link(dve.reciprocal(top_stat[:, 2, :], top_stat[:, 1, :]))
                link(dve.tensor_tensor(probs[:, :, 0:ROUTED], exps[:, :, :], spread(top_stat[:, 2, :], ROUTED),
                                       ALU.mult))
                for t in range(TILES):
                    last = dve.max(top8[:, t, :], probs[:, t, 0:ROUTED])
                link(last)
                link(dve.tensor_copy(top8[:, :, TOP_K:], pads[:, :, :]))
                for t in range(TILES):
                    last = dve.match_replace(out=rest[:, t, :], in_to_replace=top8[:, t, :],
                                             in_values=probs[:, t, :], imm_value=0.0)
                link(last)
                dve.tensor_tensor(gate[:, :, :], probs[:, :, 0:ROUTED], rest[:, :, 0:ROUTED], ALU.subtract
                                  ).then_inc(gated_rows, 1)

            for step in ORDER:
                kind, at = step[0], step[1:]
                if kind == "consts":
                    constants()
                elif kind == "patch_stats":
                    h, t = at
                    loaded(dve, f"x{h}{t}")
                    statistics(h, {t: patch[h][t]}, PATCH_DIM)
                elif kind == "patch_norm":
                    h, t = at
                    wait_rstd("patch_stats", h, t)
                    normalise(h, patch[h][t], patch[h][t], t).then_inc(patch_normed[h], 1)
                elif kind == "embed_stats":
                    h = at[0]
                    statistics(h, {t: bank[PSUM["embed_t", h, t][0]][0:ROWS[t], 0:DIM] for t in range(TILES)}, DIM,
                               lambda t: wait_full(dve, ("embed_t", h, t)))
                    dve.wait_ge(stat_ready, STATS.index(step) + 1)
                elif kind == "embed_norm":
                    h = at[0]
                    if h == 0:
                        loaded(dve, "embed_g", "embed_add", "embed_b")
                        dve.tensor_tensor(embed_add[:, :], embed_add[:, :], embed_b[:, :], ALU.add)
                    rows = [h_tok[h][0:ROWS[t], t, :] for t in range(TILES)]
                    keys = [("embed_t", h, t) for t in range(TILES)]
                    for t in range(TILES):
                        dve.scalar_tensor_tensor(out=rows[t], in0=wait_full(dve, keys[t])[0:ROWS[t], 0:DIM],
                                                 scalar=mean_var[h][0:ROWS[t], t, 0:1],
                                                 in1=embed_g[0:ROWS[t], :], op0=ALU.subtract, op1=ALU.mult
                                                 ).then_inc(bank_read(keys[t]), 1)
                    wait_rstd("embed_stats", h)
                    for t in range(TILES):
                        wait_read(dve, keys[t])
                        last = dve.scalar_tensor_tensor(out=rows[t], in0=rows[t], scalar=rstd[h][0:ROWS[t], t:t + 1],
                                                        in1=embed_add[0:ROWS[t], :], op0=ALU.mult, op1=ALU.add)
                    link(last)
                elif kind == "stats":
                    layer, h = at
                    if layer:
                        wait_read(dve, ("add", layer - 1, h, TILES - 1))
                    statistics(h, {t: h_tok[h][0:ROWS[t], t, :] for t in range(TILES)}, DIM)
                elif kind == "tile_stats":
                    h, t = at
                    wait_read(dve, ("out_rows", h, t))
                    statistics(h, {t: h_tok[h][0:ROWS[t], t, :]}, DIM)
                elif kind == "tile_norm":
                    h, t = at
                    wait_rstd("tile_stats", h, t)
                    wait_full(dve, TURNED[LN_NTH[3, h] - 1])
                    tile = xn[t][0:ROWS[t], :]
                    link(normalise(h, tile, h_tok[h][0:ROWS[t], t, :], t))
                    for ins in quantise({t: tile}, q_stat, q_scale[h]):
                        ins.then_inc(xn_ready, 1)
                elif kind == "norm":
                    layer, h = at
                    wait_rstd("stats", layer, h)
                    if LN_NTH[layer, h]:
                        wait_full(dve, TURNED[LN_NTH[layer, h] - 1])
                    tiles = [xn[t][0:ROWS[t], :] for t in range(TILES)]
                    for t in range(TILES):
                        last = normalise(h, tiles[t], h_tok[h][0:ROWS[t], t, :], t)
                        if layer < 3:
                            last.then_inc(xn_ready, 1)
                    if layer == 3:
                        link(last)
                        for ins in quantise(dict(enumerate(tiles)), q_stat, q_scale[h]):
                            ins.then_inc(xn_ready, 1)
                elif kind == "norms0":
                    h = at[0]
                    b = wait_full(dve, step)
                    for t in range(TILES):
                        last = dve.tensor_scalar(
                            qk_sq[h][0:ROWS[t], t, :, :].rearrange("p a (c i) -> p c a i", i=4),
                            b[0:ROWS[t], 32 * t:32 * (t + 1)].rearrange("p (c a i) -> p c a i", a=2, i=4),
                            1e-24, None, ALU.max)
                    last.then_inc(bank_read(step), 1)
                    wait_read(dve, step)
                    dve.reciprocal(qk_inv[h][:, :, :, :], qk_sq[h][:, :, :, :]).then_inc(qk_inv_ready[h], 1)
                elif kind == "v0":
                    h, t, n = at
                    r = slice(0, ROWS[t])
                    wait_read(dve, step)
                    i = TILES * h + t
                    if i >= 2:
                        dve.wait_ge(v_rooted, i - 1)
                    dve.tensor_reduce(v_sq[i % 2][r, 8 * n:8 * n + 8], sq_val[r, :].rearrange("p (h n) -> p h n", n=DV),
                                      AX, ALU.add).then_inc(v_summed, 1)
                elif kind == "v_scale":
                    h, t = at
                    r = slice(0, ROWS[t])
                    i = TILES * h + t
                    dve.wait_ge(v_rooted, i + 1)
                    dve.wait_ge(v_copied, 2 * (TILES * h + t + 1))
                    v = val[h][r, t, :, 0:DV]
                    dve.tensor_tensor(v, v, spread(v_scale[i % 2][r, :], DV), ALU.mult).then_inc(v_ready[h], 1)
                elif kind == "gate0":
                    h, m = at
                    dve.wait_ge(tanh1_ready, KI * h + m + 1)
                    b = wait_full(dve, step)
                    dve.scalar_tensor_tensor(out=half_tanh[m % 2][:, :], in0=half_tanh[m % 2][:, :], scalar=1.0,
                                             in1=b[:, 0:TOKENS], op0=ALU.add, op1=ALU.mult
                                             ).then_inc(bank_read(step), 1)
                elif kind == "score0":
                    h, t, p = at
                    n = 6 * h + 2 * t + p
                    if n >= 2:
                        dve.wait_ge(prob_ready, n - 1)
                    if n == 0:
                        loaded(dve, "same_image")
                    mask = same_image[0:ROWS[t], 0:ROWS[t]].unsqueeze(1).to_broadcast([ROWS[t], 4, ROWS[t]])
                    for j in range(2):
                        key = step + (j,)
                        b = wait_full(dve, key)
                        dve.scalar_tensor_tensor(out=raw[n % 2][0:ROWS[t], j, :, 0:ROWS[t]],
                                                 in0=b[0:ROWS[t], 0:4 * ROWS[t]].rearrange("p (c n) -> p c n", c=4),
                                                 scalar=0.0, in1=mask, op0=ALU.max, op1=ALU.mult
                                                 ).then_inc(bank_read(key), 1)
                elif kind == "mix0":
                    h, t, p = at
                    r = slice(0, ROWS[t])
                    wait_read(dve, step)
                    n = TILES * h + t
                    if n:
                        dve.wait_ge(norm_ready, 2 * (n - 1) + p + 1)
                    dve.tensor_reduce(of_part(o_sq[r, :], p),
                                      sq_mix[r, :].rearrange("p (c i n) -> p c i n", c=4, i=2), AX, ALU.add
                                      ).then_inc(mix_summed, 1)
                elif kind == "mix_scale":
                    h, t = at
                    n = TILES * h + t
                    r = slice(0, ROWS[t])
                    dve.wait_ge(norm_ready, 2 * (n + 1))
                    link(dve.tensor_scalar(o_inv[r, :], o_norm[n % 2][r, :], 1e-12, None, ALU.max))
                    link(dve.reciprocal(o_inv[r, :], o_inv[r, :]))
                    link(dve.tensor_tensor(o_fac[r, :], o_inv[r, :], qk_inv[h][r, t, 0, :], ALU.mult))
                    dve.wait_ge(norm_tanh, n + 1)
                    link(dve.tensor_tensor(o_fac[r, :], o_fac[r, :], o_tanh[r, :], ALU.mult))
                    view = mix[n % 2][r, :].rearrange("p (h n) -> p h n", n=DV)
                    dve.wait_ge(mix_copied, 2 * (n + 1))
                    dve.tensor_tensor(view, view, spread(o_fac[r, :], DV), ALU.mult).then_inc(mix_ready, 1)
                elif kind == "turn0":
                    h, t = at
                    if t == 0:
                        dve.wait_ge(gate_ready[h], KI)
                    for u in range(2):
                        key = step + (u,)
                        b = wait_full(dve, key)
                        to = qk[h][:, KI + 4 * u:KI + 4 * u + 4, START[t]:START[t] + ROWS[t]]
                        dve.tensor_tensor(to, b[:, 0:4 * ROWS[t]].rearrange("p (c n) -> p c n", c=4), to, ALU.mult
                                          ).then_inc(bank_read(key), 1)
                elif kind == "add":
                    layer, h, t = at
                    b = wait_full(dve, step)
                    rows = h_tok[h][0:ROWS[t], t, :]
                    if layer == 2:
                        dve.wait_ge(h_biased[h], t + 1)
                    dve.tensor_tensor(rows, b[0:ROWS[t], 0:DIM], rows, ALU.add).then_inc(bank_read(step), 1)
                elif kind == "out_rows":
                    h, t = at
                    b = wait_full(dve, step)
                    rows = h_tok[h][0:ROWS[t], t, :]
                    dve.wait_ge(h_biased[h], t + 1)
                    dve.tensor_tensor(rows, b[0:ROWS[t], 0:DIM], rows, ALU.add).then_inc(bank_read(step), 1)
                elif kind == "router":
                    start_softmax(at[0])
                elif kind == "route":
                    route(at[0])
                elif kind == "qk1":
                    h, c = at
                    if c < KI:
                        b = wait_full(dve, step)
                        dve.tensor_copy(qk[h][:, c, :], b[:, 0:TOKENS]).then_inc(bank_read(step), 1)
                elif kind == "v1":
                    h, t, n = at
                    if n == 1:
                        b = wait_full(dve, step)
                        dve.tensor_copy(val[h][0:ROWS[t], t, 8 * n:8 * n + 8, 0:DV],
                                        b[0:ROWS[t], :].rearrange("p (h n) -> p h n", n=DV)
                                        ).then_inc(bank_read(step), 1)
                elif kind == "score1":
                    h, t, u = at
                    n = 12 + 6 * h + 2 * t + u
                    r = slice(0, ROWS[t])
                    if n < 14:
                        dve.wait_ge(prob_ready, n - 1)
                    else:
                        wait_full(dve, PROB_KEYS[n - 14])
                    for j in range(2):
                        key = step + (j,)
                        b = wait_full(dve, key)[r, 0:4 * ROWS[t]].rearrange("p (c n) -> p c n", c=4)
                        link(dve.tensor_reduce(row_max[j][r, :], b, AX, ALU.max))
                        dve.tensor_tensor(raw[n % 2][r, j, :, 0:ROWS[t]], b, spread(row_max[j][r, :], ROWS[t]),
                                          ALU.subtract).then_inc(bank_read(key), 1)
                elif kind == "sum1":
                    h, t, u = at
                    n = 6 * h + 2 * t + u
                    r = slice(0, ROWS[t])
                    dve.wait_ge(exp_ready, n + 1)
                    if n:
                        dve.wait_ge(inv_ready, n)
                    exponentials = raw[n % 2][r, :, :, 0:ROWS[t]].rearrange("p j c n -> p (j c) n")
                    link(dve.tensor_reduce(row_sum[r, :], exponentials, AX, ALU.add))
                    if n >= 2:
                        dve.wait_ge(exp_scaled, n - 1)
                    dve.reciprocal(row_inv[n % 2][r, :], row_sum[r, :]).then_inc(inv_ready, 1)
                elif kind == "quant_w":
                    loaded(dve, "ident", "masked", "w_last")
                    dve.tensor_copy(ident_b[:, :], ident[:, :])
                    dve.tensor_copy(masked_b[:, :], masked[:, :]).then_inc(masks_ready, 1)
                    for ins in quantise({k: w_last[:, k, :] for k in range(KD)}, wq_stat, wq_scale):
                        last = ins
                    last.then_inc(wq_ready, 1)
                elif kind == "last":
                    h, t = at
                    r = slice(0, ROWS[t])
                    if t == 0:
                        wait_read(dve, ("quant_w", 1))
                    if h == 1:
                        dve.wait_ge(stored[t], 16)
                    b = wait_full(dve, step)
                    dve.scalar_tensor_tensor(out=result[t][r, :], in0=b[r, 0:DIM], scalar=q_scale[h][r, t:t + 1],
                                             in1=last_scale[r, :], op0=ALU.mult, op1=ALU.mult
                                             ).then_inc(bank_read(step), 1)

        @block.gpsimd
        def _(pool):
            chained = [0]

            def link(ins):
                chained[0] += 1
                ins.then_inc(pool_chain, 1)
                pool.wait_ge(pool_chain, chained[0])

            def reciprocal_std(step, h, t):
                pool.wait_ge(stat_ready, STATS.index(step) + 1)
                link(pool.tensor_scalar(var_eps[:, t], mean_var[h][:, t, 1], 1e-5, None, ALU.add))
                pool.tensor_tensor(rstd[h][:, t], var_eps[:, t], minus_half[0:MAX_ROWS, t], ALU.pow
                                   ).then_inc(rstd_ready, 1)

            def add_bias(layer, h, t):
                pool.wait_ge(xn_ready, TILES * LN_NTH[layer, h] + t + 1)
                loaded(pool, f"bias{layer}")
                rows = h_tok[h][0:ROWS[t], t, :]
                pool.tensor_tensor(rows, rows, bias[layer][0:ROWS[t], :], ALU.add).then_inc(h_biased[h], 1)

            for step in ORDER:
                kind, at = step[0], step[1:]
                if kind == "consts":
                    pool.memset(w_last_t[:, :, :], 0.0).then_inc(warm_ready, 1)
                    for h in range(HALVES):
                        pool.memset(y_t[h][:, :, :].rearrange("p k (s n) -> p k s n", n=SEQ)[:, :, :, 0:1], 0.0)
                    pool.memset(minus_round[:, :], -ROUND)
                    pool.memset(half[:, :], 0.5)
                    pool.memset(minus_half[:, :], -0.5).then_inc(zeroed, 1)
                    pool.wait_ge(zeroed, 1)
                elif kind in ("patch_stats", "tile_stats"):
                    h, t = at
                    reciprocal_std(step, h, slice(t, t + 1))
                elif kind in ("embed_stats", "stats"):
                    reciprocal_std(step, at[-1], slice(0, TILES))
                elif kind == "norm":
                    layer, h = at
                    if layer in bias:
                        for t in range(TILES):
                            add_bias(layer, h, t)
                elif kind == "tile_norm":
                    add_bias(3, *at)
                elif kind == "v_root":
                    h, t = at
                    r = slice(0, ROWS[t])
                    i = TILES * h + t
                    if i >= 2:
                        pool.wait_ge(v_ready[(i - 2) // TILES], (i - 2) % TILES + 1)
                    pool.wait_ge(v_summed, 2 * (i + 1))
                    link(pool.tensor_scalar(v_scale[i % 2][r, :], v_sq[i % 2][r, :], 1e-24, None, ALU.max))
                    link(pool.tensor_tensor(v_scale[i % 2][r, :], v_scale[i % 2][r, :], minus_half[r, :], ALU.pow))
                    pool.wait_ge(qk_inv_ready[h], 1)
                    pool.tensor_tensor(v_scale[i % 2][r, :], v_scale[i % 2][r, :], qk_inv[h][r, t, 1, :], ALU.mult
                                       ).then_inc(v_rooted, 1)
                elif kind == "scale1":
                    h, t, u = at
                    n = 6 * h + 2 * t + u
                    r = slice(0, ROWS[t])
                    pool.wait_ge(inv_ready, n + 1)
                    view = raw[n % 2][r, :, :, 0:ROWS[t]].rearrange("p j c n -> p (j c) n")
                    pool.tensor_tensor(view, view, spread(row_inv[n % 2][r, :], ROWS[t]), ALU.mult
                                       ).then_inc(exp_scaled, 1)
                elif kind == "mix_root":
                    h, t, p = at
                    r = slice(0, ROWS[t])
                    n = TILES * h + t
                    to = of_part(o_norm[n % 2][r, :], p)
                    if n >= 2:
                        pool.wait_ge(mix_ready, n - 1)
                    pool.wait_ge(mix_summed, 2 * n + p + 1)
                    link(pool.tensor_tensor(to, of_part(o_sq[r, :], p),
                                            half[r, :].rearrange("p (c i) -> p c i", c=4), ALU.pow))
                    pool.tensor_tensor(to, to, of_part(qk_inv[h][r, t, 0, :], p), ALU.mult).then_inc(norm_ready, 1)
                elif kind == "qk0":
                    h, c = at
                    if c >= 4:
                        continue
                    n = 4 * h + c
                    wait_read(pool, step)
                    before = n - 2
                    if before >= 0 and before % 4 == 3:
                        wait_full(pool, ("norms0", before // 4))
                    elif before >= 0:
                        pool.wait_ge(summed, before + 1 - before // 4)
                    pool.tensor_tensor(square[n % 2][:, :], qk[h][:, c, :], qk[h][:, c, :], ALU.mult
                                       ).then_inc(squared, 1)
                elif kind == "up":
                    h, e = at
                    if e >= SHARED:
                        n = EXPERTS * h + e
                        i = ROUTED * h + e - SHARED
                        a = act_t[n % ACT_RING]
                        wait_read(pool, step)
                        pool.wait_ge(gate_loaded[i % GATE_RING], 16 * (i // GATE_RING + 1))
                        pool.tensor_tensor(a[:, :], a[:, :], gate_bc[i % GATE_RING][:, :], ALU.mult
                                           ).then_inc(gated, 1)
                elif kind == "last":
                    h, t = at
                    r = slice(0, ROWS[t])
                    pool.wait_ge(h_biased[h], TILES + t + 1)
                    wait_read(pool, step)
                    pool.tensor_tensor(result[t][r, :], result[t][r, :], h_tok[h][r, t, :], ALU.add
                                       ).then_inc(result_ready, 1)


def _layouts(x):
    f = lambda name: np.ascontiguousarray(x[name])
    split = lambda a: np.ascontiguousarray(a.reshape(-1, 128).T)
    images = max(TILE_IMAGES)
    side = 6
    img = f("x").reshape(BATCH, 3, side, 16, side, 16).transpose(0, 2, 4, 3, 5, 1)
    rows = lambda a: np.ascontiguousarray(np.broadcast_to(a.reshape(1, DIM), (MAX_ROWS, DIM)))
    shift = np.concatenate([f("L0_tok_cls_token").reshape(1, DIM),
                            np.broadcast_to(f("L0_tok_ln2_b").reshape(1, DIM), (PATCHES, DIM))])
    token = np.arange(MAX_ROWS)
    same = (token[:, None] // SEQ) == (token[None, :] // SEQ)
    seen = same & (token[None, :] <= token[:, None])
    feature = np.arange(128)
    of_head = 4 * (feature % 32 // DK) + feature // 32
    qg, kv = (f(name).reshape(DIM, HEADS, DK + DV) for name in ("L0_attn_Wqg", "L0_attn_Wkv"))
    up = np.concatenate([f("L0_ffn_shared_up"), f("L0_ffn_routed_up")])
    down = np.concatenate([f("L0_ffn_shared_down"), f("L0_ffn_routed_down")])
    return {
        "patches": np.ascontiguousarray(img.reshape(HALVES, IMAGES * PATCHES, PATCH_DIM)),
        "patch_g": split(f("L0_tok_ln1_g")), "patch_b": split(f("L0_tok_ln1_b")),
        "w_patch": f("L0_tok_W_proj"), "embed_bias": split(f("L0_tok_b_proj")),
        "embed_g": rows(f("L0_tok_ln2_g")),
        "embed_b": np.ascontiguousarray(np.tile(shift, (images, 1))),
        "embed_pos": np.ascontiguousarray(np.tile(f("L0_tok_pos_emb").reshape(SEQ, DIM), (images, 1))),
        "w_qk": np.concatenate([np.stack([qg[:, :, :DK], kv[:, :, :DK]], 2).reshape(DIM, -1),
                                np.zeros((DIM, DK), np.float32)], 1),
        "w_gate": np.ascontiguousarray(qg[:, :, DK:].reshape(DIM, INNER)),
        "w_val": np.ascontiguousarray(kv[:, :, DK:].reshape(DIM, INNER)), "w_out": f("L0_attn_Wout"),
        "w_up": np.ascontiguousarray(up.transpose(2, 0, 1).reshape(KD, 128, EXPERTS, EXPERT).transpose(1, 2, 0, 3)),
        "w_down": np.ascontiguousarray(down.transpose(2, 0, 1)),
        "w_router": np.ascontiguousarray(f("L0_ffn_router_w").T.reshape(KD, 128, ROUTED).transpose(1, 0, 2)),
        "w_q1": f("L1_attn_Wq"), "w_k1": f("L1_attn_Wk"), "w_v1": f("L1_attn_Wv"), "w_out1": f("L1_attn_Wo"),
        "out_b1": rows(f("L1_attn_bo")), "w_last": f("L1_ffn_weight"), "last_b": rows(f("L1_ffn_bias")),
        "ident": np.eye(128, dtype=np.float32),
        "same_image": same.astype(np.float32),
        "masked": np.where(seen, 0.0, NEG).astype(np.float32),
        "head_sum": (of_head[:, None] == np.arange(8)[None, :]).astype(np.float32),
    }


def kernel(**inputs):
    import concourse.bacc as bacc
    from concourse.bass_utils import run_bass_kernel_spmd

    arrays = _layouts({k: np.asarray(v) for k, v in inputs.items()})
    nc = bacc.Bacc("TRN2", target_bir_lowering=False, num_devices=1)
    dram = {name: nc.dram_tensor(name + "_dram", a.shape, mybir.dt.from_np(a.dtype), kind="ExternalInput").ap()
            for name, a in arrays.items()}
    out = nc.dram_tensor("out_dram", (BATCH * SEQ, DIM), F32, kind="ExternalOutput").ap()
    vit_tower(nc, dram, out)
    r = run_bass_kernel_spmd(nc, [{name + "_dram": a for name, a in arrays.items()}], core_ids=[0])
    return r.results[0]["out_dram"].reshape(BATCH, SEQ, DIM)
```
